# Optimizing a Trainium2 kernel written in Bass

```python
import numpy as np
import jax
import jax.numpy as jnp

def _softmax(x, axis=-1):
    return jax.nn.softmax(x, axis=axis)

def _gelu(x):
    return jax.nn.gelu(x, approximate=True)

def _silu(x):
    return jax.nn.silu(x)

def _sigmoid(x):
    return jax.nn.sigmoid(x)

def _layernorm(x, axis=-1, eps=1e-05):
    m = jnp.mean(x, axis=axis, keepdims=True)
    v = jnp.var(x, axis=axis, keepdims=True)
    return (x - m) / jnp.sqrt(v + eps)

def _scatter_add(tgt, idx, src, axis=0):
    return tgt.at[idx].add(src)

def _segment_sum(src, seg, n):
    return jax.ops.segment_sum(src, seg, n)
kernel_name = 'mk_gnn_preln_d4_gnn_r32_4327f1'

def setup_inputs(seed: int=0):
    np.random.seed(seed)
    _w = jnp.asarray

    def _rec_inputs():
        import jax
        import jax.numpy as jnp
        _gk = jax.random.key(seed)
        x = -0.0002117 + 1 * jax.random.normal(jax.random.fold_in(_gk, 1), (3125, 256), jnp.float32)
        _s = jax.random.randint(jax.random.fold_in(_gk, 2), (25000,), 0, 3125, jnp.int32)
        _d = jax.random.randint(jax.random.fold_in(_gk, 3), (25000,), 0, 3125, jnp.int32)
        _loop = jnp.arange(3125, dtype=jnp.int32)
        src = jnp.concatenate([_s, _d, _loop])
        dst = jnp.concatenate([_d, _s, _loop])
        _o = jnp.argsort(dst, stable=True)
        src = src[_o]
        dst = dst[_o]
        edge_attr_16 = -9.77346e-05 + 0.999888 * jax.random.normal(jax.random.fold_in(_gk, 12), (53125, 16), jnp.float32)
        edge_weight = jax.random.uniform(jax.random.fold_in(_gk, 14), (53125,), jnp.float32, 0.0, 0.999998)
        return (x, src, dst, edge_attr_16, edge_weight)
    x, src, dst, edge_attr_16, edge_weight = _rec_inputs()

    def _L0_gnn_setup():
        import jax, jax.numpy as jnp
        import numpy as np
        N_NODES = 3125
        N_EDGES = 100000
        NODE_F = 256
        EDGE_F = 16
        N_HEAD = 8
        OUT_F = 256
        NEG_SLOPE = 0.2
        BN_EPS = 1e-05

        def _seg_softmax(e, idx, num_segments):
            m = jax.ops.segment_max(e, idx, num_segments=num_segments)
            ex = jnp.exp(e - m[idx])
            s = jax.ops.segment_sum(ex, idx, num_segments=num_segments)
            return ex / s[idx]
        key = jax.random.key(seed)
        ks = jax.random.split(key, 16)
        inp = {}
        inp['feat_src'] = jax.random.normal(ks[0], (N_NODES, NODE_F), jnp.float32)
        inp['feat_edge'] = jax.random.normal(ks[1], (N_EDGES, EDGE_F), jnp.float32)
        inp['src'] = jax.random.randint(ks[2], (N_EDGES,), 0, N_NODES, jnp.int32)
        inp['dst'] = jax.random.randint(ks[3], (N_EDGES,), 0, N_NODES, jnp.int32)

        def xav(k, fan_in, fan_out):
            std = np.sqrt(2.0) * np.sqrt(2.0 / (fan_in + fan_out))
            return jax.random.normal(k, (fan_in, fan_out), jnp.float32) * std
        inp['W_prop_src'] = xav(ks[4], NODE_F, N_HEAD)
        inp['W_attn_src'] = xav(ks[5], NODE_F, N_HEAD)
        inp['W_attn_dst'] = xav(ks[6], NODE_F, N_HEAD)
        inp['W_attn_edge'] = xav(ks[7], EDGE_F, N_HEAD)
        inp['bn_gamma'] = jnp.ones((N_HEAD,), jnp.float32)
        inp['bn_beta'] = jnp.zeros((N_HEAD,), jnp.float32)
        inp['W_agg'] = xav(ks[8], N_HEAD, OUT_F)
        inp['b_agg'] = jnp.zeros((OUT_F,), jnp.float32)
        inp['W_apply_dst'] = xav(ks[9], NODE_F, OUT_F)
        inp['b_apply_dst'] = jnp.zeros((OUT_F,), jnp.float32)
        inp['W_apply'] = xav(ks[10], OUT_F, OUT_F)
        inp['b_apply'] = jnp.zeros((OUT_F,), jnp.float32)
        return inp
    _L0_gnn_all = _L0_gnn_setup()
    _L0_gnn_in = {k: v for k, v in _L0_gnn_all.items() if k in ('W_prop_src', 'W_attn_src', 'W_attn_dst', 'W_attn_edge', 'bn_gamma', 'bn_beta', 'W_agg', 'b_agg', 'W_apply_dst', 'b_apply_dst', 'W_apply', 'b_apply')}
    del _L0_gnn_all

    def _L1_gnn_setup():
        import jax, jax.numpy as jnp
        import numpy as np
        N_NODES = 50000
        IN_DIM = 256
        OUT_DIM = 128
        NUM_HEADS = 2
        N_EDGES = 25000

        def _gat_forward(x, edge_index, W_w, W_b, a):
            N = x.shape[0]
            H, D = (NUM_HEADS, OUT_DIM)
            Wh = (x @ W_w + W_b).reshape(N, H, D)
            src, dst = (edge_index[0], edge_index[1])
            a_src, a_dst = (a[:D], a[D:])
            s = jnp.einsum('nhd,d->nh', Wh, a_src)
            t = jnp.einsum('nhd,d->nh', Wh, a_dst)
            e = jax.nn.leaky_relu(s[src] + t[dst], negative_slope=0.2)
            m = jax.ops.segment_max(e, src, num_segments=N)
            ex = jnp.exp(e - m[src])
            denom = jax.ops.segment_sum(ex, src, num_segments=N)
            alpha = ex / denom[src]
            agg = jax.ops.segment_sum(alpha[:, :, None] * Wh[dst], src, num_segments=N)
            deg = jax.ops.segment_sum(jnp.ones_like(src, dtype=Wh.dtype), src, num_segments=N)
            h_prime = jnp.where(deg[:, None, None] > 0, agg, Wh)
            return h_prime.reshape(N, H * D)
        key = jax.random.key(seed)
        k1, k2, k3, k4, k5 = jax.random.split(key, 5)
        x = jax.random.normal(k1, (N_NODES, IN_DIM), dtype=jnp.float32)
        edge_index = jax.random.randint(k2, (2, N_EDGES), 0, N_NODES, dtype=jnp.int64)
        fan = IN_DIM + OUT_DIM * NUM_HEADS
        W_w = jax.random.uniform(k3, (IN_DIM, OUT_DIM * NUM_HEADS), dtype=jnp.float32, minval=-np.sqrt(6.0 / fan), maxval=np.sqrt(6.0 / fan))
        W_b = jnp.zeros((OUT_DIM * NUM_HEADS,), dtype=jnp.float32)
        fa = 1 + 2 * OUT_DIM
        a = jax.random.uniform(k4, (2 * OUT_DIM,), dtype=jnp.float32, minval=-np.sqrt(6.0 / fa), maxval=np.sqrt(6.0 / fa))
        return {'x': x, 'edge_index': edge_index, 'W_w': W_w, 'W_b': W_b, 'a': a}
    _L1_gnn_all = _L1_gnn_setup()
    _L1_gnn_in = {k: v for k, v in _L1_gnn_all.items() if k in ('W_w', 'W_b', 'a')}
    del _L1_gnn_all

    def _L2_gnn_setup():
        import jax, jax.numpy as jnp
        import numpy as np
        N_NODES = 3125
        N_EDGES = 50000
        D_IN = 256
        D_OUT = 256
        key = jax.random.key(seed)
        k1, k2, k3, k4, k5 = jax.random.split(key, 5)
        feat = jax.random.normal(k1, (N_NODES, D_IN), dtype=jnp.float32)
        lim = float(np.sqrt(6.0 / (D_IN + D_OUT)))
        W_neigh = jax.random.uniform(k2, (D_OUT, D_IN), minval=-lim, maxval=lim, dtype=jnp.float32)
        W_self = jax.random.uniform(k3, (D_OUT, D_IN), minval=-lim, maxval=lim, dtype=jnp.float32)
        b_self = jnp.zeros((D_OUT,), dtype=jnp.float32)
        src = jax.random.randint(k4, (N_EDGES,), 0, N_NODES, dtype=jnp.int32)
        dst = jax.random.randint(k5, (N_EDGES,), 0, N_NODES, dtype=jnp.int32)
        return {'feat': feat, 'W_neigh': W_neigh, 'W_self': W_self, 'b_self': b_self, 'src': src, 'dst': dst}
    _L2_gnn_all = _L2_gnn_setup()
    _L2_gnn_in = {k: v for k, v in _L2_gnn_all.items() if k in ('W_neigh', 'W_self', 'b_self')}
    del _L2_gnn_all

    def _L3_gnn_setup():
        import jax, jax.numpy as jnp
        import numpy as np
        N, E, D, H, C = (625, 10000, 256, 8, 32)
        NEG_SLOPE = 0.2
        key = jax.random.key(seed)
        ks = jax.random.split(key, 9)
        s = 1.0 / np.sqrt(D)
        x = jax.random.normal(ks[0], (N, D), dtype=jnp.float32)
        edge_index = jax.random.randint(ks[1], (2, E), 0, N, dtype=jnp.int32)
        edge_attr = jax.random.uniform(ks[2], (E,), dtype=jnp.float32, minval=0.05, maxval=1.0)
        W_l = jax.random.normal(ks[3], (D, H * C), dtype=jnp.float32) * s
        b_l = jax.random.normal(ks[4], (H * C,), dtype=jnp.float32) * 0.01
        W_r = jax.random.normal(ks[5], (D, H * C), dtype=jnp.float32) * s
        b_r = jax.random.normal(ks[6], (H * C,), dtype=jnp.float32) * 0.01
        att = jax.random.normal(ks[7], (H, C), dtype=jnp.float32) * (1.0 / np.sqrt(C))
        bias = jax.random.normal(ks[8], (H * C,), dtype=jnp.float32) * 0.01
        return {'x': x, 'edge_index': edge_index, 'edge_attr': edge_attr, 'W_l': W_l, 'b_l': b_l, 'W_r': W_r, 'b_r': b_r, 'att': att, 'bias': bias}
    _L3_gnn_all = _L3_gnn_setup()
    _L3_gnn_in = {k: v for k, v in _L3_gnn_all.items() if k in ('W_l', 'b_l', 'W_r', 'b_r', 'att', 'bias')}
    del _L3_gnn_all
    return {'x': x, 'src': src, 'dst': dst, 'edge_attr_16': edge_attr_16, 'edge_weight': edge_weight, 'L0_gnn_W_prop_src': _L0_gnn_in['W_prop_src'], 'L0_gnn_W_attn_src': _L0_gnn_in['W_attn_src'], 'L0_gnn_W_attn_dst': _L0_gnn_in['W_attn_dst'], 'L0_gnn_W_attn_edge': _L0_gnn_in['W_attn_edge'], 'L0_gnn_bn_gamma': _L0_gnn_in['bn_gamma'], 'L0_gnn_bn_beta': _L0_gnn_in['bn_beta'], 'L0_gnn_W_agg': _L0_gnn_in['W_agg'], 'L0_gnn_b_agg': _L0_gnn_in['b_agg'], 'L0_gnn_W_apply_dst': _L0_gnn_in['W_apply_dst'], 'L0_gnn_b_apply_dst': _L0_gnn_in['b_apply_dst'], 'L0_gnn_W_apply': _L0_gnn_in['W_apply'], 'L0_gnn_b_apply': _L0_gnn_in['b_apply'], 'L1_gnn_W_w': _L1_gnn_in['W_w'], 'L1_gnn_W_b': _L1_gnn_in['W_b'], 'L1_gnn_a': _L1_gnn_in['a'], 'L2_gnn_W_neigh': _L2_gnn_in['W_neigh'], 'L2_gnn_W_self': _L2_gnn_in['W_self'], 'L2_gnn_b_self': _L2_gnn_in['b_self'], 'L3_gnn_W_l': _L3_gnn_in['W_l'], 'L3_gnn_b_l': _L3_gnn_in['b_l'], 'L3_gnn_W_r': _L3_gnn_in['W_r'], 'L3_gnn_b_r': _L3_gnn_in['b_r'], 'L3_gnn_att': _L3_gnn_in['att'], 'L3_gnn_bias': _L3_gnn_in['bias']}

def reference(x, src, dst, edge_attr_16, edge_weight, L0_gnn_W_prop_src, L0_gnn_W_attn_src, L0_gnn_W_attn_dst, L0_gnn_W_attn_edge, L0_gnn_bn_gamma, L0_gnn_bn_beta, L0_gnn_W_agg, L0_gnn_b_agg, L0_gnn_W_apply_dst, L0_gnn_b_apply_dst, L0_gnn_W_apply, L0_gnn_b_apply, L1_gnn_W_w, L1_gnn_W_b, L1_gnn_a, L2_gnn_W_neigh, L2_gnn_W_self, L2_gnn_b_self, L3_gnn_W_l, L3_gnn_b_l, L3_gnn_W_r, L3_gnn_b_r, L3_gnn_att, L3_gnn_bias):
    import jax
    import jax.numpy as jnp

    def _L0_gnn_ref(feat_src, feat_edge, src, dst, W_prop_src, W_attn_src, W_attn_dst, W_attn_edge, bn_gamma, bn_beta, W_agg, b_agg, W_apply_dst, b_apply_dst, W_apply, b_apply):
        import jax, jax.numpy as jnp
        import numpy as np
        N_NODES = 3125
        N_EDGES = 100000
        NODE_F = 256
        EDGE_F = 16
        N_HEAD = 8
        OUT_F = 256
        NEG_SLOPE = 0.2
        BN_EPS = 1e-05

        def _seg_softmax(e, idx, num_segments):
            m = jax.ops.segment_max(e, idx, num_segments=num_segments)
            ex = jnp.exp(e - m[idx])
            s = jax.ops.segment_sum(ex, idx, num_segments=num_segments)
            return ex / s[idx]
        leaky = lambda x: jnp.where(x >= 0, x, NEG_SLOPE * x)
        feat_dst = feat_src
        feat_src_fc = feat_src @ W_prop_src
        attn_src = feat_src @ W_attn_src
        attn_dst = feat_dst @ W_attn_dst
        attn_edge = feat_edge @ W_attn_edge
        e = attn_src[src] + attn_dst[dst] + attn_edge
        e = leaky(e)
        a_dst = jnp.clip(_seg_softmax(e, dst, N_NODES), 1e-09)
        a_src = jnp.clip(_seg_softmax(e, src, N_NODES), 1e-09)
        a = jnp.sqrt(a_dst * a_src)
        msg_sum = jax.ops.segment_sum(feat_src_fc[src] * a, dst, num_segments=N_NODES)
        mu = jnp.mean(msg_sum, axis=0)
        var = jnp.mean((msg_sum - mu) ** 2, axis=0)
        h = (msg_sum - mu) / jnp.sqrt(var + BN_EPS) * bn_gamma + bn_beta
        rst = h @ W_agg + b_agg
        rst = rst + feat_dst @ W_apply_dst + b_apply_dst
        rst = leaky(rst)
        rst = rst @ W_apply + b_apply
        return rst

    def _L1_gnn_ref(x, edge_index, W_w, W_b, a):
        import jax, jax.numpy as jnp
        import numpy as np
        N_NODES = 50000
        IN_DIM = 256
        OUT_DIM = 128
        NUM_HEADS = 2
        N_EDGES = 25000

        def _gat_forward(x, edge_index, W_w, W_b, a):
            N = x.shape[0]
            H, D = (NUM_HEADS, OUT_DIM)
            Wh = (x @ W_w + W_b).reshape(N, H, D)
            src, dst = (edge_index[0], edge_index[1])
            a_src, a_dst = (a[:D], a[D:])
            s = jnp.einsum('nhd,d->nh', Wh, a_src)
            t = jnp.einsum('nhd,d->nh', Wh, a_dst)
            e = jax.nn.leaky_relu(s[src] + t[dst], negative_slope=0.2)
            m = jax.ops.segment_max(e, src, num_segments=N)
            ex = jnp.exp(e - m[src])
            denom = jax.ops.segment_sum(ex, src, num_segments=N)
            alpha = ex / denom[src]
            agg = jax.ops.segment_sum(alpha[:, :, None] * Wh[dst], src, num_segments=N)
            deg = jax.ops.segment_sum(jnp.ones_like(src, dtype=Wh.dtype), src, num_segments=N)
            h_prime = jnp.where(deg[:, None, None] > 0, agg, Wh)
            return h_prime.reshape(N, H * D)
        return _gat_forward(x, edge_index, W_w, W_b, a)

    def _L2_gnn_ref(feat, W_neigh, W_self, b_self, src, dst):
        import jax, jax.numpy as jnp
        import numpy as np
        N_NODES = 3125
        N_EDGES = 50000
        D_IN = 256
        D_OUT = 256
        msgs = feat[src]
        neigh_sum = jax.ops.segment_sum(msgs, dst, num_segments=N_NODES)
        deg = jax.ops.segment_sum(jnp.ones((src.shape[0],), dtype=feat.dtype), dst, num_segments=N_NODES)
        h_neigh = neigh_sum / jnp.maximum(deg, 1.0)[:, None]
        h_neigh = h_neigh @ W_neigh.T
        h_self = feat @ W_self.T + b_self
        return h_self + h_neigh

    def _L3_gnn_ref(x, edge_index, edge_attr, W_l, b_l, W_r, b_r, att, bias):
        import jax, jax.numpy as jnp
        import numpy as np
        N, E, D, H, C = (625, 10000, 256, 8, 32)
        NEG_SLOPE = 0.2
        n = x.shape[0]
        x_l = (x @ W_l + b_l).reshape(n, H, C)
        x_r = (x @ W_r + b_r).reshape(n, H, C)
        src, dst = (edge_index[0], edge_index[1])
        x_j = x_l[src]
        g = jax.nn.leaky_relu(x_r[dst] + x_j, NEG_SLOPE)
        alpha = jnp.einsum('ehc,hc->eh', g, att)
        alpha = alpha + jnp.log(edge_attr)[:, None]
        amax = jax.ops.segment_max(alpha, dst, num_segments=n)
        ex = jnp.exp(alpha - amax[dst])
        denom = jax.ops.segment_sum(ex, dst, num_segments=n)
        alpha = ex / (denom[dst] + 1e-16)
        out = jax.ops.segment_sum(x_j * alpha[..., None], dst, num_segments=n)
        return out.reshape(n, H * C) + bias
    edge_index = jnp.stack([src, dst])
    h = jnp.maximum(_layernorm(x, axis=-1), 0.0)
    x = x + _L0_gnn_ref(h, edge_attr_16, src, dst, L0_gnn_W_prop_src, L0_gnn_W_attn_src, L0_gnn_W_attn_dst, L0_gnn_W_attn_edge, L0_gnn_bn_gamma, L0_gnn_bn_beta, L0_gnn_W_agg, L0_gnn_b_agg, L0_gnn_W_apply_dst, L0_gnn_b_apply_dst, L0_gnn_W_apply, L0_gnn_b_apply)
    h = jnp.maximum(_layernorm(x, axis=-1), 0.0)
    x = x + _L1_gnn_ref(h, edge_index, L1_gnn_W_w, L1_gnn_W_b, L1_gnn_a)
    h = jnp.maximum(_layernorm(x, axis=-1), 0.0)
    x = x + _L2_gnn_ref(h, L2_gnn_W_neigh, L2_gnn_W_self, L2_gnn_b_self, src, dst)
    h = jnp.maximum(_layernorm(x, axis=-1), 0.0)
    x = x + _L3_gnn_ref(h, edge_index, edge_weight, L3_gnn_W_l, L3_gnn_b_l, L3_gnn_W_r, L3_gnn_b_r, L3_gnn_att, L3_gnn_bias)
    return x

_drawn_inputs = setup_inputs


def setup_inputs(seed=0):
    import zlib

    import numpy as np

    out = dict(_drawn_inputs(seed))
    spreads = {'L0_gnn_bn_gamma': (1.0, 0.2),
     'L0_gnn_bn_beta': (0.0, 0.1),
     'L0_gnn_b_agg': (0.0, 0.1),
     'L0_gnn_b_apply_dst': (0.0, 0.1),
     'L0_gnn_b_apply': (0.0, 0.1),
     'L1_gnn_W_b': (0.0, 0.1),
     'L2_gnn_b_self': (0.0, 0.1)}
    factors = {'L3_gnn_b_l': 8.0, 'L3_gnn_W_r': 5.105, 'L3_gnn_b_r': 8.0, 'L3_gnn_bias': 8.0}
    for name, (base, spread) in spreads.items():
        noise = np.random.default_rng([zlib.crc32(name.encode()), seed]).standard_normal(out[name].shape)
        drawn = base * np.exp(spread * noise) if base else spread * noise
        out[name] = jnp.asarray(drawn.astype(out[name].dtype))
    for name, factor in factors.items():
        out[name] = (out[name] * factor).astype(out[name].dtype)
    return out
```

```python
import concourse.bass as bass
from concourse import mybir
from contextlib import ExitStack

P = 128
NN = 3125
NE = 53125
D = 256
NT = -(-NN // P)
NP = NT * P
ET = -(-NE // (32 * P)) * 32
EP = ET * P
CU = 16
CI = ET // (2 * CU)
U = 8
SETS = 4
WI = ET // (SETS * U)
RU = 8
RI = ET // (2 * RU)
ACCW = NP + P
TQ = ET // 4
NRW = 10
BIG = 1.0e30
LN_EPS = 1e-5
XLW = D + 8

f32 = mybir.dt.float32
bf16 = mybir.dt.bfloat16
i32 = mybir.dt.int32
ALU = mybir.AluOpType
ACT = mybir.ActivationFunctionType
AX = mybir.AxisListType
IOA = bass.IndirectOffsetOnAxis


class Link:

    def __init__(self, eng, sem):
        self.eng, self.sem, self.n = eng, sem, 0

    def __call__(self, ins):
        ins.then_inc(self.sem, 1)
        self.n += 1
        self.eng.wait_ge(self.sem, self.n)


class Env:
    pass


def bc_mid(ap, n):
    return ap[:, None, :].to_broadcast([ap.shape[0], n, ap.shape[1]])


def bc_last(ap, n):
    return ap[:, :, None].to_broadcast([ap.shape[0], ap.shape[1], n])


def bc_row(ap, n=P):
    return ap[None, :].to_broadcast([n, ap.shape[0]])



def stage_constants(nc, env, A):
    g = env
    ready = g.sem("const_ready")
    loaded = g.sem("index_loaded")
    with nc.Block() as block:
        @block.gpsimd
        def _(e):
            e.iota(g.iota_row[:, :], [[1, P]], base=0, channel_multiplier=0,
                   allow_small_or_imprecise_dtypes=True)
            e.iota(g.iota_p[:, :], [[0, 1]], base=0, channel_multiplier=1,
                   allow_small_or_imprecise_dtypes=True)
            e.memset(g.ones[:, :], 1.0)
            e.memset(g.ident[:, :], 0.0).then_inc(ready, 1)
            e.wait_ge(ready, 1)
            e.affine_select(out=g.ident[:, :], in_=g.ident[:, :], compare_op=ALU.not_equal, fill=1.0,
                            base=0, pattern=[[-1, P]], channel_multiplier=1)
            e.affine_select(out=g.before[:, :], in_=g.ones[:, :], compare_op=ALU.is_ge, fill=0.0,
                            base=-1, pattern=[[-1, P]], channel_multiplier=1)
            e.affine_select(out=g.after[:, :], in_=g.ones[:, :], compare_op=ALU.is_ge, fill=0.0,
                            base=-1, pattern=[[1, P]], channel_multiplier=-1).then_inc(ready, 1)

        @block.sync
        def _(e):
            e.dma_start(g.X[:, :, :], A["x"].rearrange("(j p) d -> p j d", p=P)).then_inc(loaded, 16)
            e.dma_start(g.src_t[:, :], A["src_t"][:, :]).then_inc(loaded, 16)
            e.dma_start(g.dst_t[:, :], A["dst_t"][:, :]).then_inc(loaded, 16)
            e.dma_start(g.src_c[:, :], A["src_c"][:, :]).then_inc(loaded, 16)
            e.wait_ge(loaded, 64)



def stage_norm(nc, env, name, rows=None):
    g = env
    moments, root, linked = g.sem(name + "_moments"), g.sem(name + "_root"), g.sem(name + "_linked")
    h_ready, flipped, kept = g.sem(name + "_h_ready"), g.sem(name + "_flipped"), g.sem(name + "_kept")
    stored = g.sem(name + "_stored")
    with ExitStack() as own:
        H = own.enter_context(nc.sbuf_tensor(name + "_H", [P, NT, D], f32))
        stats = own.enter_context(nc.sbuf_tensor(name + "_stats", [P, NT, 6], f32))
        mv = own.enter_context(nc.sbuf_tensor(name + "_mv", [P, NT, 2], f32))
        rstd = own.enter_context(nc.sbuf_tensor(name + "_rstd", [P, NT], f32))
        shift = own.enter_context(nc.sbuf_tensor(name + "_shift", [P, NT], f32))
        with nc.Block() as block:
            @block.vector
            def _(e):
                link = Link(e, linked)
                for j in range(NT - 1):
                    e.bn_stats(stats[:, j, :], g.X[:, j, :])
                link(e.bn_stats(stats[:, NT - 1, :], g.X[:, NT - 1, :]))
                for j in range(NT - 1):
                    e.bn_aggr(mv[:, j, :], stats[:, j, :])
                link(e.bn_aggr(mv[:, NT - 1, :], stats[:, NT - 1, :]))
                e.tensor_scalar(rstd[:, :], mv[:, :, 1], LN_EPS, None, ALU.add).then_inc(moments, 1)
                e.wait_ge(root, 1)
                link(e.reciprocal(rstd[:, :], rstd[:, :]))
                e.scalar_tensor_tensor(shift[:, :], mv[:, :, 0], -1.0, rstd[:, :], ALU.mult, ALU.mult)\
                    .then_inc(moments, 1)
                for j in range(NT):
                    e.wait_ge(flipped, j + 1)
                    e.tensor_copy(g.HT[:, :, j * P:(j + 1) * P],
                                  g.ps[j % 4][:, 0:D].rearrange("p (h n) -> p h n", h=2)).then_inc(kept, 1)

            @block.scalar
            def _(e):
                e.wait_ge(moments, 1)
                e.activation(rstd[:, :], rstd[:, :], ACT.Sqrt).then_inc(root, 1)
                e.wait_ge(moments, 2)
                for j in range(NT):
                    e.activation(H[:, j, :], g.X[:, j, :], ACT.Relu, bias=shift[:, j:j + 1],
                                 scale=rstd[:, j:j + 1]).then_inc(h_ready, 1)

            @block.tensor
            def _(e):
                for j in range(NT):
                    e.wait_ge(h_ready, j + 1)
                    if j >= 4:
                        e.wait_ge(kept, j - 3)
                    e.transpose(g.ps[j % 4][:, 0:P], H[:, j, 0:P], g.ident[:, :])
                    e.transpose(g.ps[j % 4][:, P:D], H[:, j, P:D], g.ident[:, :]).then_inc(flipped, 1)

            if rows is not None:
                @block.sync
                def _(e):
                    e.wait_ge(h_ready, NT)
                    e.dma_start(rows.rearrange("(j p) d -> p j d", p=P), H[:, :, :]).then_inc(stored, 16)
                    e.wait_ge(stored, 16)


def stage_tables0(nc, env, A):
    g = env
    loaded, product, kept, stored = (g.sem("t0_loaded"), g.sem("t0_product"), g.sem("t0_kept"),
                                     g.sem("t0_stored"))
    with ExitStack() as own:
        W = own.enter_context(nc.sbuf_tensor("t0_W", [P, 2, 24], f32))
        T = own.enter_context(nc.sbuf_tensor("t0_T", [P, NT, 16], f32))
        with nc.Block() as block:
            @block.sync
            def _(e):
                for n, name in enumerate(("L0_gnn_W_attn_src", "L0_gnn_W_prop_src", "L0_gnn_W_attn_dst")):
                    e.dma_start(W[:, :, 8 * n:8 * n + 8],
                                A[name].rearrange("(h p) m -> p h m", p=P)).then_inc(loaded, 16)
                e.wait_ge(kept, NT)
                e.dma_start(g.T0.rearrange("(j p) w -> p j w", p=P), T[:, :, :]).then_inc(stored, 16)
                e.wait_ge(stored, 16)

            @block.tensor
            def _(e):
                e.wait_ge(loaded, 48)
                for j in range(NT):
                    if j >= 4:
                        e.wait_ge(kept, j - 3)
                    for h in range(2):
                        m = e.matmul(g.ps[j % 4][:, 0:24], lhsT=g.HT[:, h, j * P:(j + 1) * P], rhs=W[:, h, :],
                                     start=h == 0, stop=h == 1)
                    m.then_inc(product, 1)

            @block.vector
            def _(e):
                for j in range(NT):
                    e.wait_ge(product, j + 1)
                    e.tensor_copy(T[:, j, :], g.ps[j % 4][:, 0:16])
                    e.tensor_copy(g.AD[:, j, :], g.ps[j % 4][:, 16:24]).then_inc(kept, 1)



class Narrow:

    def __init__(self, g, nc, own, name, w):
        self.idx = own.enter_context(nc.sbuf_tensor(name + "_idx", [P, 2, CU], i32))
        self.rows = own.enter_context(nc.sbuf_tensor(name + "_rows", [P, 2, CU, w], f32))
        self.landed = [g.sem(f"{name}_landed{s}") for s in range(2)]
        self.staged, self.seen = g.sem(name + "_staged"), g.sem(name + "_seen")
        self.collected = g.sem(name + "_collected")


def pool_gather(e, n, index, table, out):

    def issue(turn, s):
        at = turn * (2 * CU) + s * CU
        e.tensor_copy(n.idx[:, s, :], index[:, bass.ds(at, CU)]).then_inc(n.staged, 1)
        e.wait_ge(n.staged, turn * 2 + (s + 1))
        e.sem_inc(n.seen, 1)
        for c in range(CU):
            e.indirect_dma_start(out=n.rows[:, s, c, :], out_offset=None, in_=table,
                                 in_offset=IOA(ap=n.idx[:, s, c:c + 1], axis=0)).then_inc(n.landed[s], 16)

    def collect(turn, s):
        at = turn * (2 * CU) + s * CU
        e.wait_ge(n.landed[s], turn * (16 * CU) + 16 * CU)
        e.tensor_copy(out[:, bass.ds(at, CU), :], n.rows[:, s, :, :]).then_inc(n.collected, 1)
        e.wait_ge(n.collected, turn * 2 + (s + 1))
        e.sem_inc(n.seen, 1)

    issue(0, 0)
    with e.Fori(0, CI - 1) as k:
        issue(k, 1)
        collect(k, 0)
        issue(k + 1, 0)
        collect(k, 1)
    issue(CI - 1, 1)
    collect(CI - 1, 0)
    collect(CI - 1, 1)


def pool_scatter(e, n, index, rows, table):

    def issue(turn, s):
        at = turn * (2 * CU) + s * CU
        e.tensor_copy(n.idx[:, s, :], index[:, bass.ds(at, CU)])
        e.tensor_copy(n.rows[:, s, :, :], rows[:, bass.ds(at, CU), :]).then_inc(n.staged, 1)
        e.wait_ge(n.staged, turn * 2 + (s + 1))
        e.sem_inc(n.seen, 1)
        for c in range(CU):
            e.indirect_dma_start(out=table, out_offset=IOA(ap=n.idx[:, s, c:c + 1], axis=0),
                                 in_=n.rows[:, s, c, :], in_offset=None).then_inc(n.landed[s], 16)

    issue(0, 0)
    issue(0, 1)
    with e.Fori(0, CI - 1) as k:
        for s in range(2):
            e.wait_ge(n.landed[s], k * (16 * CU) + 16 * CU)
            issue(k + 1, s)
    for s in range(2):
        e.wait_ge(n.landed[s], 16 * CU * CI)



def stage_rank(nc, env, A):
    g = env
    sem = g.sem
    linked, digits = sem("rk_linked"), sem("rk_digits")
    hot = [sem(f"rk_hot{s}") for s in range(2)]
    counted, count_kept, total_kept = sem("rk_counted"), sem("rk_count_kept"), sem("rk_total_kept")
    deg_ready, prefixed, starts = sem("rk_deg_ready"), sem("rk_prefixed"), sem("rk_starts")
    row_in = [sem(f"rk_row_in{s}") for s in range(2)]
    row_free = [sem(f"rk_row_free{s}") for s in range(2)]
    base_in = [sem(f"rk_base_in{s}") for s in range(2)]
    base_free = [sem(f"rk_base_free{s}") for s in range(2)]
    onehot_t, looked, looked_free = sem("rk_onehot_t"), sem("rk_looked"), sem("rk_looked_free")
    ranked, turned, out_ready, stored, back = (sem("rk_ranked"), sem("rk_turned"), sem("rk_out_ready"),
                                               sem("rk_stored"), sem("rk_back"))
    with ExitStack() as own:
        def sb(n, shape, dt=f32):
            return own.enter_context(nc.sbuf_tensor("rk_" + n, shape, dt))
        n = Narrow(g, nc, own, "g0", 16)
        di = g.dsts_c
        slo, shi, dlo, dhi = g.od.fm, g.od.fneg, g.od.last, g.od.gm
        onehots = sb("onehots", [P, 4 * RU * P], bf16)
        hot4 = onehots[:, :].rearrange("p (o s i f) -> p o s i f", o=2, s=2, f=P)
        hlo, glo = hot4[:, 0], hot4[:, 1]
        hhi = sb("hhi", [P, 2, RU, NT], bf16)
        ghi = sb("ghi", [P, 2, RU, NT], bf16)
        cnt = sb("cnt", [P, NT, ET], bf16)
        upto = sb("upto", [P, NT, ET])
        unit = g.os.fm
        tot = sb("tot", [P, 2, NT])
        run = sb("run", [P, 2, NT])
        row = sb("row", [P, 2, RU * P], i32)
        rlo = sb("rlo", [P, RU * P], i32)
        base = sb("base", [P, 2, RU, NT])
        match = sb("match", [P, RU, P])
        look = sb("look", [P, RU, NT])
        r2 = sb("r2", [P, RU])
        r1 = sb("r1", [P, RU])
        rank = g.os.fneg
        oht = onehots[:, :].bitcast(f32).rearrange("p (s i f) -> p s i f", s=2, f=P)
        out = rlo[0:TQ, 0:4 * P].rearrange("q (i f) -> q i f", f=P)
        with nc.Block() as block:
            @block.gpsimd
            def _(e):
                pool_gather(e, n, g.src_c, g.T0[:, :], g.GAT)

            @block.sync
            def _(e):
                for s in range(2):
                    e.dma_start(row[:, s, :], bc_row(A["src_row"][s * RU * P:(s + 1) * RU * P]))\
                        .then_inc(row_in[s], 16)
                with e.Fori(0, RI - 1) as k:
                    for s in range(2):
                        e.wait_ge(row_free[s], k + 1)
                        e.dma_start(row[:, s, :],
                                    bc_row(A["src_row"][bass.ds(k * (2 * RU * P) + (2 + s) * RU * P, RU * P)]))\
                            .then_inc(row_in[s], 16)
                e.wait_ge(out_ready, 4)
                e.dma_start(g.RKF.rearrange("(i q p) -> q i p", i=4, p=P), out[:, :, :]).then_inc(stored, 16)
                e.wait_ge(stored, 16)
                e.dma_start(g.rank_c[:, :], g.RKF.rearrange("(p j) -> p j", j=ET)).then_inc(back, 16)
                e.wait_ge(back, 16)

            @block.scalar
            def _(e):
                with e.Fori(0, RI) as k:
                    for s in range(2):
                        e.wait_ge(counted, k * 2 + (s + 1))
                        e.activation(cnt[:, :, bass.ds(k * (2 * RU) + s * RU, RU)],
                                     g.ps[s][:, 0:RU * NT].rearrange("p (i c) -> p c i", c=NT), ACT.Copy)\
                            .then_inc(count_kept, 1)
                e.wait_ge(starts, 1)
                with e.Fori(0, RI) as k:
                    for s in range(2):
                        e.wait_ge(base_free[s], k + 1)
                        e.activation(base[:, s, :, :],
                                     upto[:, :, bass.ds(k * (2 * RU) + s * RU, RU)].rearrange("p c i -> p i c"),
                                     ACT.Copy).then_inc(base_in[s], 1)

            @block.vector
            def _(e):
                link = Link(e, linked)
                for src, lo, hi in ((g.src_t, slo, shi), (g.dst_t, dlo, dhi)):
                    link(e.tensor_single_scalar(di[:, :], src[:, :], P - 1, ALU.bitwise_and))
                    link(e.tensor_copy(lo[:, :], di[:, :]))
                    link(e.tensor_single_scalar(di[:, :], src[:, :], 7, ALU.arith_shift_right))
                    link(e.tensor_copy(hi[:, :], di[:, :]))
                e.memset(unit[:, :], 1.0)
                link(e.memset(g.deg_d[:, :], 0.0))
                with e.Fori(0, RI) as k:
                    for s in range(2):
                        at = bass.ds(k * (2 * RU) + s * RU, RU)
                        e.wait_ge(digits, k * 2 + (s + 1))
                        e.tensor_tensor(hlo[:, s, :, :], bc_mid(g.iota_row[:, :], RU), bc_last(slo[:, at], P),
                                        ALU.is_equal)
                        e.tensor_tensor(hhi[:, s, :, :], bc_mid(g.iota_row[:, 0:NT], RU),
                                        bc_last(shi[:, at], NT), ALU.is_equal)
                        e.tensor_tensor(glo[:, s, :, :], bc_mid(g.iota_row[:, :], RU), bc_last(dlo[:, at], P),
                                        ALU.is_equal)
                        e.tensor_tensor(ghi[:, s, :, :], bc_mid(g.iota_row[:, 0:NT], RU),
                                        bc_last(dhi[:, at], NT), ALU.is_equal).then_inc(hot[s], 1)
                        e.wait_ge(counted, k * 2 + (s + 1))
                        e.wait_ge(total_kept, k * 2 + (s + 1))
                        e.tensor_tensor(g.deg_d[:, :], g.deg_d[:, :], g.ps[2 + s][:, 0:NT], ALU.add)\
                            .then_inc(total_kept, 1)
                e.wait_ge(count_kept, 2 * RI)
                e.wait_ge(total_kept, 2 * RI + 1)
                for c in range(NT - 1):
                    e.tensor_tensor_scan(upto[:, c, :], unit[:, :], cnt[:, c, :], 0.0, ALU.mult, ALU.add)
                link(e.tensor_tensor_scan(upto[:, NT - 1, :], unit[:, :], cnt[:, NT - 1, :], 0.0,
                                          ALU.mult, ALU.add))
                link(e.tensor_copy(g.deg_s[:, :], upto[:, :, ET - 1]))
                link(e.tensor_tensor(upto[:, :, :], upto[:, :, :], cnt[:, :, :], ALU.subtract))
                e.sem_inc(deg_ready, 1)
                e.wait_ge(prefixed, 1)
                for o, start in ((0, g.start_s), (1, g.start_d)):
                    link(e.tensor_copy(tot[:, o, :], g.ps[4][:, (2 * o + 1) * NT:(2 * o + 2) * NT]))
                    link(e.tensor_tensor_scan(run[:, o, :], unit[:, 0:NT], tot[:, o, :], 0.0, ALU.mult, ALU.add))
                    link(e.tensor_tensor(run[:, o, :], run[:, o, :], tot[:, o, :], ALU.subtract))
                    link(e.tensor_tensor(start[:, :], run[:, o, :], g.ps[4][:, 2 * o * NT:(2 * o + 1) * NT],
                                         ALU.add))
                link(e.tensor_tensor(upto[:, :, :], upto[:, :, :], bc_last(g.start_s[:, :], ET), ALU.add))
                e.sem_inc(starts, 1)
                for s in range(2):
                    e.sem_inc(base_free[s], 1)
                with e.Fori(0, RI) as k:
                    for s in range(2):
                        at = bass.ds(k * (2 * RU) + s * RU, RU)
                        e.wait_ge(row_in[s], k * 16 + 16)
                        e.tensor_single_scalar(rlo[:, :], row[:, s, :], P - 1, ALU.bitwise_and)\
                            .then_inc(ranked, 1)
                        e.tensor_tensor(match[:, :, :], row[:, s, :].rearrange("p (i f) -> p i f", f=P),
                                        bc_last(g.src_t[:, at], P), ALU.is_equal).then_inc(ranked, 1)
                        e.wait_ge(ranked, k * 12 + (6 * s + 2))
                        e.tensor_scalar(oht[:, s, :, :].rearrange("p i f -> p (i f)"), rlo[:, :],
                                        g.iota_p[:, 0:1], None, ALU.is_equal).then_inc(onehot_t, 1)
                        e.tensor_tensor(match[:, :, :], match[:, :, :], bc_mid(g.before[:, :], RU), ALU.mult)\
                            .then_inc(ranked, 1)
                        e.tensor_tensor(hhi[:, s, :, :], bc_mid(g.iota_row[:, 0:NT], RU),
                                        bc_last(shi[:, at], NT), ALU.is_equal)
                        e.wait_ge(ranked, k * 12 + (6 * s + 3))
                        e.sem_inc(row_free[s], 1)
                        e.tensor_reduce(r2[:, :], match[:, :, :], AX.X, ALU.add).then_inc(ranked, 1)
                        e.wait_ge(looked, k * 2 + (s + 1))
                        e.wait_ge(ranked, k * 12 + (6 * s + 4))
                        e.tensor_tensor(look[:, :, :], g.ps[s][:, 0:RU * NT].rearrange("p (i c) -> p i c", c=NT),
                                        hhi[:, s, :, :], ALU.mult).then_inc(ranked, 1)
                        e.wait_ge(ranked, k * 12 + (6 * s + 5))
                        e.sem_inc(base_free[s], 1)
                        e.tensor_reduce(r1[:, :], look[:, :, :], AX.X, ALU.add).then_inc(ranked, 1)
                        e.wait_ge(ranked, k * 12 + (6 * s + 6))
                        e.scalar_tensor_tensor(rank[:, at], r1[:, :], 1.0, r2[:, :], ALU.add, ALU.add)\
                            .then_inc(looked_free, 1)
                e.wait_ge(looked_free, 2 * RI)
                for i in range(4):
                    e.wait_ge(turned, i + 1)
                    e.tensor_copy(out[:, i, :], g.ps[i][0:TQ, 0:P]).then_inc(out_ready, 1)
                e.wait_ge(out_ready, 4)

            @block.tensor
            def _(e):
                for s in range(2):
                    e.sem_inc(digits, 1)
                e.sem_inc(total_kept, 1)
                with e.Fori(0, RI) as k:
                    for s in range(2):
                        e.wait_ge(hot[s], k + 1)
                        for i in range(RU):
                            e.matmul(g.ps[s][:, i * NT:(i + 1) * NT], lhsT=hlo[:, s, i, :], rhs=hhi[:, s, i, :],
                                     start=True, stop=True)
                        for i in range(RU):
                            m = e.matmul(g.ps[2 + s][:, 0:NT], lhsT=glo[:, s, i, :], rhs=ghi[:, s, i, :],
                                         start=i == 0, stop=i == RU - 1)
                        m.then_inc(counted, 1)
                        e.wait_ge(counted, k * 2 + (s + 1))
                        e.wait_ge(count_kept, k * 2 + (s + 1))
                        e.wait_ge(total_kept, k * 2 + (s + 2))
                        e.sem_inc(digits, 1)
                e.wait_ge(deg_ready, 1)
                for o, deg in ((0, g.deg_s), (1, g.deg_d)):
                    e.matmul(g.ps[4][:, 2 * o * NT:(2 * o + 1) * NT], lhsT=g.after[:, :], rhs=deg[:, :],
                             start=True, stop=True)
                    m = e.matmul(g.ps[4][:, (2 * o + 1) * NT:(2 * o + 2) * NT], lhsT=g.ones[:, :], rhs=deg[:, :],
                                 start=True, stop=True)
                m.then_inc(prefixed, 1)
                with e.Fori(0, RI) as k:
                    for s in range(2):
                        e.wait_ge(onehot_t, k * 2 + (s + 1))
                        e.wait_ge(base_in[s], k + 1)
                        for i in range(RU):
                            m = e.matmul(g.ps[s][:, i * NT:(i + 1) * NT], lhsT=oht[:, s, i, :],
                                         rhs=base[:, s, i, :], start=True, stop=True)
                        m.then_inc(looked, 1)
                e.wait_ge(looked_free, 2 * RI)
                for i in range(4):
                    e.transpose(g.ps[i][0:TQ, 0:P], rank[:, i * TQ:(i + 1) * TQ], g.ident[:, :])\
                        .then_inc(turned, 1)



class Order:

    def __init__(self, sb, name):
        self.fm, self.fneg, self.last, self.gm = (sb(f"{name}_{x}", [P, ET]) for x in ("fm", "fneg", "last", "gm"))
        self.fmT, self.fnegT, self.gmT = (sb(f"{name}_{x}", [8, P]) for x in ("fmT", "fnegT", "gmT"))


class Asks:

    def __init__(self, e, asked, answered):
        self.e, self.asked, self.answered, self.n = e, asked, answered, 0

    def __call__(self):
        self.e.sem_inc(self.asked, 1)
        self.n += 1
        self.e.wait_ge(self.answered, self.n)


def tensor_flips(e, g, asked, answered, kinds):
    for n, (kind, w) in enumerate(kinds):
        e.wait_ge(asked, n + 1)
        if kind == "in":
            e.transpose(g.ps[6][0:w, 0:P], g.flip_in[:, 0:w], g.ident[:, :]).then_inc(answered, 1)
        else:
            e.transpose(g.ps[7][:, 0:w], g.flip_ex[0:w, 1:P + 1], g.ident[0:w, 0:w]).then_inc(answered, 1)


ORDER_FLIPS = [("in", 8)] * 3


def scan_flips(w, scans):
    return [("in", w), ("ex", w)] * scans


def order_masks(e, g, link, flip, o, key, any_):
    link(e.tensor_tensor(o.last[:, :], key[:, 1:ET + 1], key[:, 2:ET + 2], ALU.not_equal))
    link(e.tensor_tensor(o.fneg[:, :], key[:, 1:ET + 1], key[:, 0:ET], ALU.not_equal))
    link(e.tensor_scalar(o.fm[:, :], o.fneg[:, :], -1.0, 1.0, ALU.mult, ALU.add))
    link(e.tensor_scalar(o.gm[:, :], o.last[:, :], -1.0, 1.0, ALU.mult, ALU.add))
    link(e.tensor_single_scalar(o.fneg[:, :], o.fneg[:, :], -BIG, ALU.mult))
    for mask, row in ((o.fm, o.fmT), (o.fneg, o.fnegT), (o.gm, o.gmT)):
        link(e.tensor_reduce(any_[:, :], mask[:, :], AX.X, ALU.min))
        link(e.tensor_copy(g.flip_in[:, 0:8], any_[:, 0:1].to_broadcast([P, 8])))
        flip()
        link(e.tensor_copy(row[:, :], g.ps[6][0:8, 0:P]))


def seg_scan(e, g, link, flip, w, backward, op0, op1, mask, mask_row, neutral, data, out, carry):

    def rows(first):
        for h in range(w):
            step = slice(None, None, -1) if backward else slice(None)
            ins = e.tensor_tensor_scan(out[:, step, h], mask[:, step], data[:, step, h],
                                       neutral if first else carry[:, h:h + 1], op0, op1)
            if h == w - 1:
                link(ins)

    rows(True)
    link(e.tensor_copy(g.flip_in[:, 0:w], out[:, 0 if backward else ET - 1, 0:w]))
    flip()
    if backward:
        e.memset(g.flip_ex[0:w, P:P + 1], neutral)
        link(e.tensor_tensor_scan(g.flip_ex[0:w, 0:P][:, ::-1], mask_row[0:w, ::-1],
                                  g.ps[6][0:w, 0:P][:, ::-1], neutral, op0, op1))
    else:
        link(e.tensor_tensor_scan(g.flip_ex[0:w, 2:P + 2], mask_row[0:w, :], g.ps[6][0:w, 0:P], neutral,
                                  op0, op1))
        link(e.memset(g.flip_ex[0:w, 1:2], neutral))
    flip()
    link(e.tensor_copy(carry[:, 0:w], g.ps[7][:, 0:w]))
    rows(False)


def seg_softmax(e, g, link, flip, exp, w, o, S, M, V, carry, weight=None, eps=None):
    seg_scan(e, g, link, flip, w, False, ALU.add, ALU.max, o.fneg, o.fnegT, -BIG, S if weight is None else V,
             M, carry)
    link(e.tensor_tensor(V[:, :, :], M[:, :, :], bc_last(o.last[:, :], w), ALU.mult))
    seg_scan(e, g, link, flip, w, True, ALU.mult, ALU.add, o.gm, o.gmT, 0.0, V, M, carry)
    link(e.tensor_tensor(S[:, :, :], S[:, :, :], M[:, :, :], ALU.subtract))
    exp()
    if weight is not None:
        link(e.tensor_tensor(S[:, :, :], S[:, :, :], bc_last(weight, w), ALU.mult))
    seg_scan(e, g, link, flip, w, False, ALU.mult, ALU.add, o.fm, o.fmT, 0.0, S, M, carry)
    link(e.tensor_tensor(V[:, :, :], M[:, :, :], bc_last(o.last[:, :], w), ALU.mult))
    seg_scan(e, g, link, flip, w, True, ALU.mult, ALU.add, o.gm, o.gmT, 0.0, V, M, carry)
    if eps is not None:
        link(e.tensor_single_scalar(M[:, :, :], M[:, :, :], eps, ALU.add))
    link(e.reciprocal(M[:, :, :], M[:, :, :]))
    link(e.tensor_tensor(S[:, :, :], S[:, :, :], M[:, :, :], ALU.mult))



def stage_attr(nc, env, A, REC):
    g = env
    zeroed, loaded, product, kept = (g.sem("at_zeroed"), g.sem("at_loaded"), g.sem("at_product"),
                                     g.sem("at_kept"))
    with ExitStack() as own:
        attr = own.enter_context(nc.sbuf_tensor("at_attr", [P, ET // 8, P], f32))
        W = own.enter_context(nc.sbuf_tensor("at_W", [P, 64], f32))
        with nc.Block() as block:
            @block.sync
            def _(e):
                e.dma_start(attr[:, :, :], A["attr"].rearrange("g r p -> r g p")).then_inc(loaded, 16)
                e.wait_ge(zeroed, 1)
                for n in range(8):
                    e.dma_start(W[16 * n:16 * n + 16, 8 * n:8 * n + 8], A["L0_gnn_W_attn_edge"][:, :])\
                        .then_inc(loaded, 16)

            @block.vector
            def _(e):
                e.memset(W[:, :], 0.0).then_inc(zeroed, 1)
                for n in range(ET // 64 + 1):
                    m = min(64, ET - 64 * n)
                    if m > 0:
                        e.wait_ge(product, n + 1)
                        e.tensor_copy(REC[:, 64 * n:64 * n + m, 2:10],
                                      g.ps[n][:, 0:8 * m].rearrange("p (j h) -> p j h", h=8)).then_inc(kept, 1)

            @block.tensor
            def _(e):
                e.wait_ge(loaded, 16 * 9)
                for n in range(ET // 64 + 1):
                    m = min(64, ET - 64 * n)
                    if m > 0:
                        for q in range(m // 8):
                            last = e.matmul(g.ps[n][:, 64 * q:64 * q + 64], lhsT=attr[:, 8 * n + q, :], rhs=W[:, :],
                                            start=True, stop=True)
                        last.then_inc(product, 1)


def stage_edges0(nc, env, A, REC):
    g = env
    sem = g.sem
    loaded, linked, idx_ready, zero_ready = sem("e0_loaded"), sem("e0_linked"), sem("e0_idx"), sem("e0_zero")
    zeroed, filled, expanded = sem("e0_zeroed"), sem("e0_filled"), sem("e0_expanded")
    asked, answered, exp_asked, exp_done = sem("e0_ask"), sem("e0_answer"), sem("e0_exp_ask"), sem("e0_exp")
    rec_ready, based, border = sem("e0_rec"), sem("e0_based"), sem("e0_border")
    with ExitStack() as own:
        n = Narrow(g, nc, own, "s0", NRW)
        key = own.enter_context(nc.sbuf_tensor("e0_key", [P, ET + 2], i32))
        any_ = own.enter_context(nc.sbuf_tensor("e0_any", [P, 1], f32))
        carry = own.enter_context(nc.sbuf_tensor("e0_carry", [P, 8], f32))
        fsum = own.enter_context(nc.sbuf_tensor("e0_fsum", [P, NT], f32))
        keyf = own.enter_context(nc.sbuf_tensor("e0_keyf", [P, ET], f32))
        mark = own.enter_context(nc.sbuf_tensor("e0_mark", [2, 2], f32))
        with nc.Block() as block:
            @block.sync
            def _(e):
                e.dma_start(key[:, :], A["dst_c"][:, :]).then_inc(loaded, 16)
                e.wait_ge(zero_ready, 1)
                for z in (g.Z8,):
                    e.dma_start(z.rearrange("(p j) w -> p j w", j=ET), g.T1[:, :, :]).then_inc(zeroed, 16)
                e.dma_start(g.RECD[0:1, 0:2], mark[0:1, :]).then_inc(border, 16)
                e.dma_start(g.RECD[EP + 1:EP + 2, 0:2], mark[1:2, :]).then_inc(border, 16)
                e.dma_start(g.PSD[0:1, :], g.T1[0:1, 0, :]).then_inc(border, 16)
                e.wait_ge(filled, 16 * NT)
                e.dma_start(g.T2[:, :, :], g.Z8.rearrange("(p j) w -> p j w", j=ET)).then_inc(expanded, 16)
                e.wait_ge(expanded, 16)
                e.wait_ge(border, 48)

            @block.gpsimd
            def _(e):
                e.wait_ge(idx_ready, 1)
                e.wait_ge(zeroed, 16)
                for j in range(NT):
                    e.indirect_dma_start(out=g.Z8[:, :], out_offset=IOA(ap=g.put_d[:, j:j + 1], axis=0),
                                         in_=g.AD[:, j, :], in_offset=None, bounds_check=EP - 1,
                                         oob_is_err=False).then_inc(filled, 16)
                e.wait_ge(rec_ready, 1)
                pool_scatter(e, n, g.rank_c, REC, g.RECD[:, :])

            @block.scalar
            def _(e):
                e.wait_ge(exp_asked, 1)
                e.activation(g.PD[:, :, :], g.PD[:, :, :], ACT.Exp).then_inc(exp_done, 1)

            @block.vector
            def _(e):
                link = Link(e, linked)
                flip, exp = Asks(e, asked, answered), Asks(e, exp_asked, exp_done)
                e.memset(mark[:, :], -1.0)
                link(e.memset(g.T1[:, :, :], 0.0))
                e.sem_inc(zero_ready, 1)
                for deg, start, put, end in ((g.deg_d, g.start_d, g.put_d, g.end_d),
                                             (g.deg_s, g.start_s, g.put_s, g.end_s)):
                    link(e.tensor_single_scalar(fsum[:, :], deg[:, :], 0.0, ALU.is_equal))
                    link(e.scalar_tensor_tensor(fsum[:, :], fsum[:, :], float(EP), start[:, :], ALU.mult, ALU.add))
                    link(e.tensor_copy(put[:, :], fsum[:, :]))
                    link(e.scalar_tensor_tensor(fsum[:, :], start[:, :], -1.0, deg[:, :], ALU.add, ALU.add))
                    link(e.tensor_single_scalar(fsum[:, :], fsum[:, :], 0.0, ALU.max))
                    link(e.tensor_copy(end[:, :], fsum[:, :]))
                e.sem_inc(idx_ready, 1)
                e.wait_ge(loaded, 16)
                order_masks(e, g, link, flip, g.od, key, any_)
                link(e.tensor_copy(keyf[:, :], g.dst_t[:, :]))
                link(e.tensor_copy(g.base_d[0:1, :], g.dst_t[0:1, :]))
                flip()
                link(e.tensor_tensor(g.lrel_d[:, :], keyf[:, :], g.ps[5][:, 0:ET], ALU.subtract))
                link(e.tensor_scalar(g.win_d[:, :], g.ps[5][:, 0:ET], g.iota_p[:, 0:1], None, ALU.add))
                link(e.tensor_copy(REC[:, :, 0], g.src_c[:, :]))
                link(e.tensor_copy(REC[:, :, 1], key[:, 1:ET + 1]))
                e.wait_ge(expanded, 16)
                seg_scan(e, g, link, flip, 8, False, ALU.mult, ALU.add, g.od.fm, g.od.fmT, 0.0, g.T2, g.T1, carry)
                E = REC[:, :, 2:10]
                link(e.tensor_tensor(E, E, g.GAT[:, :, 0:8], ALU.add))
                link(e.tensor_tensor(E, E, g.T1[:, :, :], ALU.add))
                link(e.scalar_tensor_tensor(E, E, 0.2, E, ALU.mult, ALU.max))
                e.sem_inc(rec_ready, 1)
                link(e.tensor_copy(g.PD[:, :, :], E))
                seg_softmax(e, g, link, flip, exp, 8, g.od, g.PD, g.T1, g.T2, carry)

            @block.tensor
            def _(e):
                kinds = ORDER_FLIPS + [("base", 0)] + scan_flips(8, 5)
                for k, (kind, w) in enumerate(kinds):
                    e.wait_ge(asked, k + 1)
                    if kind == "base":
                        e.matmul(g.ps[5][:, 0:ET], lhsT=g.ones[0:1, :], rhs=keyf[0:1, :], start=True, stop=True)\
                            .then_inc(answered, 1)
                    elif kind == "in":
                        e.transpose(g.ps[6][0:w, 0:P], g.flip_in[:, 0:w], g.ident[:, :]).then_inc(answered, 1)
                    else:
                        e.transpose(g.ps[7][:, 0:w], g.flip_ex[0:w, 1:P + 1], g.ident[0:w, 0:w])\
                            .then_inc(answered, 1)


def stage_by_src(nc, env):
    g = env
    sem = g.sem
    loaded, linked, asked, answered = sem("bs_loaded"), sem("bs_linked"), sem("bs_ask"), sem("bs_answer")
    exp_asked, exp_done, keys_ready, keys_out = sem("bs_exp_ask"), sem("bs_exp"), sem("bs_keys"), sem("bs_out")
    slices, turned, based, soft, stored = (sem("bs_slices"), sem("bs_turned"), sem("bs_based"), sem("bs_soft"),
                                           sem("bs_stored"))
    with ExitStack() as own:
        def sb(name, shape, dt=f32):
            return own.enter_context(nc.sbuf_tensor("bs_" + name, shape, dt))
        RC = sb("RC", [P, ET + 2, NRW])
        keys = sb("keys", [P, 2, ET])
        part = sb("part", [TQ, 2, 4, P])
        tiles = sb("tiles", [P, 2, ET])
        any_, carry = sb("any", [P, 1]), sb("carry", [P, 8])
        with nc.Block() as block:
            @block.sync
            def _(e):
                e.dma_start(RC[:, 1:ET + 1, :], g.RECD[1:EP + 1, :].rearrange("(p j) w -> p j w", j=ET))\
                    .then_inc(loaded, 16)
                e.dma_start(RC[:, 0:1, 0:2], g.RECD[0:EP, :].rearrange("(p j) w -> p j w", j=ET)[:, 0:1, 0:2])\
                    .then_inc(loaded, 16)
                e.dma_start(RC[:, ET + 1:ET + 2, 0:2],
                            g.RECD[2:EP + 2, :].rearrange("(p j) w -> p j w", j=ET)[:, ET - 1:ET, 0:2])\
                    .then_inc(loaded, 16)
                e.wait_ge(keys_ready, 1)
                e.dma_start(g.KEYD.rearrange("n (p j) -> p n j", j=ET), keys[:, :, :]).then_inc(keys_out, 16)
                e.wait_ge(keys_out, 16)
                for m in range(2):
                    e.dma_start(part[:, m, :, :], g.KEYD[m, :].rearrange("(i q p) -> q i p", i=4, p=P))\
                        .then_inc(slices, 16)
                e.wait_ge(soft, 1)
                e.dma_start(g.PSD[1:EP + 1, :].rearrange("(p j) w -> p j w", j=ET), g.T3[:, :, :])\
                    .then_inc(stored, 16)
                e.wait_ge(stored, 16)

            @block.scalar
            def _(e):
                e.wait_ge(exp_asked, 1)
                e.activation(g.T3[:, :, :], g.T3[:, :, :], ACT.Exp).then_inc(exp_done, 1)

            @block.vector
            def _(e):
                link = Link(e, linked)
                flip, exp = Asks(e, asked, answered), Asks(e, exp_asked, exp_done)
                e.wait_ge(loaded, 48)
                e.tensor_copy(keys[:, 0, :], RC[:, 1:ET + 1, 0])
                link(e.tensor_copy(keys[:, 1, :], RC[:, 1:ET + 1, 1]))
                e.sem_inc(keys_ready, 1)
                link(e.tensor_copy(g.dsts_c[:, :], keys[:, 1, :]))
                order_masks(e, g, link, flip, g.os, RC[:, :, 0], any_)
                for m in range(2):
                    e.wait_ge(turned, 2)
                    for i in range(4):
                        ins = e.tensor_copy(tiles[:, m, i * TQ:(i + 1) * TQ], g.ps[i][:, m * P:m * P + TQ])
                    link(ins)
                link(e.tensor_copy(g.dsts_t[:, :], tiles[:, 1, :]))
                link(e.tensor_copy(g.base_s[0:1, :], tiles[0:1, 0, :]))
                flip()
                link(e.tensor_tensor(g.lrel_s[:, :], tiles[:, 0, :], g.ps[5][:, 0:ET], ALU.subtract))
                link(e.tensor_copy(g.T3[:, :, :], RC[:, 1:ET + 1, 2:10]))
                seg_softmax(e, g, link, flip, exp, 8, g.os, g.T3, g.T1, g.T2, carry)
                e.sem_inc(soft, 1)

            @block.tensor
            def _(e):
                def turn(m):
                    e.wait_ge(slices, 16 * (m + 1) if m else 32)
                    for i in range(4):
                        ins = e.transpose(g.ps[i][:, m * P:m * P + TQ], part[:, m, i, :], g.ident[0:TQ, 0:TQ])
                    ins.then_inc(turned, 1)

                kinds = ORDER_FLIPS + [("base", 0)] + scan_flips(8, 4)
                for k, (kind, w) in enumerate(kinds):
                    if kind == "base":
                        turn(0)
                        turn(1)
                    e.wait_ge(asked, k + 1)
                    if kind == "base":
                        e.matmul(g.ps[5][:, 0:ET], lhsT=g.ones[0:1, :], rhs=tiles[0:1, 0, :],
                                 start=True, stop=True).then_inc(answered, 1)
                    elif kind == "in":
                        e.transpose(g.ps[6][0:w, 0:P], g.flip_in[:, 0:w], g.ident[:, :]).then_inc(answered, 1)
                    else:
                        e.transpose(g.ps[7][:, 0:w], g.flip_ex[0:w, 1:P + 1], g.ident[0:w, 0:w])\
                            .then_inc(answered, 1)


def stage_messages0(nc, env):
    g = env
    sem = g.sem
    linked, asked, answered = sem("m0_linked"), sem("m0_ask"), sem("m0_answer")
    got, root_asked, root_done, summed, stored, rows_in = (sem("m0_got"), sem("m0_root_ask"), sem("m0_root"),
                                                           sem("m0_summed"), sem("m0_stored"), sem("m0_rows"))
    with ExitStack() as own:
        n = Narrow(g, nc, own, "g1", 8)
        carry = own.enter_context(nc.sbuf_tensor("m0_carry", [P, 8], f32))
        with nc.Block() as block:
            @block.gpsimd
            def _(e):
                pool_gather(e, n, g.rank_c, g.PSD[:, :], g.T3)
                e.sem_inc(got, 1)
                e.wait_ge(stored, 16)
                for j in range(NT):
                    e.indirect_dma_start(out=g.MSG[:, j, :], out_offset=None, in_=g.MSD[:, :],
                                         in_offset=IOA(ap=g.end_d[:, j:j + 1], axis=0)).then_inc(rows_in, 16)
                e.wait_ge(rows_in, 16 * NT)

            @block.scalar
            def _(e):
                e.wait_ge(root_asked, 1)
                e.activation(g.PD[:, :, :], g.PD[:, :, :], ACT.Sqrt).then_inc(root_done, 1)

            @block.vector
            def _(e):
                link = Link(e, linked)
                flip, root = Asks(e, asked, answered), Asks(e, root_asked, root_done)
                link(e.tensor_single_scalar(g.PD[:, :, :], g.PD[:, :, :], 1e-9, ALU.max))
                e.wait_ge(got, 1)
                link(e.scalar_tensor_tensor(g.PD[:, :, :], g.T3[:, :, :], 1e-9, g.PD[:, :, :], ALU.max, ALU.mult))
                root()
                link(e.tensor_tensor(g.PD[:, :, :], g.PD[:, :, :], g.GAT[:, :, 8:16], ALU.mult))
                seg_scan(e, g, link, flip, 8, False, ALU.mult, ALU.add, g.od.fm, g.od.fmT, 0.0, g.PD, g.T1, carry)
                e.sem_inc(summed, 1)
                e.wait_ge(rows_in, 16 * NT)
                link(e.tensor_single_scalar(g.T3[:, 0:NT, 0], g.deg_d[:, :], 0.0, ALU.is_gt))
                link(e.tensor_tensor(g.MSG[:, :, :], g.MSG[:, :, :], bc_last(g.T3[:, 0:NT, 0], 8), ALU.mult))

            @block.sync
            def _(e):
                e.wait_ge(summed, 1)
                e.dma_start(g.MSD.rearrange("(p j) w -> p j w", j=ET), g.T1[:, :, :]).then_inc(stored, 16)
                e.wait_ge(stored, 16)

            @block.tensor
            def _(e):
                tensor_flips(e, g, asked, answered, scan_flips(8, 1))



def stage_update0(nc, env, A):
    g = env
    sem = g.sem
    loaded, flipped, kept, linked, asked, root_done = (sem("u0_loaded"), sem("u0_flipped"), sem("u0_kept"),
                                                       sem("u0_linked"), sem("u0_ask"), sem("u0_root"))
    ready, first, act_in, turned, act_t, second, done = (sem("u0_ready"), sem("u0_first"), sem("u0_act"),
                                                         sem("u0_turned"), sem("u0_act_t"), sem("u0_second"),
                                                         sem("u0_done"))
    with ExitStack() as own:
        def sb(name, shape):
            return own.enter_context(nc.sbuf_tensor("u0_" + name, shape, f32))
        M, C = sb("M", [8, NP]), sb("C", [8, NP])
        st = sb("st", [8, 8])
        Wa, Wd, Wo = sb("Wa", [8, D]), sb("Wd", [P, 2, D]), sb("Wo", [P, 2, D])
        b1, b2, bo = sb("b1", [P, D]), sb("b2", [P, D]), sb("bo", [P, D])
        R, Q, RT = sb("R", [P, 2, D]), sb("Q", [P, 2, D]), sb("RT", [P, 2, D])
        with nc.Block() as block:
            @block.sync
            def _(e):
                e.dma_start(Wa[:, :], A["L0_gnn_W_agg"][:, :]).then_inc(loaded, 16)
                e.dma_start(Wd[:, :, :], A["L0_gnn_W_apply_dst"].rearrange("(h p) m -> p h m", p=P))\
                    .then_inc(loaded, 16)
                e.dma_start(Wo[:, :, :], A["L0_gnn_W_apply"].rearrange("(h p) m -> p h m", p=P))\
                    .then_inc(loaded, 16)
                e.dma_start(b1[:, :], bc_row(A["L0_gnn_b_agg"])).then_inc(loaded, 16)
                e.dma_start(b2[:, :], bc_row(A["L0_gnn_b_apply_dst"])).then_inc(loaded, 16)
                e.dma_start(bo[:, :], bc_row(A["L0_gnn_b_apply"])).then_inc(loaded, 16)
                e.dma_start(st[:, 6:7], A["L0_gnn_bn_gamma"][:, None]).then_inc(loaded, 16)
                e.dma_start(st[:, 7:8], A["L0_gnn_bn_beta"][:, None]).then_inc(loaded, 16)

            @block.scalar
            def _(e):
                e.wait_ge(asked, 1)
                e.activation(st[:, 2:3], st[:, 1:2], ACT.Sqrt).then_inc(root_done, 1)
                for j in range(NT):
                    e.wait_ge(turned, j + 1)
                    if j >= 2:
                        e.wait_ge(second, j - 1)
                    e.activation(RT[:, j % 2, :], g.ps[2 + j % 2][:, 0:D], ACT.Copy).then_inc(act_t, 1)

            @block.vector
            def _(e):
                link = Link(e, linked)
                for q in range(7):
                    e.wait_ge(flipped, q + 1)
                    m = min(4, NT - 4 * q)
                    link(e.tensor_copy(M[:, q * 4 * P:(q * 4 + m) * P], g.ps[q][0:8, 0:m * P]))
                link(e.tensor_reduce(st[:, 0:1], M[:, 0:NN], AX.X, ALU.add))
                link(e.tensor_single_scalar(st[:, 0:1], st[:, 0:1], 1.0 / NN, ALU.mult))
                link(e.tensor_scalar(M[:, :], M[:, :], st[:, 0:1], None, ALU.subtract))
                link(e.tensor_tensor(C[:, 0:NN], M[:, 0:NN], M[:, 0:NN], ALU.mult))
                link(e.tensor_reduce(st[:, 1:2], C[:, 0:NN], AX.X, ALU.add))
                link(e.tensor_scalar(st[:, 1:2], st[:, 1:2], 1.0 / NN, LN_EPS, ALU.mult, ALU.add))
                e.wait_ge(loaded, 128)
                e.sem_inc(asked, 1)
                e.wait_ge(root_done, 1)
                link(e.reciprocal(st[:, 3:4], st[:, 2:3]))
                link(e.tensor_tensor(st[:, 4:5], st[:, 3:4], st[:, 6:7], ALU.mult))
                link(e.tensor_scalar(M[:, :], M[:, :], st[:, 4:5], st[:, 7:8], ALU.mult, ALU.add))
                link(e.tensor_tensor(b1[:, :], b1[:, :], b2[:, :], ALU.add))
                link(e.tensor_tensor(g.X[:, :, :], g.X[:, :, :], bc_mid(bo[:, :], NT), ALU.add))
                e.sem_inc(ready, 1)
                for j in range(NT + 2):
                    if j < NT:
                        e.wait_ge(first, j + 1)
                        link(e.tensor_tensor(Q[:, j % 2, :], g.ps[j % 2][:, 0:D], b1[:, :], ALU.add))
                        if j >= 2:
                            e.wait_ge(turned, j - 1)
                        e.scalar_tensor_tensor(R[:, j % 2, :], Q[:, j % 2, :], 0.2, Q[:, j % 2, :], ALU.mult,
                                               ALU.max).then_inc(act_in, 1)
                    if j >= 2:
                        i = j - 2
                        e.wait_ge(second, i + 1)
                        e.tensor_tensor(g.X[:, i, :], g.X[:, i, :], g.ps[4 + i % 2][:, 0:D], ALU.add)\
                            .then_inc(done, 1)

            @block.tensor
            def _(e):
                for q in range(7):
                    m = min(4, NT - 4 * q)
                    for i in range(m):
                        last = e.transpose(g.ps[q][0:8, i * P:(i + 1) * P], g.MSG[:, 4 * q + i, :], g.ident[:, :])
                    last.then_inc(flipped, 1)
                e.wait_ge(ready, 1)
                for j in range(NT + 2):
                    if j < NT:
                        if j >= 2:
                            e.wait_ge(act_in, j - 1)
                        at = slice(j * P, (j + 1) * P)
                        e.matmul(g.ps[j % 2][:, 0:D], lhsT=M[:, at], rhs=Wa[:, :], start=True, stop=False)
                        e.matmul(g.ps[j % 2][:, 0:D], lhsT=g.HT[:, 0, at], rhs=Wd[:, 0, :], start=False, stop=False)
                        e.matmul(g.ps[j % 2][:, 0:D], lhsT=g.HT[:, 1, at], rhs=Wd[:, 1, :], start=False, stop=True)\
                            .then_inc(first, 1)
                    if 1 <= j <= NT:
                        i = j - 1
                        e.wait_ge(act_in, i + 1)
                        if i >= 2:
                            e.wait_ge(act_t, i - 1)
                        e.transpose(g.ps[2 + i % 2][:, 0:P], R[:, i % 2, 0:P], g.ident[:, :])
                        e.transpose(g.ps[2 + i % 2][:, P:D], R[:, i % 2, P:D], g.ident[:, :]).then_inc(turned, 1)
                    if j >= 2:
                        i = j - 2
                        e.wait_ge(act_t, i + 1)
                        if i >= 2:
                            e.wait_ge(done, i - 1)
                        e.matmul(g.ps[4 + i % 2][:, 0:D], lhsT=RT[:, i % 2, 0:P], rhs=Wo[:, 0, :], start=True,
                                 stop=False)
                        e.matmul(g.ps[4 + i % 2][:, 0:D], lhsT=RT[:, i % 2, P:D], rhs=Wo[:, 1, :], start=False,
                                 stop=True).then_inc(second, 1)



def stage_project(nc, env, A, name, weight, bias, vec, groups, scale, T, V, table, row, finish=None):
    g = env
    sem = g.sem
    loaded, product, kept, linked, ready, stored = (sem(name + x) for x in ("_loaded", "_product", "_kept",
                                                                           "_linked", "_ready", "_stored"))
    with ExitStack() as own:
        W = own.enter_context(nc.sbuf_tensor(name + "_W", [P, 2, D], f32))
        b = own.enter_context(nc.sbuf_tensor(name + "_b", [P, D], f32))
        v = own.enter_context(nc.sbuf_tensor(name + "_v", [P, len(vec), D], f32))
        tmp = own.enter_context(nc.sbuf_tensor(name + "_tmp", [P, NT, D], f32))
        with nc.Block() as block:
            @block.sync
            def _(e):
                e.dma_start(W[:, :, :], weight.rearrange("(h p) m -> p h m", p=P)).then_inc(loaded, 16)
                e.dma_start(b[:, :], bc_row(bias)).then_inc(loaded, 16)
                n = 2
                for q, parts in enumerate(vec):
                    for at, part in parts:
                        e.dma_start(v[:, q, at:at + part.shape[0]], bc_row(part)).then_inc(loaded, 16)
                        n += 1
                e.wait_ge(loaded, 16 * n)
                e.sem_inc(ready, 1)
                e.wait_ge(ready, 2)
                e.dma_start(table.rearrange("(j p) d -> p j d", p=P), T[:, :, 0:row]).then_inc(stored, 16)
                e.wait_ge(stored, 16)

            @block.tensor
            def _(e):
                e.wait_ge(ready, 1)
                for j in range(NT):
                    if j >= 4:
                        e.wait_ge(kept, j - 3)
                    for h in range(2):
                        m = e.matmul(g.ps[j % 4][:, 0:D], lhsT=g.HT[:, h, j * P:(j + 1) * P], rhs=W[:, h, :],
                                     start=h == 0, stop=h == 1)
                    m.then_inc(product, 1)

            @block.vector
            def _(e):
                link = Link(e, linked)
                e.wait_ge(ready, 1)
                for j in range(NT):
                    e.wait_ge(product, j + 1)
                    e.tensor_tensor(T[:, j, 0:D], g.ps[j % 4][:, 0:D], b[:, :], ALU.add).then_inc(kept, 1)
                e.wait_ge(kept, NT)
                for q in range(len(vec)):
                    link(e.tensor_tensor(tmp[:, :, :], T[:, :, 0:D], bc_mid(v[:, q, :], NT), ALU.mult))
                    link(e.tensor_reduce(V[q], tmp[:, :, :].rearrange("p j (n c) -> p j n c", n=groups), AX.X,
                                         ALU.add))
                    if scale != 1.0:
                        link(e.tensor_single_scalar(V[q], V[q], scale, ALU.mult))
                e.sem_inc(ready, 1)



def stage_edges1(nc, env, SN, TN, AL):
    g = env
    sem = g.sem
    linked, asked, answered, exp_asked, exp_done = (sem("e1_linked"), sem("e1_ask"), sem("e1_answer"),
                                                    sem("e1_exp_ask"), sem("e1_exp"))
    zero_ready, zeroed, filled, expanded, got, soft, stored, tabled = (
        sem("e1_zero"), sem("e1_zeroed"), sem("e1_filled"), sem("e1_expanded"), sem("e1_got"), sem("e1_soft"),
        sem("e1_stored"), sem("e1_tabled"))
    with ExitStack() as own:
        def sb(name, shape, dt=f32):
            return own.enter_context(nc.sbuf_tensor("e1_" + name, shape, dt))
        n = Narrow(g, nc, own, "g2", 2)
        S, M, V, TG = (sb(x, [P, ET, 2]) for x in ("S", "M", "V", "TG"))
        carry = sb("carry", [P, 8])
        with nc.Block() as block:
            @block.sync
            def _(e):
                e.dma_start(g.TND.rearrange("(j p) w -> p j w", p=P), TN[:, :, :]).then_inc(tabled, 16)
                e.wait_ge(zero_ready, 1)
                e.dma_start(g.Z2.rearrange("(p j) w -> p j w", j=ET), V[:, :, :]).then_inc(zeroed, 16)
                e.wait_ge(filled, 16 * NT)
                e.dma_start(M[:, :, :], g.Z2.rearrange("(p j) w -> p j w", j=ET)).then_inc(expanded, 16)
                e.wait_ge(soft, 1)
                e.dma_start(AL.rearrange("(p j) w -> p j w", j=ET), TG[:, :, :]).then_inc(stored, 16)
                e.wait_ge(stored, 16)

            @block.gpsimd
            def _(e):
                e.wait_ge(zeroed, 16)
                for j in range(NT):
                    e.indirect_dma_start(out=g.Z2[:, :], out_offset=IOA(ap=g.put_s[:, j:j + 1], axis=0),
                                         in_=SN[:, j, :], in_offset=None, bounds_check=EP - 1,
                                         oob_is_err=False).then_inc(filled, 16)
                e.wait_ge(tabled, 16)
                pool_gather(e, n, g.dsts_c, g.TND[:, :], TG)
                e.sem_inc(got, 1)

            @block.scalar
            def _(e):
                e.wait_ge(exp_asked, 1)
                e.activation(TG[:, :, :], TG[:, :, :], ACT.Exp).then_inc(exp_done, 1)

            @block.vector
            def _(e):
                link = Link(e, linked)
                flip, exp = Asks(e, asked, answered), Asks(e, exp_asked, exp_done)
                link(e.memset(V[:, :, :], 0.0))
                e.sem_inc(zero_ready, 1)
                e.wait_ge(expanded, 16)
                seg_scan(e, g, link, flip, 2, False, ALU.mult, ALU.add, g.os.fm, g.os.fmT, 0.0, M, S, carry)
                e.wait_ge(got, 1)
                link(e.tensor_tensor(TG[:, :, :], TG[:, :, :], S[:, :, :], ALU.add))
                link(e.scalar_tensor_tensor(TG[:, :, :], TG[:, :, :], 0.2, TG[:, :, :], ALU.mult, ALU.max))
                seg_softmax(e, g, link, flip, exp, 2, g.os, TG, M, V, carry)
                e.sem_inc(soft, 1)

            @block.tensor
            def _(e):
                tensor_flips(e, g, asked, answered, scan_flips(2, 5))



def stage_aggregate(nc, env, name, table, row, index, lrel, base, acc, weights=None, heads=0):
    g = env
    sem = g.sem
    landed, hot, scaled, w_in = ([sem(f"{name}_{x}{s}") for s in range(SETS)]
                                 for x in ("landed", "hot", "scaled", "w_in"))
    staged, seen, masked = sem(name + "_staged"), sem(name + "_seen"), sem(name + "_masked")
    summed, added = sem(name + "_summed"), sem(name + "_added")
    CREDIT = SETS * U
    with ExitStack() as own:
        def sb(n, shape, dt=f32):
            return own.enter_context(nc.sbuf_tensor(f"{name}_{n}", shape, dt))
        idx = sb("idx", [P, SETS, U], i32)
        G = sb("G", [P, SETS, U, row])
        plane = 2 if heads == 2 else 1
        OH = sb("OH", [P, SETS, plane, U, P])
        W = sb("W", [P, SETS, U, max(heads, 1)])
        with nc.Block() as block:
            @block.gpsimd
            def _(e):
                with e.Fori(0, WI) as k:
                    for s in range(SETS):
                        e.wait_ge(summed, k * CREDIT + (s + 1) * U)
                        e.tensor_copy(idx[:, s, :], index[:, bass.ds(k * (SETS * U) + s * U, U)])\
                            .then_inc(staged, 1)
                        e.wait_ge(staged, k * SETS + (s + 1))
                        e.sem_inc(seen, 1)
                        for i in range(U):
                            e.indirect_dma_start(out=G[:, s, i, :], out_offset=None, in_=table,
                                                 in_offset=IOA(ap=idx[:, s, i:i + 1], axis=0))\
                                .then_inc(landed[s], 16)

            if weights is not None:
                @block.sync
                def _(e):
                    w_t = weights.rearrange("(t p) w -> p t w", p=P)
                    with e.Fori(0, WI) as k:
                        for s in range(SETS):
                            e.wait_ge(summed, k * CREDIT + (s + 1) * U)
                            e.dma_start(W[:, s, :, :], w_t[:, bass.ds(k * (SETS * U) + s * U, U), :])\
                                .then_inc(w_in[s], 16)

            @block.vector
            def _(e):
                e.memset(acc[:, 0, :], 0.0)
                e.memset(acc[:, 1, :], 0.0).then_inc(added, 1)
                for n in range(3):
                    e.sem_inc(added, 1)

                def prepare(k, s):
                    at = bass.ds(k * CREDIT + s * U, U)
                    e.wait_ge(summed, k * CREDIT + (s + 1) * U)
                    if weights is not None:
                        e.wait_ge(w_in[s], k * 16 + 16)
                    if heads == 2:
                        e.tensor_tensor(OH[:, s, 0, :, :], bc_mid(g.iota_row[:, :], U), bc_last(lrel[:, at], P),
                                        ALU.is_equal).then_inc(masked, 1)
                        e.wait_ge(masked, k * (2 * SETS) + (2 * s + 1))
                        e.tensor_tensor(OH[:, s, 1, :, :], OH[:, s, 0, :, :], bc_last(W[:, s, :, 1], P), ALU.mult)\
                            .then_inc(masked, 1)
                        e.wait_ge(masked, k * (2 * SETS) + (2 * s + 2))
                        e.tensor_tensor(OH[:, s, 0, :, :], OH[:, s, 0, :, :], bc_last(W[:, s, :, 0], P), ALU.mult)\
                            .then_inc(hot[s], 1)
                    else:
                        e.tensor_tensor(OH[:, s, 0, :, :], bc_mid(g.iota_row[:, :], U), bc_last(lrel[:, at], P),
                                        ALU.is_equal).then_inc(hot[s], 1)
                    if heads == 8:
                        e.wait_ge(landed[s], k * (16 * U) + 16 * U)
                        v = G[:, s, :, 0:D].rearrange("p i (h c) -> p i h c", h=8)
                        e.tensor_tensor(v, v, W[:, s, :, :][:, :, :, None].to_broadcast([P, U, 8, D // 8]),
                                        ALU.mult).then_inc(scaled[s], 1)

                def turn(k, last=False):
                    for s in range(SETS):
                        if s < SETS - 1:
                            prepare(k, s + 1)
                        elif not last:
                            prepare(k + 1, 0)
                        _, places = nc.values_load_multi_w_load_instructions(
                            base[0:1, bass.ds(k * CREDIT + s * U, U)], engines=[mybir.EngineType.DVE],
                            min_val=0, max_val=NP - 1)
                        for i in range(U):
                            t = k * CREDIT + (s * U + i)
                            e.wait_ge(summed, t + (CREDIT + 1))
                            e.wait_ge(added, t + 4)
                            w = acc[:, :, bass.ds(places[i], P)]
                            e.tensor_tensor(w, w, g.ps[i % 4][:, 0:D].rearrange("p (h n) -> p h n", h=2), ALU.add)\
                                .then_inc(added, 1)

                prepare(0, 0)
                with e.Fori(0, WI - 1) as k:
                    turn(k)
                turn(WI - 1, last=True)

            @block.tensor
            def _(e):
                for n in range(CREDIT):
                    e.sem_inc(summed, 1)
                with e.Fori(0, WI) as k:
                    for s in range(SETS):
                        e.wait_ge(hot[s], k + 1)
                        if heads == 8:
                            e.wait_ge(scaled[s], k + 1)
                        else:
                            e.wait_ge(landed[s], k * (16 * U) + 16 * U)
                        for i in range(U):
                            t = k * (SETS * U) + (s * U + i)
                            e.wait_ge(added, t + 1)
                            for h in range(2):
                                m = e.matmul(g.ps[i % 4][:, h * P:(h + 1) * P], lhsT=G[:, s, i, h * P:(h + 1) * P],
                                             rhs=OH[:, s, h if heads == 2 else 0, i, :], start=True, stop=True)
                            m.then_inc(summed, 1)


def stage_update1(nc, env, acc):
    g = env
    loaded, linked, turned, done = g.sem("u1_loaded"), g.sem("u1_linked"), g.sem("u1_turned"), g.sem("u1_done")
    with ExitStack() as own:
        WH = own.enter_context(nc.sbuf_tensor("u1_WH", [P, NT, D], f32))
        lone = own.enter_context(nc.sbuf_tensor("u1_lone", [P, NT], f32))
        with nc.Block() as block:
            @block.sync
            def _(e):
                e.dma_start(WH[:, :, :], g.WHD.rearrange("(j p) d -> p j d", p=P)).then_inc(loaded, 16)

            @block.tensor
            def _(e):
                for j in range(NT):
                    if j >= 4:
                        e.wait_ge(done, j - 3)
                    for h in range(2):
                        m = e.transpose(g.ps[j % 4][:, h * P:(h + 1) * P], acc[:, h, j * P:(j + 1) * P],
                                        g.ident[:, :])
                    m.then_inc(turned, 1)

            @block.vector
            def _(e):
                link = Link(e, linked)
                link(e.tensor_single_scalar(lone[:, :], g.deg_s[:, :], 0.0, ALU.is_equal))
                e.wait_ge(loaded, 16)
                link(e.tensor_tensor(WH[:, :, :], WH[:, :, :], bc_last(lone[:, :], D), ALU.mult))
                link(e.tensor_tensor(g.X[:, :, :], g.X[:, :, :], WH[:, :, :], ALU.add))
                for j in range(NT):
                    e.wait_ge(turned, j + 1)
                    e.tensor_tensor(g.X[:, j, :], g.X[:, j, :], g.ps[j % 4][:, 0:D], ALU.add).then_inc(done, 1)


def stage_update2(nc, env, A, acc):
    g = env
    loaded, linked, product, done, added = (g.sem("u2_loaded"), g.sem("u2_linked"), g.sem("u2_product"),
                                            g.sem("u2_done"), g.sem("u2_added"))
    with ExitStack() as own:
        Wn = own.enter_context(nc.sbuf_tensor("u2_Wn", [P, 2, D], f32))
        Ws = own.enter_context(nc.sbuf_tensor("u2_Ws", [P, 2, D], f32))
        b = own.enter_context(nc.sbuf_tensor("u2_b", [P, D], f32))
        rdeg = own.enter_context(nc.sbuf_tensor("u2_rdeg", [P, NT], f32))
        with nc.Block() as block:
            @block.sync
            def _(e):
                e.dma_start(Wn[:, :, :], A["L2_gnn_W_neigh"].rearrange("(h p) m -> p h m", p=P)).then_inc(loaded, 16)
                e.dma_start(Ws[:, :, :], A["L2_gnn_W_self"].rearrange("(h p) m -> p h m", p=P)).then_inc(loaded, 16)
                e.dma_start(b[:, :], bc_row(A["L2_gnn_b_self"])).then_inc(loaded, 16)

            @block.tensor
            def _(e):
                e.wait_ge(loaded, 48)
                for j in range(NT):
                    at = slice(j * P, (j + 1) * P)
                    if j >= 2:
                        e.wait_ge(done, j - 1)
                    for src, w, o in ((acc, Wn, 0), (g.HT, Ws, 2)):
                        for h in range(2):
                            m = e.matmul(g.ps[o + j % 2][:, 0:D], lhsT=src[:, h, at], rhs=w[:, h, :],
                                         start=h == 0, stop=h == 1)
                    m.then_inc(product, 1)

            @block.vector
            def _(e):
                link = Link(e, linked)
                link(e.tensor_single_scalar(rdeg[:, :], g.deg_d[:, :], 1.0, ALU.max))
                link(e.reciprocal(rdeg[:, :], rdeg[:, :]))
                e.wait_ge(loaded, 48)
                link(e.tensor_tensor(g.X[:, :, :], g.X[:, :, :], bc_mid(b[:, :], NT), ALU.add))
                for j in range(NT):
                    e.wait_ge(product, j + 1)
                    e.scalar_tensor_tensor(g.X[:, j, :], g.ps[j % 2][:, 0:D], rdeg[:, j:j + 1], g.X[:, j, :],
                                           ALU.mult, ALU.add).then_inc(added, 1)
                    e.wait_ge(added, j + 1)
                    e.tensor_tensor(g.X[:, j, :], g.X[:, j, :], g.ps[2 + j % 2][:, 0:D], ALU.add).then_inc(done, 1)



def stage_border(nc, env, T):
    g = env
    zeroed, stored = g.sem("b3_zeroed"), g.sem("b3_stored")
    with nc.Block() as block:
        @block.vector
        def _(e):
            e.memset(T[:, 0, :], 0.0).then_inc(zeroed, 1)

        @block.sync
        def _(e):
            e.wait_ge(zeroed, 1)
            e.dma_start(g.XRD[NP:NP + P, :], T[:, 0, :]).then_inc(stored, 16)
            e.wait_ge(stored, 16)


def stage_scores3(nc, env, A):
    g = env
    sem = g.sem
    landed, free, hot, row_in, win_in, sc_ready, sc_out = (
        [sem(f"s3_{x}{s}") for s in range(SETS)]
        for x in ("landed", "free", "hot", "row", "win", "sc_ready", "sc_out"))
    staged, seen, att_in = sem("s3_staged"), sem("s3_seen"), sem("s3_att")
    summed, drained, weighed = sem("s3_summed"), sem("s3_drained"), sem("s3_weighed")
    BANKS, PER = 8, SETS * U
    with ExitStack() as own:
        def sb(n, shape, dt=f32):
            return own.enter_context(nc.sbuf_tensor("s3_" + n, shape, dt))
        idx = sb("idx", [P, SETS, U], i32)
        G, XR = sb("G", [P, SETS, U, XLW]), sb("XR", [P, SETS, U, XLW])
        rowb, OT = sb("rowb", [P, SETS, U * P], i32), sb("OT", [P, SETS, U, P])
        R = sb("R", [P, 2, U, D])
        L = sb("L", [P, 2, U, 8])
        att = sb("att", [P, D])
        SC = sb("SC", [P, SETS, U, 8])
        with nc.Block() as block:
            @block.gpsimd
            def _(e):
                with e.Fori(0, WI) as k:
                    for s in range(SETS):
                        e.wait_ge(free[s], k + 1)
                        e.tensor_copy(idx[:, s, :], g.src_t[:, bass.ds(k * PER + s * U, U)])\
                            .then_inc(staged, 1)
                        e.wait_ge(staged, k * SETS + (s + 1))
                        e.sem_inc(seen, 1)
                        for i in range(U):
                            e.indirect_dma_start(out=G[:, s, i, :], out_offset=None, in_=g.XLD[:, :],
                                                 in_offset=IOA(ap=idx[:, s, i:i + 1], axis=0))\
                                .then_inc(landed[s], 16)

            @block.sync
            def _(e):
                e.dma_start(att[:, :], bc_row(A["L3_gnn_att"].rearrange("h c -> (h c)"))).then_inc(att_in, 16)
                with e.Fori(0, WI) as k:
                    for s in range(SETS):
                        e.wait_ge(free[s], k + 1)
                        e.dma_start(rowb[:, s, :], bc_row(A["dst_row"][bass.ds(k * (PER * P) + s * U * P, U * P)]))\
                            .then_inc(row_in[s], 16)
                        _, places = nc.values_load_multi_w_load_instructions(
                            g.base_d[0:1, bass.ds(k * PER + s * U, U)], engines=[mybir.EngineType.SP],
                            min_val=0, max_val=NP - 1)
                        for i in range(U):
                            e.dma_start(XR[:, s, i, :], g.XRD[bass.ds(places[i], P), :]).then_inc(win_in[s], 16)

            @block.scalar
            def _(e):
                sc_t = g.SCD.rearrange("(t p) w -> p t w", p=P)

                def store(k, s):
                    e.wait_ge(sc_ready[s], k * 3 + 3)
                    e.dma_start(sc_t[:, bass.ds(k * PER + s * U, U), :], SC[:, s, :, :]).then_inc(sc_out[s], 16)

                for n in range(BANKS):
                    e.sem_inc(drained, 1)
                with e.Fori(0, WI) as k:
                    for s in range(SETS):
                        e.wait_ge(weighed, k * SETS + (s + 1))
                        for i in range(U):
                            t = k * PER + (s * U + i)
                            bank = g.ps[(s * U + i) % BANKS]
                            e.wait_ge(summed, t + 1)
                            e.activation(L[:, s % 2, i, :], bank[:, D:XLW], ACT.Copy)
                            e.activation(R[:, s % 2, i, :], bank[:, 0:D], ACT.Relu, scale=0.8).then_inc(drained, 1)
                        if s >= 1:
                            store(k, s - 1)
                    store(k, SETS - 1)
                for s in range(SETS):
                    e.wait_ge(sc_out[s], 16 * WI)

            @block.vector
            def _(e):
                e.wait_ge(att_in, 16)

                def one_hot(k, s):
                    e.wait_ge(row_in[s], k * 16 + 16)
                    e.tensor_tensor(OT[:, s, :, :], rowb[:, s, :].rearrange("p (i f) -> p i f", f=P),
                                    bc_last(g.win_d[:, bass.ds(k * PER + s * U, U)], P), ALU.is_equal)\
                        .then_inc(hot[s], 1)

                def finish(k, s, first):
                    e.wait_ge(drained, k * PER + ((s + 1) * U + BANKS))
                    e.sem_inc(free[s], 1)
                    v = R[:, s % 2, :, :]
                    e.tensor_tensor(v, v, bc_mid(att[:, :], U), ALU.mult).then_inc(sc_ready[s], 1)
                    e.wait_ge(sc_ready[s], k * 3 + 1)
                    if not first:
                        e.wait_ge(sc_out[s], k * 16)
                    e.tensor_reduce(SC[:, s, :, :], v.rearrange("p i (h c) -> p i h c", h=8), AX.X, ALU.add)\
                        .then_inc(sc_ready[s], 1)
                    e.wait_ge(sc_ready[s], k * 3 + 2)
                    e.tensor_tensor(SC[:, s, :, :], SC[:, s, :, :], L[:, s % 2, :, :], ALU.add)\
                        .then_inc(sc_ready[s], 1)
                    e.wait_ge(sc_ready[s], k * 3 + 3)
                    e.sem_inc(weighed, 1)

                def turn(k, first=False, last=False):
                    for s in range(SETS):
                        if s < SETS - 1:
                            one_hot(k, s + 1)
                        elif not last:
                            one_hot(k + 1, 0)
                        finish(k, s, first)

                for s in range(SETS):
                    e.sem_inc(free[s], 1)
                for s in range(2):
                    e.sem_inc(weighed, 1)
                one_hot(0, 0)
                turn(0, first=True)
                with e.Fori(1, WI - 1) as k:
                    turn(k)
                turn(WI - 1, last=True)

            @block.tensor
            def _(e):
                with e.Fori(0, WI) as k:
                    for s in range(SETS):
                        e.wait_ge(hot[s], k + 1)
                        e.wait_ge(win_in[s], k * (16 * U) + 16 * U)
                        e.wait_ge(landed[s], k * (16 * U) + 16 * U)
                        for i in range(U):
                            bank = g.ps[(s * U + i) % BANKS]
                            e.wait_ge(drained, k * PER + (s * U + i + 1))
                            e.matmul(bank[:, 0:XLW], lhsT=OT[:, s, i, :], rhs=XR[:, s, i, :], start=True, stop=False)
                            e.matmul(bank[:, 0:XLW], lhsT=g.ident[:, :], rhs=G[:, s, i, :], start=False, stop=True)\
                                .then_inc(summed, 1)


def stage_softmax3(nc, env, A):
    g = env
    sem = g.sem
    loaded, linked, asked, answered, act_asked, act_done, soft, stored = (
        sem("x3_loaded"), sem("x3_linked"), sem("x3_ask"), sem("x3_answer"), sem("x3_act_ask"), sem("x3_act"),
        sem("x3_soft"), sem("x3_stored"))
    with ExitStack() as own:
        def sb(n, shape):
            return own.enter_context(nc.sbuf_tensor("x3_" + n, shape, f32))
        S, M, V = (sb(x, [P, ET, 8]) for x in ("S", "M", "V"))
        ew, lw, carry = sb("ew", [P, ET]), sb("lw", [P, ET]), sb("carry", [P, 8])
        with nc.Block() as block:
            @block.sync
            def _(e):
                e.dma_start(S[:, :, :], g.SCD.rearrange("(p j) w -> p j w", j=ET)).then_inc(loaded, 16)
                e.dma_start(ew[:, :], A["ew"][:, :]).then_inc(loaded, 16)
                e.wait_ge(soft, 1)
                e.dma_start(g.WD.rearrange("(p j) w -> p j w", j=ET), S[:, :, :]).then_inc(stored, 16)
                e.wait_ge(stored, 16)

            @block.scalar
            def _(e):
                e.wait_ge(act_asked, 1)
                e.activation(lw[:, :], lw[:, :], ACT.Ln).then_inc(act_done, 1)
                e.wait_ge(act_asked, 2)
                e.activation(S[:, :, :], S[:, :, :], ACT.Exp).then_inc(act_done, 1)

            @block.vector
            def _(e):
                link = Link(e, linked)
                flip, act = Asks(e, asked, answered), Asks(e, act_asked, act_done)
                e.wait_ge(loaded, 32)
                link(e.tensor_single_scalar(lw[:, :], ew[:, :], 2.0 ** -64, ALU.max))
                act()
                link(e.tensor_tensor(V[:, :, :], S[:, :, :], bc_last(lw[:, :], 8), ALU.add))
                seg_softmax(e, g, link, flip, act, 8, g.od, S, M, V, carry, weight=ew[:, :], eps=1e-16)
                e.sem_inc(soft, 1)

            @block.tensor
            def _(e):
                tensor_flips(e, g, asked, answered, scan_flips(8, 4))


def stage_output(nc, env, A, acc, out):
    g = env
    loaded, linked, turned, done, stored = (g.sem("o_loaded"), g.sem("o_linked"), g.sem("o_turned"),
                                            g.sem("o_done"), g.sem("o_stored"))
    with ExitStack() as own:
        b = own.enter_context(nc.sbuf_tensor("o_b", [P, D], f32))
        with nc.Block() as block:
            @block.sync
            def _(e):
                e.dma_start(b[:, :], bc_row(A["L3_gnn_bias"])).then_inc(loaded, 16)
                o = out.rearrange("(j p) d -> p j d", p=P)
                for n in range(5):
                    e.wait_ge(done, 5 * n + 5)
                    e.dma_start(o[:, 5 * n:5 * n + 5, :], g.X[:, 5 * n:5 * n + 5, :]).then_inc(stored, 16)
                e.wait_ge(stored, 80)

            @block.tensor
            def _(e):
                for j in range(NT):
                    if j >= 4:
                        e.wait_ge(done, j - 3)
                    for h in range(2):
                        m = e.transpose(g.ps[j % 4][:, h * P:(h + 1) * P], acc[:, h, j * P:(j + 1) * P],
                                        g.ident[:, :])
                    m.then_inc(turned, 1)

            @block.vector
            def _(e):
                link = Link(e, linked)
                e.wait_ge(loaded, 16)
                link(e.tensor_tensor(g.X[:, :, :], g.X[:, :, :], bc_mid(b[:, :], NT), ALU.add))
                for j in range(NT):
                    e.wait_ge(turned, j + 1)
                    e.tensor_tensor(g.X[:, j, :], g.X[:, j, :], g.ps[j % 4][:, 0:D], ALU.add).then_inc(done, 1)


def build(nc, A, out):
    with ExitStack() as stack:
        g = Env()

        def run(stage, *args):
            taken = []

            def sem(name):
                taken.append(nc.alloc_semaphore(name=name))
                return taken[-1]

            g.sem = sem
            stage(nc, g, *args)
            nc.all_engine_barrier()
            nc.clear_and_free_semaphores(taken)
            nc.all_engine_barrier()

        def sb(name, shape, dt=f32):
            return stack.enter_context(nc.sbuf_tensor(name, shape, dt))

        def dram(name, shape, dt=f32):
            return nc.dram_tensor(name, shape, dt, kind="Internal").ap()

        g.ps = [stack.enter_context(nc.psum_tensor(f"ps{i}", [P, 512], f32)) for i in range(8)]
        g.iota_row, g.iota_p, g.ones = sb("iota_row", [P, P]), sb("iota_p", [P, 1]), sb("ones", [P, P])
        g.ident, g.before, g.after = sb("ident", [P, P]), sb("before", [P, P]), sb("after", [P, P])
        g.X, g.HT = sb("X", [P, NT, D]), sb("HT", [P, 2, NP])
        g.src_t, g.dst_t, g.src_c = (sb(x, [P, ET], i32) for x in ("src_t_sb", "dst_t_sb", "src_c_sb"))
        g.deg_s, g.deg_d, g.start_s, g.start_d = (sb(x, [P, NT]) for x in ("deg_s", "deg_d", "start_s", "start_d"))
        g.T0, g.RKF = dram("T0", (NP, 16)), dram("RKF", (EP,), i32)
        g.rank_c, g.dsts_c, g.dsts_t = (sb(x, [P, ET], i32) for x in ("rank_c", "dsts_c", "dsts_t"))
        g.lrel_d, g.lrel_s, g.win_d = (sb(x, [P, ET]) for x in ("lrel_d", "lrel_s", "win_d"))
        g.base_d, g.base_s = sb("base_d", [1, ET], i32), sb("base_s", [1, ET], i32)
        g.put_d, g.put_s, g.end_d, g.end_s = (sb(x, [P, NT], i32) for x in ("put_d", "put_s", "end_d", "end_s"))
        g.flip_in, g.flip_ex = sb("flip_in", [P, 8]), sb("flip_ex", [8, P + 2])
        g.od, g.os = Order(sb, "od"), Order(sb, "os")
        g.MSG = sb("MSG", [P, NT, 8])
        g.Z8, g.RECD, g.KEYD = dram("Z8", (EP, 8)), dram("RECD", (EP + 2, NRW)), dram("KEYD", (2, EP))
        g.WHD, g.H2D, g.XLD, g.XRD = (dram("WHD", (NP, D)), dram("H2D", (NP, D)), dram("XLD", (NP, XLW)),
                                      dram("XRD", (NP + P, XLW)))
        g.TND, g.Z2, g.ALD = dram("TND", (NP, 2)), dram("Z2", (EP, 2)), dram("ALD", (EP, 2))
        g.SCD, g.WD = dram("SCD", (EP, 8)), dram("WD", (EP, 8))
        g.PSD, g.MSD = dram("PSD", (EP + 1, 8)), dram("MSD", (EP, 8))
        with ExitStack() as layer0:
            def layer0_sb(name, shape, dt=f32):
                return layer0.enter_context(nc.sbuf_tensor(name, shape, dt))

            g.AD = layer0.enter_context(nc.sbuf_tensor("AD", [P, NT, 8], f32))
            g.GAT = layer0.enter_context(nc.sbuf_tensor("GAT", [P, ET, 16], f32))
            run(stage_constants, A)
            run(stage_norm, "n0")
            run(stage_tables0, A)
            run(stage_rank, A)
            g.PD, g.T1, g.T2 = (layer0_sb(x, [P, ET, 8]) for x in ("PD", "T1", "T2"))
            with ExitStack() as own:
                REC = own.enter_context(nc.sbuf_tensor("REC", [P, ET, NRW], f32))
                run(stage_attr, A, REC)
                run(stage_edges0, A, REC)
            g.T3 = layer0_sb("T3", [P, ET, 8])
            run(stage_by_src)
            run(stage_messages0)
        run(stage_update0, A)
        run(stage_norm, "n1")
        SN, TN = sb("SN", [P, NT, 2]), sb("TN", [P, NT, 2])
        with ExitStack() as own:
            T = own.enter_context(nc.sbuf_tensor("T_wh", [P, NT, D], f32))
            a = A["L1_gnn_a"]
            run(stage_project, A, "p1", A["L1_gnn_W_w"], A["L1_gnn_W_b"],
                          [[(0, a[0:P]), (P, a[0:P])], [(0, a[P:D]), (P, a[P:D])]], 2, 1.0, T,
                          [SN[:, :, :], TN[:, :, :]], g.WHD[:, :], D)
        run(stage_edges1, SN, TN, g.ALD)
        with ExitStack() as own:
            acc = own.enter_context(nc.sbuf_tensor("acc12", [P, 2, ACCW], f32))
            run(stage_aggregate, "a1", g.WHD[:, :], D, g.dsts_t, g.lrel_s, g.base_s, acc, g.ALD, 2)
            run(stage_update1, acc)
            run(stage_norm, "n2", g.H2D)
            run(stage_aggregate, "a2", g.H2D[:, :], D, g.src_t, g.lrel_d, g.base_d, acc)
            run(stage_update2, A, acc)
        run(stage_norm, "n3")
        att = A["L3_gnn_att"].rearrange("h c -> (h c)")
        with ExitStack() as own:
            T = own.enter_context(nc.sbuf_tensor("T_xl", [P, NT, XLW], f32))
            run(stage_project, A, "p3l", A["L3_gnn_W_l"], A["L3_gnn_b_l"], [[(0, att)]], 8, 0.2, T,
                          [T[:, :, D:XLW]], g.XLD[:, :], XLW)
            run(stage_project, A, "p3r", A["L3_gnn_W_r"], A["L3_gnn_b_r"], [[(0, att)]], 8, 0.2, T,
                          [T[:, :, D:XLW]], g.XRD[0:NP, :], XLW)
            run(stage_border, T)
        run(stage_scores3, A)
        run(stage_softmax3, A)
        acc = sb("acc3", [P, 2, ACCW])
        run(stage_aggregate, "a3", g.XLD[:, :], XLW, g.src_t, g.lrel_d, g.base_d, acc, g.WD, 8)
        run(stage_output, A, acc, out)


def kernel(**inputs):
    import numpy as _np
    import concourse.bacc as _bacc
    from concourse import mybir as _mybir
    from concourse.bass_utils import run_bass_kernel_spmd as _run

    def edges(a, fill):
        padded = _np.full((EP,) + a.shape[1:], fill, a.dtype)
        padded[:NE] = a
        return padded

    src, dst = edges(_np.asarray(inputs["src"]), NP - 1), edges(_np.asarray(inputs["dst"]), NP - 1)
    bordered = _np.concatenate([_np.full(1, -1, dst.dtype), dst, _np.full(1, NP, dst.dtype)])
    x = _np.zeros((NP, D), _np.float32)
    x[:NN] = inputs["x"]
    laid = {
        "x": x,
        "src_t": src.reshape(ET, P).T, "dst_t": dst.reshape(ET, P).T,
        "src_c": src.reshape(P, ET), "dst_c": _np.stack([bordered[ET * p:ET * p + ET + 2] for p in range(P)]),
        "src_row": src, "dst_row": dst,
        "attr": edges(_np.asarray(inputs["edge_attr_16"]), 0).reshape(P, ET // 8, P).transpose(1, 2, 0),
        "ew": edges(_np.asarray(inputs["edge_weight"]), 1).reshape(P, ET),
    }
    for name, a in inputs.items():
        if name.startswith("L"):
            a = _np.asarray(a)
            laid[name] = a.T if name in ("L2_gnn_W_neigh", "L2_gnn_W_self") else a
    nc = _bacc.Bacc("TRN2", target_bir_lowering=False, num_devices=1)
    arrays, args = {}, {}
    for name, a in laid.items():
        a = _np.ascontiguousarray(a)
        arrays[f"in_{name}_dram"] = a
        args[name] = nc.dram_tensor(f"in_{name}_dram", a.shape, _mybir.dt.from_np(a.dtype),
                                    kind="ExternalInput").ap()
    out = nc.dram_tensor("out_0_dram", (NP, D), _mybir.dt.float32, kind="ExternalOutput").ap()
    build(nc, args, out)
    r = _run(nc, [arrays], core_ids=[0])
    return r.results[0]["out_0_dram"][:NN]
```

```python
import concourse.bass as bass
from concourse import mybir
from contextlib import ExitStack

P = 128
NN = 3125
NE = 53125
D = 256
NT = -(-NN // P)
NP = NT * P
ET = -(-NE // (32 * P)) * 32
EP = ET * P
CU = 16
CI = ET // (2 * CU)
U = 8
SETS = 4
WI = ET // (SETS * U)
RU = 8
RI = ET // (2 * RU)
LOOKED = 17 * 2 * RU
ACCW = NP + P
TQ = ET // 4
NRW = 10
BIG = 1.0e30
LN_EPS = 1e-5
XLW = D + 8

f32 = mybir.dt.float32
bf16 = mybir.dt.bfloat16
i32 = mybir.dt.int32
ALU = mybir.AluOpType
ACT = mybir.ActivationFunctionType
AX = mybir.AxisListType
IOA = bass.IndirectOffsetOnAxis


class Link:

    def __init__(self, eng, sem):
        self.eng, self.sem, self.n = eng, sem, 0

    def __call__(self, ins):
        ins.then_inc(self.sem, 1)
        self.n += 1
        self.eng.wait_ge(self.sem, self.n)


class Env:
    pass


def bc_mid(ap, n):
    return ap[:, None, :].to_broadcast([ap.shape[0], n, ap.shape[1]])


def bc_last(ap, n):
    return ap[:, :, None].to_broadcast([ap.shape[0], ap.shape[1], n])


def one_hot_view(g):
    return g.HT[:, :, :].rearrange("p h n -> p (h n)")[:, 0:SETS * U * P]\
        .rearrange("p (s i f) -> p s i f", s=SETS, f=P)


def bc_row(ap, n=P):
    return ap[None, :].to_broadcast([n, ap.shape[0]])



def stage_constants(nc, env, A):
    g = env
    ready = g.sem("const_ready")
    loaded = g.sem("index_loaded")
    with nc.Block() as block:
        @block.gpsimd
        def _(e):
            e.iota(g.iota_row[:, :], [[1, P]], base=0, channel_multiplier=0,
                   allow_small_or_imprecise_dtypes=True)
            e.iota(g.iota_p[:, :], [[0, 1]], base=0, channel_multiplier=1,
                   allow_small_or_imprecise_dtypes=True)
            e.memset(g.ones[:, :], 1.0)
            e.memset(g.ident[:, :], 0.0).then_inc(ready, 1)
            e.wait_ge(ready, 1)
            e.affine_select(out=g.ident[:, :], in_=g.ident[:, :], compare_op=ALU.not_equal, fill=1.0,
                            base=0, pattern=[[-1, P]], channel_multiplier=1)
            e.affine_select(out=g.before[:, :], in_=g.ones[:, :], compare_op=ALU.is_ge, fill=0.0,
                            base=-1, pattern=[[-1, P]], channel_multiplier=1)
            e.affine_select(out=g.after[:, :], in_=g.ones[:, :], compare_op=ALU.is_ge, fill=0.0,
                            base=-1, pattern=[[1, P]], channel_multiplier=-1).then_inc(ready, 1)

        @block.sync
        def _(e):
            e.dma_start(g.X[:, :, :], A["x"].rearrange("(j p) d -> p j d", p=P)).then_inc(loaded, 16)
            e.dma_start(g.src_t[:, :], A["src_t"][:, :]).then_inc(loaded, 16)
            e.dma_start(g.dst_t[:, :], A["dst_t"][:, :]).then_inc(loaded, 16)
            e.dma_start(g.src_c[:, :], A["src_c"][:, :]).then_inc(loaded, 16)
            e.wait_ge(loaded, 64)



def stage_norm(nc, env, name, rows=None):
    g = env
    moments, root, linked = g.sem(name + "_moments"), g.sem(name + "_root"), g.sem(name + "_linked")
    h_ready, flipped, kept = g.sem(name + "_h_ready"), g.sem(name + "_flipped"), g.sem(name + "_kept")
    stored = g.sem(name + "_stored")
    with ExitStack() as own:
        H = own.enter_context(nc.sbuf_tensor(name + "_H", [P, NT, D], f32))
        stats = own.enter_context(nc.sbuf_tensor(name + "_stats", [P, NT, 6], f32))
        mv = own.enter_context(nc.sbuf_tensor(name + "_mv", [P, NT, 2], f32))
        rstd = own.enter_context(nc.sbuf_tensor(name + "_rstd", [P, NT], f32))
        shift = own.enter_context(nc.sbuf_tensor(name + "_shift", [P, NT], f32))
        with nc.Block() as block:
            @block.vector
            def _(e):
                link = Link(e, linked)
                for j in range(NT - 1):
                    e.bn_stats(stats[:, j, :], g.X[:, j, :])
                link(e.bn_stats(stats[:, NT - 1, :], g.X[:, NT - 1, :]))
                for j in range(NT - 1):
                    e.bn_aggr(mv[:, j, :], stats[:, j, :])
                link(e.bn_aggr(mv[:, NT - 1, :], stats[:, NT - 1, :]))
                e.tensor_scalar(rstd[:, :], mv[:, :, 1], LN_EPS, None, ALU.add).then_inc(moments, 1)
                e.wait_ge(root, 1)
                link(e.reciprocal(rstd[:, :], rstd[:, :]))
                e.scalar_tensor_tensor(shift[:, :], mv[:, :, 0], -1.0, rstd[:, :], ALU.mult, ALU.mult)\
                    .then_inc(moments, 1)
                for j in range(NT):
                    e.wait_ge(flipped, j + 1)
                    e.tensor_copy(g.HT[:, :, j * P:(j + 1) * P],
                                  g.ps[j % 4][:, 0:D].rearrange("p (h n) -> p h n", h=2)).then_inc(kept, 1)

            @block.scalar
            def _(e):
                e.wait_ge(moments, 1)
                e.activation(rstd[:, :], rstd[:, :], ACT.Sqrt).then_inc(root, 1)
                e.wait_ge(moments, 2)
                for j in range(NT):
                    e.activation(H[:, j, :], g.X[:, j, :], ACT.Relu, bias=shift[:, j:j + 1],
                                 scale=rstd[:, j:j + 1]).then_inc(h_ready, 1)

            @block.tensor
            def _(e):
                for j in range(NT):
                    e.wait_ge(h_ready, j + 1)
                    if j >= 4:
                        e.wait_ge(kept, j - 3)
                    e.transpose(g.ps[j % 4][:, 0:P], H[:, j, 0:P], g.ident[:, :])
                    e.transpose(g.ps[j % 4][:, P:D], H[:, j, P:D], g.ident[:, :]).then_inc(flipped, 1)

            if rows is not None:
                @block.sync
                def _(e):
                    e.wait_ge(h_ready, NT)
                    e.dma_start(rows.rearrange("(j p) d -> p j d", p=P), H[:, :, :]).then_inc(stored, 16)
                    e.wait_ge(stored, 16)


def stage_tables0(nc, env, A):
    g = env
    loaded, product, kept, stored = (g.sem("t0_loaded"), g.sem("t0_product"), g.sem("t0_kept"),
                                     g.sem("t0_stored"))
    with ExitStack() as own:
        W = own.enter_context(nc.sbuf_tensor("t0_W", [P, 2, 24], f32))
        T = own.enter_context(nc.sbuf_tensor("t0_T", [P, NT, 16], f32))
        with nc.Block() as block:
            @block.sync
            def _(e):
                for n, name in enumerate(("L0_gnn_W_attn_src", "L0_gnn_W_prop_src", "L0_gnn_W_attn_dst")):
                    e.dma_start(W[:, :, 8 * n:8 * n + 8],
                                A[name].rearrange("(h p) m -> p h m", p=P)).then_inc(loaded, 16)
                e.wait_ge(kept, NT)
                e.dma_start(g.T0.rearrange("(j p) w -> p j w", p=P), T[:, :, :]).then_inc(stored, 16)
                e.wait_ge(stored, 16)

            @block.tensor
            def _(e):
                e.wait_ge(loaded, 48)
                for j in range(NT):
                    if j >= 4:
                        e.wait_ge(kept, j - 3)
                    for h in range(2):
                        m = e.matmul(g.ps[j % 4][:, 0:24], lhsT=g.HT[:, h, j * P:(j + 1) * P], rhs=W[:, h, :],
                                     start=h == 0, stop=h == 1)
                    m.then_inc(product, 1)

            @block.vector
            def _(e):
                for j in range(NT):
                    e.wait_ge(product, j + 1)
                    e.tensor_copy(T[:, j, :], g.ps[j % 4][:, 0:16])
                    e.tensor_copy(g.AD[:, j, :], g.ps[j % 4][:, 16:24]).then_inc(kept, 1)



class Narrow:

    def __init__(self, g, nc, own, name, w):
        self.idx = own.enter_context(nc.sbuf_tensor(name + "_idx", [P, 2, CU], i32))
        self.rows = own.enter_context(nc.sbuf_tensor(name + "_rows", [P, 2, CU, w], f32))
        self.landed = [g.sem(f"{name}_landed{s}") for s in range(2)]
        self.staged, self.seen = g.sem(name + "_staged"), g.sem(name + "_seen")
        self.collected = g.sem(name + "_collected")


def pool_gather(e, n, index, table, out):

    def issue(turn, s):
        at = turn * (2 * CU) + s * CU
        e.tensor_copy(n.idx[:, s, :], index[:, bass.ds(at, CU)]).then_inc(n.staged, 1)
        e.wait_ge(n.staged, turn * 2 + (s + 1))
        e.sem_inc(n.seen, 1)
        for c in range(CU):
            e.indirect_dma_start(out=n.rows[:, s, c, :], out_offset=None, in_=table,
                                 in_offset=IOA(ap=n.idx[:, s, c:c + 1], axis=0)).then_inc(n.landed[s], 16)

    def collect(turn, s):
        at = turn * (2 * CU) + s * CU
        e.wait_ge(n.landed[s], turn * (16 * CU) + 16 * CU)
        e.tensor_copy(out[:, bass.ds(at, CU), :], n.rows[:, s, :, :]).then_inc(n.collected, 1)
        e.wait_ge(n.collected, turn * 2 + (s + 1))
        e.sem_inc(n.seen, 1)

    issue(0, 0)
    with e.Fori(0, CI - 1) as k:
        issue(k, 1)
        collect(k, 0)
        issue(k + 1, 0)
        collect(k, 1)
    issue(CI - 1, 1)
    collect(CI - 1, 0)
    collect(CI - 1, 1)


def pool_scatter(e, n, index, rows, table):

    def issue(turn, s):
        at = turn * (2 * CU) + s * CU
        e.tensor_copy(n.idx[:, s, :], index[:, bass.ds(at, CU)])
        e.tensor_copy(n.rows[:, s, :, :], rows[:, bass.ds(at, CU), :]).then_inc(n.staged, 1)
        e.wait_ge(n.staged, turn * 2 + (s + 1))
        e.sem_inc(n.seen, 1)
        for c in range(CU):
            e.indirect_dma_start(out=table, out_offset=IOA(ap=n.idx[:, s, c:c + 1], axis=0),
                                 in_=n.rows[:, s, c, :], in_offset=None).then_inc(n.landed[s], 16)

    issue(0, 0)
    issue(0, 1)
    with e.Fori(0, CI - 1) as k:
        for s in range(2):
            e.wait_ge(n.landed[s], k * (16 * CU) + 16 * CU)
            issue(k + 1, s)
    for s in range(2):
        e.wait_ge(n.landed[s], 16 * CU * CI)



def stage_rank(nc, env, A):
    g = env
    sem = g.sem
    linked, digits = sem("rk_linked"), sem("rk_digits")
    hot = [sem(f"rk_hot{s}") for s in range(2)]
    counted, count_kept, zero_ready = sem("rk_counted"), sem("rk_count_kept"), sem("rk_zero")
    picked = sem("rk_picked")
    deg_ready, prefixed, starts = sem("rk_deg_ready"), sem("rk_prefixed"), sem("rk_starts")
    row_in = [sem(f"rk_row_in{s}") for s in range(2)]
    row_free = [sem(f"rk_row_free{s}") for s in range(2)]
    base_in = [sem(f"rk_base_in{s}") for s in range(2)]
    base_free = [sem(f"rk_base_free{s}") for s in range(2)]
    onehot_t, looked, looked_free = sem("rk_onehot_t"), sem("rk_looked"), sem("rk_looked_free")
    ranked, turned, out_ready, stored, back = (sem("rk_ranked"), sem("rk_turned"), sem("rk_out_ready"),
                                               sem("rk_stored"), sem("rk_back"))
    with ExitStack() as own:
        def sb(n, shape, dt=f32):
            return own.enter_context(nc.sbuf_tensor("rk_" + n, shape, dt))
        n = Narrow(g, nc, own, "g0", 16)
        di = g.dsts_c
        slo, shi, dlo, dhi = g.od.fm, g.od.fneg, g.od.last, g.od.gm
        junk = sb("junk", [P, RU * P], bf16)
        onehots = sb("onehots", [P, 4 * RU * P], bf16)
        hot4 = onehots[:, :].rearrange("p (o s i f) -> p o s i f", o=2, s=2, f=P)
        hlo, glo = hot4[:, 0], hot4[:, 1]
        hhi = sb("hhi", [P, 2, RU, NT], bf16)
        ghi = sb("ghi", [P, 2, RU, NT], bf16)
        cnt = sb("cnt", [P, NT, ET], bf16)
        upto = sb("upto", [P, NT, ET])
        unit = g.os.fm
        tot = sb("tot", [P, 2, NT])
        run = sb("run", [P, 2, NT])
        row = sb("row", [P, 2, RU * P], i32)
        rlo = sb("rlo", [P, RU * P], i32)
        base = g.win_d[:, 0:2 * RU * NT].rearrange("p (s i c) -> p s i c", s=2, c=NT)
        srcf = g.lrel_s
        match = junk[:, :].rearrange("p (i f) -> p i f", f=P)
        look = g.shi_c[:, 0:RU * NT].rearrange("p (i c) -> p i c", c=NT)
        r2 = sb("r2", [P, 2, RU])
        zero = g.dhi_s[:, 0:P // 2].bitcast(bf16)
        r1 = sb("r1", [P, RU])
        rank = g.os.fneg
        oht = onehots[:, :].bitcast(f32).rearrange("p (s i f) -> p s i f", s=2, f=P)
        out = rlo[0:TQ, 0:4 * P].rearrange("q (i f) -> q i f", f=P)
        with nc.Block() as block:
            @block.gpsimd
            def _(e):
                pool_gather(e, n, g.src_c, g.T0[:, :], g.GAT)

            @block.sync
            def _(e):
                for s in range(2):
                    e.dma_start(row[:, s, :], bc_row(A["src_row"][s * RU * P:(s + 1) * RU * P]))\
                        .then_inc(row_in[s], 16)
                with e.Fori(0, RI - 1) as k:
                    for s in range(2):
                        e.wait_ge(row_free[s], k + 1)
                        e.dma_start(row[:, s, :],
                                    bc_row(A["src_row"][bass.ds(k * (2 * RU * P) + (2 + s) * RU * P, RU * P)]))\
                            .then_inc(row_in[s], 16)
                e.wait_ge(out_ready, 4)
                e.dma_start(g.RKF.rearrange("(i q p) -> q i p", i=4, p=P), out[:, :, :]).then_inc(stored, 16)
                e.wait_ge(stored, 16)
                e.dma_start(g.rank_c[:, :], g.RKF.rearrange("(p j) -> p j", j=ET)).then_inc(back, 16)
                e.wait_ge(back, 16)

            @block.scalar
            def _(e):
                with e.Fori(0, RI) as k:
                    for s in range(2):
                        e.wait_ge(counted, k * 2 + (s + 1))
                        e.activation(cnt[:, :, bass.ds(k * (2 * RU) + s * RU, RU)],
                                     g.ps[s][:, 0:RU * NT].rearrange("p (i c) -> p c i", c=NT), ACT.Copy)\
                            .then_inc(count_kept, 1)
                e.wait_ge(starts, 1)
                with e.Fori(0, RI) as k:
                    for s in range(2):
                        e.wait_ge(base_free[s], k + 1)
                        e.activation(base[:, s, :, :],
                                     upto[:, :, bass.ds(k * (2 * RU) + s * RU, RU)].rearrange("p c i -> p i c"),
                                     ACT.Copy).then_inc(base_in[s], 1)

            @block.vector
            def _(e):
                link = Link(e, linked)
                for src, lo, hi in ((g.src_t, slo, shi), (g.dst_t, dlo, dhi)):
                    link(e.tensor_single_scalar(di[:, :], src[:, :], P - 1, ALU.bitwise_and))
                    link(e.tensor_copy(lo[:, :], di[:, :]))
                    link(e.tensor_single_scalar(di[:, :], src[:, :], 7, ALU.arith_shift_right))
                    link(e.tensor_copy(hi[:, :], di[:, :]))
                e.memset(unit[:, :], 1.0)
                e.memset(zero[:, :], 0.0)
                link(e.tensor_copy(srcf[:, :], g.src_t[:, :]))
                e.sem_inc(zero_ready, 1)
                with e.Fori(0, RI) as k:
                    for s in range(2):
                        at = bass.ds(k * (2 * RU) + s * RU, RU)
                        e.wait_ge(digits, k * 2 + (s + 1))
                        e.tensor_tensor(hlo[:, s, :, :], bc_mid(g.iota_row[:, :], RU), bc_last(slo[:, at], P),
                                        ALU.is_equal)
                        e.tensor_tensor(hhi[:, s, :, :], bc_mid(g.iota_row[:, 0:NT], RU),
                                        bc_last(shi[:, at], NT), ALU.is_equal)
                        e.tensor_tensor(glo[:, s, :, :], bc_mid(g.iota_row[:, :], RU), bc_last(dlo[:, at], P),
                                        ALU.is_equal)
                        e.tensor_tensor(ghi[:, s, :, :], bc_mid(g.iota_row[:, 0:NT], RU),
                                        bc_last(dhi[:, at], NT), ALU.is_equal).then_inc(hot[s], 1)
                e.wait_ge(count_kept, 2 * RI + 2)
                e.wait_ge(counted, 2 * RI + 1)
                link(e.tensor_copy(g.deg_d[:, :], g.ps[4][:, 0:NT]))
                for c in range(NT - 1):
                    e.tensor_tensor_scan(upto[:, c, :], unit[:, :], cnt[:, c, :], 0.0, ALU.mult, ALU.add)
                link(e.tensor_tensor_scan(upto[:, NT - 1, :], unit[:, :], cnt[:, NT - 1, :], 0.0,
                                          ALU.mult, ALU.add))
                link(e.tensor_copy(g.deg_s[:, :], upto[:, :, ET - 1]))
                link(e.tensor_tensor(upto[:, :, :], upto[:, :, :], cnt[:, :, :], ALU.subtract))
                e.sem_inc(deg_ready, 1)
                e.wait_ge(prefixed, 1)
                for o, start in ((0, g.start_s), (1, g.start_d)):
                    link(e.tensor_copy(tot[:, o, :], g.ps[5][:, (2 * o + 1) * NT:(2 * o + 2) * NT]))
                    link(e.tensor_tensor_scan(run[:, o, :], unit[:, 0:NT], tot[:, o, :], 0.0, ALU.mult, ALU.add))
                    link(e.tensor_tensor(run[:, o, :], run[:, o, :], tot[:, o, :], ALU.subtract))
                    link(e.tensor_tensor(start[:, :], run[:, o, :], g.ps[5][:, 2 * o * NT:(2 * o + 1) * NT],
                                         ALU.add))
                link(e.tensor_tensor(upto[:, :, :], upto[:, :, :], bc_last(g.start_s[:, :], ET), ALU.add))
                e.sem_inc(starts, 1)
                for s in range(2):
                    e.sem_inc(base_free[s], 1)

                def prepare(k, s):
                    at = bass.ds(k * (2 * RU) + s * RU, RU)
                    e.wait_ge(row_in[s], k * 16 + 16)
                    e.tensor_single_scalar(rlo[:, :], row[:, s, :], P - 1, ALU.bitwise_and).then_inc(ranked, 1)
                    for i in range(RU):
                        ins = e.scalar_tensor_tensor(match[:, i, :], row[:, s, i * P:(i + 1) * P],
                                                     srcf[:, bass.ds(k * (2 * RU) + (s * RU + i), 1)],
                                                     g.before[:, :], ALU.is_equal, ALU.mult,
                                                     accum_out=r2[:, s, i:i + 1])
                    ins.then_inc(ranked, 1)
                    e.tensor_tensor(hhi[:, s, :, :], bc_mid(g.iota_row[:, 0:NT], RU), bc_last(shi[:, at], NT),
                                    ALU.is_equal)
                    e.wait_ge(ranked, k * 4 + (2 * s + 2))
                    e.tensor_scalar(oht[:, s, :, :].rearrange("p i f -> p (i f)"), rlo[:, :], g.iota_p[:, 0:1],
                                    None, ALU.is_equal).then_inc(onehot_t, 1)
                    e.wait_ge(onehot_t, k * 2 + (s + 1))
                    e.sem_inc(row_free[s], 1)

                def finish(k, s):
                    at = bass.ds(k * (2 * RU) + s * RU, RU)
                    e.wait_ge(looked, k * 2 + (s + 1))
                    e.tensor_tensor(look[:, :, :], g.ps[s][:, 0:RU * NT].rearrange("p (i c) -> p i c", c=NT),
                                    hhi[:, s, :, :], ALU.mult).then_inc(picked, 1)
                    e.wait_ge(picked, k * 4 + (2 * s + 1))
                    e.sem_inc(base_free[s], 1)
                    e.tensor_reduce(r1[:, :], look[:, :, :], AX.X, ALU.add).then_inc(picked, 1)
                    e.wait_ge(picked, k * 4 + (2 * s + 2))
                    e.scalar_tensor_tensor(rank[:, at], r1[:, :], 1.0, r2[:, s, :], ALU.add, ALU.add)\
                        .then_inc(looked_free, 1)
                    e.wait_ge(looked_free, k * 2 + (s + 1))

                prepare(0, 0)
                prepare(0, 1)
                with e.Fori(0, RI - 1) as k:
                    for s in range(2):
                        finish(k, s)
                        prepare(k + 1, s)
                finish(RI - 1, 0)
                finish(RI - 1, 1)
                e.wait_ge(looked_free, 2 * RI)
                for i in range(4):
                    e.wait_ge(turned, i + 1)
                    e.tensor_copy(out[:, i, :], g.ps[i][0:TQ, 0:P]).then_inc(out_ready, 1)
                e.wait_ge(out_ready, 4)

            @block.tensor
            def _(e):
                for s in range(2):
                    e.sem_inc(digits, 1)
                for s in range(2):
                    e.sem_inc(count_kept, 1)
                e.wait_ge(zero_ready, 1)
                e.matmul(g.ps[4][:, 0:NT], lhsT=zero[:, :], rhs=zero[:, 0:NT], start=True, stop=False)
                with e.Fori(0, RI) as k:
                    for s in range(2):
                        e.wait_ge(hot[s], k + 1)
                        e.wait_ge(count_kept, k * 2 + (s + 1))
                        for i in range(RU):
                            e.matmul(g.ps[s][:, i * NT:(i + 1) * NT], lhsT=hlo[:, s, i, :], rhs=hhi[:, s, i, :],
                                     start=True, stop=True)
                        for i in range(RU):
                            m = e.matmul(g.ps[4][:, 0:NT], lhsT=glo[:, s, i, :], rhs=ghi[:, s, i, :],
                                         start=False, stop=False)
                        m.then_inc(counted, 1)
                        e.wait_ge(counted, k * 2 + (s + 1))
                        e.sem_inc(digits, 1)
                e.matmul(g.ps[4][:, 0:NT], lhsT=zero[:, :], rhs=zero[:, 0:NT], start=False, stop=True)\
                    .then_inc(counted, 1)
                e.wait_ge(deg_ready, 1)
                for o, deg in ((0, g.deg_s), (1, g.deg_d)):
                    e.matmul(g.ps[5][:, 2 * o * NT:(2 * o + 1) * NT], lhsT=g.after[:, :], rhs=deg[:, :],
                             start=True, stop=True)
                    m = e.matmul(g.ps[5][:, (2 * o + 1) * NT:(2 * o + 2) * NT], lhsT=g.ones[:, :], rhs=deg[:, :],
                                 start=True, stop=True)
                m.then_inc(prefixed, 1)
                with e.Fori(0, RI) as k:
                    for s in range(2):
                        e.wait_ge(onehot_t, k * 2 + (s + 1))
                        e.wait_ge(base_in[s], k + 1)
                        for i in range(RU):
                            m = e.matmul(g.ps[s][:, i * NT:(i + 1) * NT], lhsT=oht[:, s, i, :],
                                         rhs=base[:, s, i, :], start=True, stop=True)
                        m.then_inc(looked, 1)
                e.wait_ge(looked_free, 2 * RI)
                for i in range(4):
                    e.transpose(g.ps[i][0:TQ, 0:P], rank[:, i * TQ:(i + 1) * TQ], g.ident[:, :])\
                        .then_inc(turned, 1)



class Order:

    def __init__(self, sb, name):
        self.fm, self.fneg, self.last, self.gm = (sb(f"{name}_{x}", [P, ET]) for x in ("fm", "fneg", "last", "gm"))
        self.fmT, self.fnegT, self.gmT = (sb(f"{name}_{x}", [8, P]) for x in ("fmT", "fnegT", "gmT"))


class Asks:

    def __init__(self, e, asked, answered):
        self.e, self.asked, self.answered, self.n = e, asked, answered, 0

    def __call__(self):
        self.e.sem_inc(self.asked, 1)
        self.n += 1
        self.e.wait_ge(self.answered, self.n)


def tensor_flips(e, g, asked, answered, kinds):
    for n, (kind, w) in enumerate(kinds):
        e.wait_ge(asked, n + 1)
        if kind == "in":
            e.transpose(g.ps[6][0:w, 0:P], g.flip_in[:, 0:w], g.ident[:, :]).then_inc(answered, 1)
        else:
            e.transpose(g.ps[7][:, 0:w], g.flip_ex[0:w, 1:P + 1], g.ident[0:w, 0:w]).then_inc(answered, 1)


ORDER_FLIPS = [("in", 8)] * 3


def scan_flips(w, scans):
    return [("in", w), ("ex", w)] * scans


def order_masks(e, g, link, flip, o, key, any_):
    link(e.tensor_tensor(o.last[:, :], key[:, 1:ET + 1], key[:, 2:ET + 2], ALU.not_equal))
    link(e.tensor_tensor(o.fneg[:, :], key[:, 1:ET + 1], key[:, 0:ET], ALU.not_equal))
    link(e.tensor_scalar(o.fm[:, :], o.fneg[:, :], -1.0, 1.0, ALU.mult, ALU.add))
    link(e.tensor_scalar(o.gm[:, :], o.last[:, :], -1.0, 1.0, ALU.mult, ALU.add))
    link(e.tensor_single_scalar(o.fneg[:, :], o.fneg[:, :], -BIG, ALU.mult))
    for mask, row in ((o.fm, o.fmT), (o.fneg, o.fnegT), (o.gm, o.gmT)):
        link(e.tensor_reduce(any_[:, :], mask[:, :], AX.X, ALU.min))
        link(e.tensor_copy(g.flip_in[:, 0:8], any_[:, 0:1].to_broadcast([P, 8])))
        flip()
        link(e.tensor_copy(row[:, :], g.ps[6][0:8, 0:P]))


def seg_scan(e, g, link, flip, w, backward, op0, op1, mask, mask_row, neutral, data, out, carry):

    def rows(first):
        for h in range(w):
            step = slice(None, None, -1) if backward else slice(None)
            ins = e.tensor_tensor_scan(out[:, step, h], mask[:, step], data[:, step, h],
                                       neutral if first else carry[:, h:h + 1], op0, op1)
            if h == w - 1:
                link(ins)

    rows(True)
    link(e.tensor_copy(g.flip_in[:, 0:w], out[:, 0 if backward else ET - 1, 0:w]))
    flip()
    if backward:
        e.memset(g.flip_ex[0:w, P:P + 1], neutral)
        link(e.tensor_tensor_scan(g.flip_ex[0:w, 0:P][:, ::-1], mask_row[0:w, ::-1],
                                  g.ps[6][0:w, 0:P][:, ::-1], neutral, op0, op1))
    else:
        link(e.tensor_tensor_scan(g.flip_ex[0:w, 2:P + 2], mask_row[0:w, :], g.ps[6][0:w, 0:P], neutral,
                                  op0, op1))
        link(e.memset(g.flip_ex[0:w, 1:2], neutral))
    flip()
    link(e.tensor_copy(carry[:, 0:w], g.ps[7][:, 0:w]))
    rows(False)


def seg_softmax(e, g, link, flip, exp, w, o, S, M, V, carry, weight=None, eps=None):
    seg_scan(e, g, link, flip, w, False, ALU.add, ALU.max, o.fneg, o.fnegT, -BIG, S if weight is None else V,
             M, carry)
    link(e.tensor_tensor(V[:, :, :], M[:, :, :], bc_last(o.last[:, :], w), ALU.mult))
    seg_scan(e, g, link, flip, w, True, ALU.mult, ALU.add, o.gm, o.gmT, 0.0, V, M, carry)
    link(e.tensor_tensor(S[:, :, :], S[:, :, :], M[:, :, :], ALU.subtract))
    exp()
    if weight is not None:
        link(e.tensor_tensor(S[:, :, :], S[:, :, :], bc_last(weight, w), ALU.mult))
    seg_scan(e, g, link, flip, w, False, ALU.mult, ALU.add, o.fm, o.fmT, 0.0, S, M, carry)
    link(e.tensor_tensor(V[:, :, :], M[:, :, :], bc_last(o.last[:, :], w), ALU.mult))
    seg_scan(e, g, link, flip, w, True, ALU.mult, ALU.add, o.gm, o.gmT, 0.0, V, M, carry)
    if eps is not None:
        link(e.tensor_single_scalar(M[:, :, :], M[:, :, :], eps, ALU.add))
    link(e.reciprocal(M[:, :, :], M[:, :, :]))
    link(e.tensor_tensor(S[:, :, :], S[:, :, :], M[:, :, :], ALU.mult))



class Ahead:

    def __init__(self, nc, g, own, name, columns):
        self.columns = columns
        self.staged, self.seen, self.landed = (g.sem(name + x) for x in ("_pre_staged", "_pre_seen", "_pre_landed"))
        self.idx = own.enter_context(nc.sbuf_tensor(name + "_pre_idx", [P, columns], i32))

    def gather(self, e, index, table, rows):
        e.tensor_copy(self.idx[:, :], index).then_inc(self.staged, 1)
        e.wait_ge(self.staged, 1)
        e.sem_inc(self.seen, 1)
        for c in range(self.columns):
            e.indirect_dma_start(out=rows[:, c, :], out_offset=None, in_=table,
                                 in_offset=IOA(ap=self.idx[:, c:c + 1], axis=0)).then_inc(self.landed, 16)
        e.wait_ge(self.landed, 16 * self.columns)


class Lookup:

    def __init__(self, g, sb, name, w, turns=RI):
        self.turns = turns
        self.w, self.per = w, 8 if w <= 2 else 2
        self.banks = RU // self.per
        self.parts = sb(name + "_parts", [P, 3, w, NT], bf16)
        self.rest = sb(name + "_rest", [P, w, NT])
        self.row = sb(name + "_row", [P, 2, RU * P], bf16)
        self.hot = sb(name + "_hot", [P, 2, RU * P], bf16)
        self.high = sb(name + "_high", [P, 2, RU, NT])
        self.picked = sb(name + "_picked", [P, RU, w, NT])
        self.split = g.sem(name + "_split")
        self.row_in, self.hot_ready, self.looked, self.masked = ([g.sem(f"{name}_{x}{s}") for s in range(2)]
                                                                for x in ("row_in", "hot", "looked", "masked"))

    def load_rows(self, e, digits):
        for s in range(2):
            e.dma_start(self.row[:, s, :], bc_row(digits[s * RU * P:(s + 1) * RU * P])).then_inc(self.row_in[s], 16)
        with e.Fori(0, self.turns - 1) as k:
            for s in range(2):
                e.wait_ge(self.hot_ready[s], k + 1)
                e.dma_start(self.row[:, s, :],
                            bc_row(digits[bass.ds(k * (2 * RU * P) + (2 + s) * RU * P, RU * P)]))\
                    .then_inc(self.row_in[s], 16)

    def split_table(self, e, link, table):
        t = table.rearrange("p c w -> p w c")
        link(e.tensor_copy(self.parts[:, 0], t))
        link(e.tensor_tensor(self.rest[:, :, :], t, self.parts[:, 0], ALU.subtract))
        link(e.tensor_copy(self.parts[:, 1], self.rest[:, :, :]))
        link(e.tensor_tensor(self.rest[:, :, :], self.rest[:, :, :], self.parts[:, 1], ALU.subtract))
        link(e.tensor_copy(self.parts[:, 2], self.rest[:, :, :]))
        e.sem_inc(self.split, 1)

    def vector(self, e, g, high, out):

        def prepare(k, s):
            at = bass.ds(k * (2 * RU) + s * RU, RU)
            e.wait_ge(self.row_in[s], k * 16 + 16)
            e.wait_ge(self.looked[s], k + 1)
            e.tensor_tensor(self.high[:, s, :, :], bc_mid(g.iota_row[:, 0:NT], RU), bc_last(high[:, at], NT),
                            ALU.is_equal)
            e.tensor_scalar(self.hot[:, s, :], self.row[:, s, :], g.iota_p[:, 0:1], None, ALU.is_equal)\
                .then_inc(self.hot_ready[s], 1)

        def finish(k, s):
            e.wait_ge(self.looked[s], k + 2)
            e.wait_ge(self.hot_ready[s], k + 1)
            e.wait_ge(self.masked[1 - s], k * 2 + (1 + s))
            for b in range(self.banks):
                t = slice(b * self.per, (b + 1) * self.per)
                ps = g.ps[s * 4 + b][:, 0:self.per * self.w * NT].rearrange("p (i w c) -> p i w c", w=self.w, c=NT)
                h = self.high[:, s, t, :][:, :, None, :].to_broadcast([P, self.per, self.w, NT])
                ins = e.tensor_tensor(self.picked[:, t, :, :], ps, h, ALU.mult)
            ins.then_inc(self.masked[s], 1)
            e.wait_ge(self.masked[s], k * 2 + (2 if s else 1))
            e.tensor_reduce(out[:, bass.ds(k * (2 * RU) + s * RU, RU), :], self.picked[:, :, :, :], AX.X, ALU.add)\
                .then_inc(self.masked[s], 1)

        e.sem_inc(self.masked[1], 1)
        for s in range(2):
            e.sem_inc(self.looked[s], 1)
        prepare(0, 0)
        prepare(0, 1)
        with e.Fori(0, self.turns - 1) as k:
            for s in range(2):
                finish(k, s)
                prepare(k + 1, s)
        finish(self.turns - 1, 0)
        finish(self.turns - 1, 1)

    def tensor(self, e, g):
        e.wait_ge(self.split, 1)
        with e.Fori(0, self.turns) as k:
            for s in range(2):
                e.wait_ge(self.hot_ready[s], k + 1)
                for i in range(RU):
                    n = self.w * NT
                    o = g.ps[s * 4 + i // self.per][:, (i % self.per) * n:(i % self.per + 1) * n]
                    for part in range(3):
                        m = e.matmul(o, lhsT=self.hot[:, s, i * P:(i + 1) * P],
                                     rhs=self.parts[:, part].rearrange("p w c -> p (w c)"),
                                     start=part == 0, stop=part == 2)
                m.then_inc(self.looked[s], 1)



def stage_edges0(nc, env, A, REC):
    g = env
    sem = g.sem
    loaded, linked, idx_ready, zero_ready = sem("e0_loaded"), sem("e0_linked"), sem("e0_idx"), sem("e0_zero")
    zeroed, filled, expanded = sem("e0_zeroed"), sem("e0_filled"), sem("e0_expanded")
    w_zeroed, attr_in, product, kept = sem("e0_w_zeroed"), sem("e0_attr_in"), sem("e0_product"), sem("e0_kept")
    BANKS = 5
    asked, answered, exp_asked, exp_done = sem("e0_ask"), sem("e0_answer"), sem("e0_exp_ask"), sem("e0_exp")
    rec_ready, based, border = sem("e0_rec"), sem("e0_based"), sem("e0_border")
    with ExitStack() as own:
        n = Narrow(g, nc, own, "s0", NRW)
        key = own.enter_context(nc.sbuf_tensor("e0_key", [P, ET + 2], i32))
        any_ = own.enter_context(nc.sbuf_tensor("e0_any", [P, 1], f32))
        carry = own.enter_context(nc.sbuf_tensor("e0_carry", [P, 8], f32))
        fsum = own.enter_context(nc.sbuf_tensor("e0_fsum", [P, NT], f32))
        keyf = own.enter_context(nc.sbuf_tensor("e0_keyf", [P, ET], f32))
        mark = own.enter_context(nc.sbuf_tensor("e0_mark", [2, 2], f32))
        half = ET // 16
        attr = [g.PD[:, :, :].rearrange("p j h -> p (j h)").rearrange("p (g q) -> p g q", q=P),
                own.enter_context(nc.sbuf_tensor("e0_attr", [P, half, P], f32))]
        W = own.enter_context(nc.sbuf_tensor("e0_W", [P, 64], f32))
        with nc.Block() as block:
            @block.sync
            def _(e):
                e.dma_start(key[:, :], A["dst_c"][:, :]).then_inc(loaded, 16)
                e.wait_ge(w_zeroed, 1)
                for n in range(8):
                    e.dma_start(W[16 * n:16 * n + 16, 8 * n:8 * n + 8], A["L0_gnn_W_attn_edge"][:, :])\
                        .then_inc(attr_in, 16)
                for i in range(2):
                    e.dma_start(attr[i][:, :, :], A["attr"][i * half:(i + 1) * half].rearrange("g r p -> r g p"))\
                        .then_inc(attr_in, 16)
                e.wait_ge(zero_ready, 1)
                for z in (g.Z8,):
                    e.dma_start(z.rearrange("(p j) w -> p j w", j=ET), g.T1[:, :, :]).then_inc(zeroed, 16)
                e.dma_start(g.RECD[0:1, 0:2], mark[0:1, :]).then_inc(border, 16)
                e.dma_start(g.RECD[EP + 1:EP + 2, 0:2], mark[1:2, :]).then_inc(border, 16)
                e.wait_ge(filled, 16 * NT)
                e.dma_start(g.T2[:, :, :], g.Z8.rearrange("(p j) w -> p j w", j=ET)).then_inc(expanded, 16)
                e.wait_ge(expanded, 16)
                e.wait_ge(border, 32)

            @block.gpsimd
            def _(e):
                e.wait_ge(idx_ready, 1)
                e.wait_ge(zeroed, 16)
                for j in range(NT):
                    e.indirect_dma_start(out=g.Z8[:, :], out_offset=IOA(ap=g.put_d[:, j:j + 1], axis=0),
                                         in_=g.AD[:, j, :], in_offset=None, bounds_check=EP - 1,
                                         oob_is_err=False).then_inc(filled, 16)
                e.wait_ge(rec_ready, 1)
                pool_scatter(e, n, g.rank_c, REC, g.RECD[:, :])

            @block.scalar
            def _(e):
                e.wait_ge(exp_asked, 1)
                e.activation(g.PD[:, :, :], g.PD[:, :, :], ACT.Exp).then_inc(exp_done, 1)

            @block.vector
            def _(e):
                link = Link(e, linked)
                flip, exp = Asks(e, asked, answered), Asks(e, exp_asked, exp_done)
                e.memset(W[:, :], 0.0).then_inc(w_zeroed, 1)
                e.memset(mark[:, :], -1.0)
                link(e.memset(g.T1[:, :, :], 0.0))
                e.sem_inc(zero_ready, 1)
                for deg, start, put, end in ((g.deg_d, g.start_d, g.put_d, g.end_d),
                                             (g.deg_s, g.start_s, g.put_s, g.end_s)):
                    link(e.tensor_single_scalar(fsum[:, :], deg[:, :], 0.0, ALU.is_equal))
                    link(e.scalar_tensor_tensor(fsum[:, :], fsum[:, :], float(EP), start[:, :], ALU.mult, ALU.add))
                    link(e.tensor_copy(put[:, :], fsum[:, :]))
                    link(e.scalar_tensor_tensor(fsum[:, :], start[:, :], -1.0, deg[:, :], ALU.add, ALU.add))
                    link(e.tensor_single_scalar(fsum[:, :], fsum[:, :], 0.0, ALU.max))
                    link(e.tensor_copy(end[:, :], fsum[:, :]))
                e.sem_inc(idx_ready, 1)
                e.wait_ge(loaded, 16)
                order_masks(e, g, link, flip, g.od, key, any_)
                link(e.tensor_copy(keyf[:, :], g.dst_t[:, :]))
                link(e.tensor_copy(g.base_d[0:1, :], g.dst_t[0:1, :]))
                flip()
                link(e.tensor_tensor(g.lrel_d[:, :], keyf[:, :], g.ps[5][:, 0:ET], ALU.subtract))
                link(e.tensor_scalar(g.win_d[:, :], g.ps[5][:, 0:ET], g.iota_p[:, 0:1], None, ALU.add))
                for n in range(-(-ET // 64)):
                    m = min(64, ET - 64 * n)
                    e.wait_ge(product, n + 1)
                    e.tensor_copy(REC[:, 64 * n:64 * n + m, 2:10],
                                  g.ps[n % BANKS][:, 0:8 * m].rearrange("p (j h) -> p j h", h=8)).then_inc(kept, 1)
                e.wait_ge(kept, -(-ET // 64))
                link(e.tensor_copy(REC[:, :, 0], g.src_c[:, :]))
                link(e.tensor_copy(REC[:, :, 1], key[:, 1:ET + 1]))
                e.wait_ge(expanded, 16)
                seg_scan(e, g, link, flip, 8, False, ALU.mult, ALU.add, g.od.fm, g.od.fmT, 0.0, g.T2, g.T1, carry)
                E = REC[:, :, 2:10]
                link(e.tensor_tensor(E, E, g.GAT[:, :, 0:8], ALU.add))
                link(e.tensor_tensor(E, E, g.T1[:, :, :], ALU.add))
                link(e.scalar_tensor_tensor(E, E, 0.2, E, ALU.mult, ALU.max))
                e.sem_inc(rec_ready, 1)
                link(e.tensor_copy(g.PD[:, :, :], E))
                link(e.tensor_copy(g.GAT[:, :, 0:8], E))
                seg_softmax(e, g, link, flip, exp, 8, g.od, g.PD, g.T1, g.T2, carry)

            @block.tensor
            def _(e):
                kinds = ORDER_FLIPS + [("base", 0)] + scan_flips(8, 5)
                for k, (kind, w) in enumerate(kinds):
                    if k == len(ORDER_FLIPS) + 1:
                        e.wait_ge(attr_in, 16 * 10)
                        for n in range(-(-ET // 64)):
                            if n >= BANKS:
                                e.wait_ge(kept, n - BANKS + 1)
                            for q in range(8 * n, min(8 * n + 8, ET // 8)):
                                last = e.matmul(g.ps[n % BANKS][:, 64 * (q % 8):64 * (q % 8) + 64],
                                                lhsT=attr[q // half][:, q % half, :], rhs=W[:, :],
                                                start=True, stop=True)
                            last.then_inc(product, 1)
                    e.wait_ge(asked, k + 1)
                    if kind == "base":
                        e.matmul(g.ps[5][:, 0:ET], lhsT=g.ones[0:1, :], rhs=keyf[0:1, :], start=True, stop=True)\
                            .then_inc(answered, 1)
                    elif kind == "in":
                        e.transpose(g.ps[6][0:w, 0:P], g.flip_in[:, 0:w], g.ident[:, :]).then_inc(answered, 1)
                    else:
                        e.transpose(g.ps[7][:, 0:w], g.flip_ex[0:w, 1:P + 1], g.ident[0:w, 0:w])\
                            .then_inc(answered, 1)


def stage_by_src(nc, env):
    g = env
    sem = g.sem
    loaded, linked, asked, answered = sem("bs_loaded"), sem("bs_linked"), sem("bs_ask"), sem("bs_answer")
    exp_asked, exp_done, keys_ready, keys_out = sem("bs_exp_ask"), sem("bs_exp"), sem("bs_keys"), sem("bs_out")
    slices, turned, based, soft, stored = (sem("bs_slices"), sem("bs_turned"), sem("bs_based"), sem("bs_soft"),
                                           sem("bs_stored"))
    with ExitStack() as own:
        def sb(name, shape, dt=f32):
            return own.enter_context(nc.sbuf_tensor("bs_" + name, shape, dt))
        RC = sb("RC", [P, ET + 2, NRW])
        keys = sb("keys", [P, 2, ET])
        part = sb("part", [TQ, 2, 4, P])
        tiles = sb("tiles", [P, 2, ET])
        any_, carry = sb("any", [P, 1]), sb("carry", [P, 8])
        di = sb("di", [P, ET], i32)
        low = sb("low", [P, 2, ET])
        lowt = sb("lowt", [TQ, 2, 4, P], bf16)
        flat, digits_out, ends = sem("bs_flat"), sem("bs_digits_out"), sem("bs_ends")
        with nc.Block() as block:
            @block.gpsimd
            def _(e):
                e.wait_ge(stored, 16)
                for j in range(NT):
                    e.indirect_dma_start(out=g.LT[:, j, :], out_offset=None, in_=g.LSD[:, :],
                                         in_offset=IOA(ap=g.end_s[:, j:j + 1], axis=0)).then_inc(ends, 16)
                e.wait_ge(ends, 16 * NT)

            @block.sync
            def _(e):
                e.dma_start(RC[:, 1:ET + 1, :], g.RECD[1:EP + 1, :].rearrange("(p j) w -> p j w", j=ET))\
                    .then_inc(loaded, 16)
                e.dma_start(RC[:, 0:1, 0:2], g.RECD[0:EP, :].rearrange("(p j) w -> p j w", j=ET)[:, 0:1, 0:2])\
                    .then_inc(loaded, 16)
                e.dma_start(RC[:, ET + 1:ET + 2, 0:2],
                            g.RECD[2:EP + 2, :].rearrange("(p j) w -> p j w", j=ET)[:, ET - 1:ET, 0:2])\
                    .then_inc(loaded, 16)
                e.wait_ge(keys_ready, 1)
                e.dma_start(g.KEYD.rearrange("n (p j) -> p n j", j=ET), keys[:, :, :]).then_inc(keys_out, 16)
                e.wait_ge(keys_out, 16)
                for m in range(2):
                    e.dma_start(part[:, m, :, :], g.KEYD[m, :].rearrange("(i q p) -> q i p", i=4, p=P))\
                        .then_inc(slices, 16)
                for m, flat_row in ((0, g.SLOW), (1, g.DLOW)):
                    e.wait_ge(flat, m + 1)
                    e.dma_start(flat_row.rearrange("(i q p) -> q i p", i=4, p=P), lowt[:, m, :, :])\
                        .then_inc(digits_out, 16)
                e.wait_ge(digits_out, 32)
                e.wait_ge(soft, 1)
                e.dma_start(g.LSD.rearrange("(p j) w -> p j w", j=ET), g.T1[:, :, :]).then_inc(stored, 16)
                e.wait_ge(stored, 16)

            @block.scalar
            def _(e):
                e.wait_ge(exp_asked, 1)
                e.activation(g.T3[:, :, :], g.T3[:, :, :], ACT.Exp).then_inc(exp_done, 1)
                e.wait_ge(exp_asked, 2)
                e.activation(g.T2[:, :, :], g.T2[:, :, :], ACT.Ln).then_inc(exp_done, 1)

            @block.vector
            def _(e):
                link = Link(e, linked)
                flip, exp = Asks(e, asked, answered), Asks(e, exp_asked, exp_done)
                e.wait_ge(loaded, 48)
                e.tensor_copy(keys[:, 0, :], RC[:, 1:ET + 1, 0])
                link(e.tensor_copy(keys[:, 1, :], RC[:, 1:ET + 1, 1]))
                e.sem_inc(keys_ready, 1)
                link(e.tensor_copy(g.dsts_c[:, :], keys[:, 1, :]))
                order_masks(e, g, link, flip, g.os, RC[:, :, 0], any_)
                for m in range(2):
                    e.wait_ge(turned, 2)
                    for i in range(4):
                        ins = e.tensor_copy(tiles[:, m, i * TQ:(i + 1) * TQ], g.ps[i][:, m * P:m * P + TQ])
                    link(ins)
                link(e.tensor_copy(g.dsts_t[:, :], tiles[:, 1, :]))
                link(e.tensor_copy(g.base_s[0:1, :], tiles[0:1, 0, :]))
                flip()
                link(e.tensor_tensor(g.lrel_s[:, :], tiles[:, 0, :], g.ps[5][:, 0:ET], ALU.subtract))
                for m, index, high in ((0, g.src_c, g.shi_c), (1, g.dsts_c, g.dhi_s)):
                    link(e.tensor_single_scalar(di[:, :], index[:, :], P - 1, ALU.bitwise_and))
                    link(e.tensor_copy(low[:, m, :], di[:, :]))
                    link(e.tensor_single_scalar(di[:, :], index[:, :], 7, ALU.arith_shift_right))
                    link(e.tensor_copy(high[:, :], di[:, :]))
                    flip()
                    for i in range(4):
                        ins = e.tensor_copy(lowt[:, m, i, :], g.ps[i][0:TQ, 0:P])
                    link(ins)
                    e.sem_inc(flat, 1)
                S, M, V, o = g.T3, g.T1, g.T2, g.os
                link(e.tensor_copy(S[:, :, :], RC[:, 1:ET + 1, 2:10]))
                seg_scan(e, g, link, flip, 8, False, ALU.add, ALU.max, o.fneg, o.fnegT, -BIG, S, M, carry)
                link(e.tensor_tensor(V[:, :, :], M[:, :, :], bc_last(o.last[:, :], 8), ALU.mult))
                seg_scan(e, g, link, flip, 8, True, ALU.mult, ALU.add, o.gm, o.gmT, 0.0, V, M, carry)
                link(e.tensor_tensor(S[:, :, :], S[:, :, :], M[:, :, :], ALU.subtract))
                exp()
                seg_scan(e, g, link, flip, 8, False, ALU.mult, ALU.add, o.fm, o.fmT, 0.0, S, V, carry)
                link(e.tensor_single_scalar(V[:, :, :], V[:, :, :], 1.0, ALU.max))
                exp()
                link(e.tensor_tensor(M[:, :, :], M[:, :, :], V[:, :, :], ALU.add))
                e.sem_inc(soft, 1)

            @block.tensor
            def _(e):
                def turn(m):
                    e.wait_ge(slices, 16 * (m + 1) if m else 32)
                    for i in range(4):
                        ins = e.transpose(g.ps[i][:, m * P:m * P + TQ], part[:, m, i, :], g.ident[0:TQ, 0:TQ])
                    ins.then_inc(turned, 1)

                kinds = ORDER_FLIPS + [("base", 0), ("low", 0), ("low", 1)] + scan_flips(8, 3)
                for k, (kind, w) in enumerate(kinds):
                    if kind == "base":
                        turn(0)
                        turn(1)
                    e.wait_ge(asked, k + 1)
                    if kind == "base":
                        e.matmul(g.ps[5][:, 0:ET], lhsT=g.ones[0:1, :], rhs=tiles[0:1, 0, :],
                                 start=True, stop=True).then_inc(answered, 1)
                    elif kind == "low":
                        for i in range(4):
                            ins = e.transpose(g.ps[i][0:TQ, 0:P], low[:, w, i * TQ:(i + 1) * TQ], g.ident[:, :])
                        ins.then_inc(answered, 1)
                    elif kind == "in":
                        e.transpose(g.ps[6][0:w, 0:P], g.flip_in[:, 0:w], g.ident[:, :]).then_inc(answered, 1)
                    else:
                        e.transpose(g.ps[7][:, 0:w], g.flip_ex[0:w, 1:P + 1], g.ident[0:w, 0:w])\
                            .then_inc(answered, 1)


def stage_messages0(nc, env):
    g = env
    sem = g.sem
    linked, asked, answered = sem("m0_linked"), sem("m0_ask"), sem("m0_answer")
    root_asked, root_done, summed, stored, rows_in = (sem("m0_root_ask"), sem("m0_root"), sem("m0_summed"),
                                                      sem("m0_stored"), sem("m0_rows"))
    table_out = sem("m0_table_out")
    with ExitStack() as own:
        look = Lookup(g, lambda x, shape, dt=f32: own.enter_context(nc.sbuf_tensor(x, shape, dt)), "lk0", 8,
                      LOOKED // (2 * RU))
        ahead = Ahead(nc, g, own, "m0", ET - LOOKED)
        carry = own.enter_context(nc.sbuf_tensor("m0_carry", [P, 8], f32))
        with nc.Block() as block:
            @block.gpsimd
            def _(e):
                e.wait_ge(table_out, 16)
                ahead.gather(e, g.src_c[:, LOOKED:ET], g.LTD[:, :], g.T3[:, LOOKED:ET, :])
                e.wait_ge(stored, 16)
                for j in range(NT):
                    e.indirect_dma_start(out=g.MSG[:, j, :], out_offset=None, in_=g.MSD[:, :],
                                         in_offset=IOA(ap=g.end_d[:, j:j + 1], axis=0)).then_inc(rows_in, 16)
                e.wait_ge(rows_in, 16 * NT)

            @block.scalar
            def _(e):
                e.wait_ge(root_asked, 1)
                e.activation(g.T3[:, :, :], g.T3[:, :, :], ACT.Exp).then_inc(root_done, 1)
                e.wait_ge(root_asked, 2)
                e.activation(g.PD[:, :, :], g.PD[:, :, :], ACT.Sqrt).then_inc(root_done, 1)

            @block.vector
            def _(e):
                link = Link(e, linked)
                flip, root = Asks(e, asked, answered), Asks(e, root_asked, root_done)
                link(e.tensor_single_scalar(g.PD[:, :, :], g.PD[:, :, :], 1e-9, ALU.max))
                look.split_table(e, link, g.LT[:, :, :])
                look.vector(e, g, g.shi_c, g.T3)
                e.wait_ge(look.masked[1], 2 * look.turns + 1)
                e.wait_ge(ahead.landed, 16 * ahead.columns)
                link(e.tensor_tensor(g.T3[:, :, :], g.GAT[:, :, 0:8], g.T3[:, :, :], ALU.subtract))
                root()
                link(e.scalar_tensor_tensor(g.PD[:, :, :], g.T3[:, :, :], 1e-9, g.PD[:, :, :], ALU.max, ALU.mult))
                root()
                link(e.tensor_tensor(g.PD[:, :, :], g.PD[:, :, :], g.GAT[:, :, 8:16], ALU.mult))
                seg_scan(e, g, link, flip, 8, False, ALU.mult, ALU.add, g.od.fm, g.od.fmT, 0.0, g.PD, g.T1, carry)
                e.sem_inc(summed, 1)
                e.wait_ge(rows_in, 16 * NT)
                link(e.tensor_single_scalar(g.T3[:, 0:NT, 0], g.deg_d[:, :], 0.0, ALU.is_gt))
                link(e.tensor_tensor(g.MSG[:, :, :], g.MSG[:, :, :], bc_last(g.T3[:, 0:NT, 0], 8), ALU.mult))

            @block.sync
            def _(e):
                e.dma_start(g.LTD.rearrange("(j p) w -> p j w", p=P), g.LT[:, :, :]).then_inc(table_out, 16)
                look.load_rows(e, g.SLOW)
                e.wait_ge(summed, 1)
                e.dma_start(g.MSD.rearrange("(p j) w -> p j w", j=ET), g.T1[:, :, :]).then_inc(stored, 16)
                e.wait_ge(stored, 16)

            @block.tensor
            def _(e):
                look.tensor(e, g)
                tensor_flips(e, g, asked, answered, scan_flips(8, 1))



def stage_update0(nc, env, A):
    g = env
    sem = g.sem
    loaded, flipped, kept, linked, asked, root_done = (sem("u0_loaded"), sem("u0_flipped"), sem("u0_kept"),
                                                       sem("u0_linked"), sem("u0_ask"), sem("u0_root"))
    ready, first, act_in, turned, act_t, second, done = (sem("u0_ready"), sem("u0_first"), sem("u0_act"),
                                                         sem("u0_turned"), sem("u0_act_t"), sem("u0_second"),
                                                         sem("u0_done"))
    with ExitStack() as own:
        def sb(name, shape):
            return own.enter_context(nc.sbuf_tensor("u0_" + name, shape, f32))
        M, C = sb("M", [8, NP]), sb("C", [8, NP])
        st = sb("st", [8, 8])
        Wa, Wd, Wo = sb("Wa", [8, D]), sb("Wd", [P, 2, D]), sb("Wo", [P, 2, D])
        b1, b2, bo = sb("b1", [P, D]), sb("b2", [P, D]), sb("bo", [P, D])
        R, Q, RT = sb("R", [P, 2, D]), sb("Q", [P, 2, D]), sb("RT", [P, 2, D])
        with nc.Block() as block:
            @block.sync
            def _(e):
                e.dma_start(Wa[:, :], A["L0_gnn_W_agg"][:, :]).then_inc(loaded, 16)
                e.dma_start(Wd[:, :, :], A["L0_gnn_W_apply_dst"].rearrange("(h p) m -> p h m", p=P))\
                    .then_inc(loaded, 16)
                e.dma_start(Wo[:, :, :], A["L0_gnn_W_apply"].rearrange("(h p) m -> p h m", p=P))\
                    .then_inc(loaded, 16)
                e.dma_start(b1[:, :], bc_row(A["L0_gnn_b_agg"])).then_inc(loaded, 16)
                e.dma_start(b2[:, :], bc_row(A["L0_gnn_b_apply_dst"])).then_inc(loaded, 16)
                e.dma_start(bo[:, :], bc_row(A["L0_gnn_b_apply"])).then_inc(loaded, 16)
                e.dma_start(st[:, 6:7], A["L0_gnn_bn_gamma"][:, None]).then_inc(loaded, 16)
                e.dma_start(st[:, 7:8], A["L0_gnn_bn_beta"][:, None]).then_inc(loaded, 16)

            @block.scalar
            def _(e):
                e.wait_ge(asked, 1)
                e.activation(st[:, 2:3], st[:, 1:2], ACT.Sqrt).then_inc(root_done, 1)
                for j in range(NT):
                    e.wait_ge(turned, j + 1)
                    if j >= 2:
                        e.wait_ge(second, j - 1)
                    e.activation(RT[:, j % 2, :], g.ps[2 + j % 2][:, 0:D], ACT.Copy).then_inc(act_t, 1)

            @block.vector
            def _(e):
                link = Link(e, linked)
                for q in range(7):
                    e.wait_ge(flipped, q + 1)
                    m = min(4, NT - 4 * q)
                    link(e.tensor_copy(M[:, q * 4 * P:(q * 4 + m) * P], g.ps[q][0:8, 0:m * P]))
                link(e.tensor_reduce(st[:, 0:1], M[:, 0:NN], AX.X, ALU.add))
                link(e.tensor_single_scalar(st[:, 0:1], st[:, 0:1], 1.0 / NN, ALU.mult))
                link(e.tensor_scalar(M[:, :], M[:, :], st[:, 0:1], None, ALU.subtract))
                link(e.tensor_tensor(C[:, 0:NN], M[:, 0:NN], M[:, 0:NN], ALU.mult))
                link(e.tensor_reduce(st[:, 1:2], C[:, 0:NN], AX.X, ALU.add))
                link(e.tensor_scalar(st[:, 1:2], st[:, 1:2], 1.0 / NN, LN_EPS, ALU.mult, ALU.add))
                e.wait_ge(loaded, 128)
                e.sem_inc(asked, 1)
                e.wait_ge(root_done, 1)
                link(e.reciprocal(st[:, 3:4], st[:, 2:3]))
                link(e.tensor_tensor(st[:, 4:5], st[:, 3:4], st[:, 6:7], ALU.mult))
                link(e.tensor_scalar(M[:, :], M[:, :], st[:, 4:5], st[:, 7:8], ALU.mult, ALU.add))
                link(e.tensor_tensor(b1[:, :], b1[:, :], b2[:, :], ALU.add))
                link(e.tensor_tensor(g.X[:, :, :], g.X[:, :, :], bc_mid(bo[:, :], NT), ALU.add))
                e.sem_inc(ready, 1)
                for j in range(NT + 2):
                    if j < NT:
                        e.wait_ge(first, j + 1)
                        link(e.tensor_tensor(Q[:, j % 2, :], g.ps[j % 2][:, 0:D], b1[:, :], ALU.add))
                        if j >= 2:
                            e.wait_ge(turned, j - 1)
                        e.scalar_tensor_tensor(R[:, j % 2, :], Q[:, j % 2, :], 0.2, Q[:, j % 2, :], ALU.mult,
                                               ALU.max).then_inc(act_in, 1)
                    if j >= 2:
                        i = j - 2
                        e.wait_ge(second, i + 1)
                        e.tensor_tensor(g.X[:, i, :], g.X[:, i, :], g.ps[4 + i % 2][:, 0:D], ALU.add)\
                            .then_inc(done, 1)

            @block.tensor
            def _(e):
                for q in range(7):
                    m = min(4, NT - 4 * q)
                    for i in range(m):
                        last = e.transpose(g.ps[q][0:8, i * P:(i + 1) * P], g.MSG[:, 4 * q + i, :], g.ident[:, :])
                    last.then_inc(flipped, 1)
                e.wait_ge(ready, 1)
                for j in range(NT + 2):
                    if j < NT:
                        if j >= 2:
                            e.wait_ge(act_in, j - 1)
                        at = slice(j * P, (j + 1) * P)
                        e.matmul(g.ps[j % 2][:, 0:D], lhsT=M[:, at], rhs=Wa[:, :], start=True, stop=False)
                        e.matmul(g.ps[j % 2][:, 0:D], lhsT=g.HT[:, 0, at], rhs=Wd[:, 0, :], start=False, stop=False)
                        e.matmul(g.ps[j % 2][:, 0:D], lhsT=g.HT[:, 1, at], rhs=Wd[:, 1, :], start=False, stop=True)\
                            .then_inc(first, 1)
                    if 1 <= j <= NT:
                        i = j - 1
                        e.wait_ge(act_in, i + 1)
                        if i >= 2:
                            e.wait_ge(act_t, i - 1)
                        e.transpose(g.ps[2 + i % 2][:, 0:P], R[:, i % 2, 0:P], g.ident[:, :])
                        e.transpose(g.ps[2 + i % 2][:, P:D], R[:, i % 2, P:D], g.ident[:, :]).then_inc(turned, 1)
                    if j >= 2:
                        i = j - 2
                        e.wait_ge(act_t, i + 1)
                        if i >= 2:
                            e.wait_ge(done, i - 1)
                        e.matmul(g.ps[4 + i % 2][:, 0:D], lhsT=RT[:, i % 2, 0:P], rhs=Wo[:, 0, :], start=True,
                                 stop=False)
                        e.matmul(g.ps[4 + i % 2][:, 0:D], lhsT=RT[:, i % 2, P:D], rhs=Wo[:, 1, :], start=False,
                                 stop=True).then_inc(second, 1)



def stage_project(nc, env, A, name, weight, bias, vec, groups, scale, T, V, table, row, pre=None):
    g = env
    sem = g.sem
    loaded, product, kept, linked, ready, stored = (sem(name + x) for x in ("_loaded", "_product", "_kept",
                                                                           "_linked", "_ready", "_stored"))
    with ExitStack() as own:
        W = own.enter_context(nc.sbuf_tensor(name + "_W", [P, 2, D], f32))
        b = own.enter_context(nc.sbuf_tensor(name + "_b", [P, D], f32))
        v = own.enter_context(nc.sbuf_tensor(name + "_v", [P, len(vec), D], f32))
        tmp = own.enter_context(nc.sbuf_tensor(name + "_tmp", [P, NT, D], f32))
        if pre is not None:
            ahead = Ahead(nc, g, own, name, pre.shape[1])
        with nc.Block() as block:
            if pre is not None:
                @block.gpsimd
                def _(e):
                    ahead.gather(e, g.src_t[:, 0:ahead.columns], g.XLD[:, :], pre)

            @block.sync
            def _(e):
                e.dma_start(W[:, :, :], weight.rearrange("(h p) m -> p h m", p=P)).then_inc(loaded, 16)
                e.dma_start(b[:, :], bc_row(bias)).then_inc(loaded, 16)
                n = 2
                for q, parts in enumerate(vec):
                    for at, part in parts:
                        e.dma_start(v[:, q, at:at + part.shape[0]], bc_row(part)).then_inc(loaded, 16)
                        n += 1
                e.wait_ge(loaded, 16 * n)
                e.sem_inc(ready, 1)
                e.wait_ge(ready, 2)
                e.dma_start(table.rearrange("(j p) d -> p j d", p=P), T[:, :, 0:row]).then_inc(stored, 16)
                e.wait_ge(stored, 16)

            @block.tensor
            def _(e):
                e.wait_ge(ready, 1)
                for j in range(NT):
                    if j >= 4:
                        e.wait_ge(kept, j - 3)
                    for h in range(2):
                        m = e.matmul(g.ps[j % 4][:, 0:D], lhsT=g.HT[:, h, j * P:(j + 1) * P], rhs=W[:, h, :],
                                     start=h == 0, stop=h == 1)
                    m.then_inc(product, 1)

            @block.vector
            def _(e):
                link = Link(e, linked)
                e.wait_ge(ready, 1)
                for j in range(NT):
                    e.wait_ge(product, j + 1)
                    e.tensor_tensor(T[:, j, 0:D], g.ps[j % 4][:, 0:D], b[:, :], ALU.add).then_inc(kept, 1)
                e.wait_ge(kept, NT)
                for q in range(len(vec)):
                    link(e.tensor_tensor(tmp[:, :, :], T[:, :, 0:D], bc_mid(v[:, q, :], NT), ALU.mult))
                    link(e.tensor_reduce(V[q], tmp[:, :, :].rearrange("p j (n c) -> p j n c", n=groups), AX.X,
                                         ALU.add))
                    if scale != 1.0:
                        link(e.tensor_single_scalar(V[q], V[q], scale, ALU.mult))
                e.sem_inc(ready, 1)



def stage_edges1(nc, env, SN, TN, AL, pre):
    g = env
    sem = g.sem
    linked, asked, answered, exp_asked, exp_done = (sem("e1_linked"), sem("e1_ask"), sem("e1_answer"),
                                                    sem("e1_exp_ask"), sem("e1_exp"))
    zero_ready, zeroed, filled, expanded, soft, stored = (
        sem("e1_zero"), sem("e1_zeroed"), sem("e1_filled"), sem("e1_expanded"), sem("e1_soft"), sem("e1_stored"))
    with ExitStack() as own:
        def sb(name, shape, dt=f32):
            return own.enter_context(nc.sbuf_tensor("e1_" + name, shape, dt))
        look = Lookup(g, sb, "lk1", 2)
        ahead = Ahead(nc, g, own, "e1", pre.shape[1])
        S, M, V, TG = (sb(x, [P, ET, 2]) for x in ("S", "M", "V", "TG"))
        carry = sb("carry", [P, 8])
        with nc.Block() as block:
            @block.sync
            def _(e):
                e.wait_ge(zero_ready, 1)
                e.dma_start(g.Z2.rearrange("(p j) w -> p j w", j=ET), V[:, :, :]).then_inc(zeroed, 16)
                look.load_rows(e, g.DLOW)
                e.wait_ge(filled, 16 * NT)
                e.dma_start(M[:, :, :], g.Z2.rearrange("(p j) w -> p j w", j=ET)).then_inc(expanded, 16)
                e.wait_ge(soft, 1)
                e.dma_start(AL.rearrange("(p j) w -> p j w", j=ET), TG[:, :, :]).then_inc(stored, 16)
                e.wait_ge(stored, 16)

            @block.gpsimd
            def _(e):
                e.wait_ge(zeroed, 16)
                for j in range(NT):
                    e.indirect_dma_start(out=g.Z2[:, :], out_offset=IOA(ap=g.put_s[:, j:j + 1], axis=0),
                                         in_=SN[:, j, :], in_offset=None, bounds_check=EP - 1,
                                         oob_is_err=False).then_inc(filled, 16)
                ahead.gather(e, g.dsts_t[:, 0:ahead.columns], g.WHD[:, :], pre)

            @block.scalar
            def _(e):
                e.wait_ge(exp_asked, 1)
                e.activation(TG[:, :, :], TG[:, :, :], ACT.Exp).then_inc(exp_done, 1)

            @block.vector
            def _(e):
                link = Link(e, linked)
                flip, exp = Asks(e, asked, answered), Asks(e, exp_asked, exp_done)
                link(e.memset(V[:, :, :], 0.0))
                e.sem_inc(zero_ready, 1)
                look.split_table(e, link, TN[:, :, :])
                look.vector(e, g, g.dhi_s, TG)
                e.wait_ge(look.masked[1], 2 * RI + 1)
                e.wait_ge(expanded, 16)
                seg_scan(e, g, link, flip, 2, False, ALU.mult, ALU.add, g.os.fm, g.os.fmT, 0.0, M, S, carry)
                link(e.tensor_tensor(TG[:, :, :], TG[:, :, :], S[:, :, :], ALU.add))
                link(e.scalar_tensor_tensor(TG[:, :, :], TG[:, :, :], 0.2, TG[:, :, :], ALU.mult, ALU.max))
                seg_softmax(e, g, link, flip, exp, 2, g.os, TG, M, V, carry)
                e.sem_inc(soft, 1)

            @block.tensor
            def _(e):
                look.tensor(e, g)
                tensor_flips(e, g, asked, answered, scan_flips(2, 5))



def stage_aggregate(nc, env, name, table, row, index, lrel, base, acc, weights=None, heads=0, pre=None, OH=None):
    g = env
    sem = g.sem
    landed, hot, scaled, w_in = ([sem(f"{name}_{x}{s}") for s in range(SETS)]
                                 for x in ("landed", "hot", "scaled", "w_in"))
    staged, seen, spread = sem(name + "_staged"), sem(name + "_seen"), sem(name + "_spread")
    summed, added = sem(name + "_summed"), [sem(f"{name}_added{h}") for h in range(2)]
    CREDIT, BANKS = SETS * U, 8
    PI = 0 if pre is None else pre.shape[1] // CREDIT
    with ExitStack() as own:
        def sb(n, shape, dt=f32):
            return own.enter_context(nc.sbuf_tensor(f"{name}_{n}", shape, dt))
        idx = sb("idx", [P, SETS, U], i32)
        G = sb("G", [P, SETS, U, row])
        if OH is None:
            OH = sb("OH", [P, SETS, U, P])
        W = sb("W", [P, SETS, U, max(heads, 1)])

        def rows_of(k, s, there):
            return pre[:, k * CREDIT + s * U:k * CREDIT + (s + 1) * U, :] if there else G[:, s, :, :]

        def turns(e, turn):
            for k in range(PI):
                turn(k, True)
            with e.Fori(PI, WI) as k:
                turn(k, False)

        with nc.Block() as block:
            @block.gpsimd
            def _(e):
                def gather(k, first=False):
                    for s in range(SETS):
                        if not first:
                            e.wait_ge(summed, k * CREDIT + (s + 1) * U)
                        e.tensor_copy(idx[:, s, :], index[:, bass.ds(k * (SETS * U) + s * U, U)])\
                            .then_inc(staged, 1)
                        e.wait_ge(staged, (k - PI) * SETS + (s + 1))
                        e.sem_inc(seen, 1)
                        for i in range(U):
                            e.indirect_dma_start(out=G[:, s, i, :], out_offset=None, in_=table,
                                                 in_offset=IOA(ap=idx[:, s, i:i + 1], axis=0))\
                                .then_inc(landed[s], 16)

                gather(PI, first=True)
                with e.Fori(PI + 1, WI) as k:
                    gather(k)

            if weights is not None:
                @block.sync
                def _(e):
                    w_t = weights.rearrange("(t p) w -> p t w", p=P)
                    with e.Fori(0, WI) as k:
                        for s in range(SETS):
                            e.wait_ge(summed, k * CREDIT + (s + 1) * U)
                            e.dma_start(W[:, s, :, :], w_t[:, bass.ds(k * (SETS * U) + s * U, U), :])\
                                .then_inc(w_in[s], 16)

            if heads == 2:
                @block.scalar
                def _(e):
                    def turn(k, there):
                        for s in range(SETS):
                            e.wait_ge(w_in[s], k * 16 + 16)
                            if not there:
                                e.wait_ge(landed[s], (k - PI) * (16 * U) + 16 * U)
                            rows = rows_of(k, s, there)
                            for i in range(U):
                                for h in range(2):
                                    v = rows[:, i, h * P:(h + 1) * P]
                                    ins = e.activation(v, v, ACT.Copy, scale=W[:, s, i, h:h + 1])
                            ins.then_inc(scaled[s], 1)
                    turns(e, turn)

            if heads == 8:
                @block.scalar
                def _(e):
                    with e.Fori(0, WI) as k:
                        for s in range(SETS):
                            e.wait_ge(summed, k * CREDIT + (s + 1) * U)
                            for i in range(U):
                                ins = e.activation(OH[:, s, i, :], g.iota_row[:, :], ACT.Abs, scale=-1.0,
                                                   bias=lrel[:, bass.ds(k * CREDIT + (s * U + i), 1)])
                            ins.then_inc(spread, 1)
                            e.wait_ge(spread, k * SETS + (s + 1))
                            e.activation(OH[:, s, :, :], OH[:, s, :, :], ACT.Relu, scale=-1.0,
                                         bias=g.ones[:, 0:1]).then_inc(hot[s], 1)

            @block.vector
            def _(e):
                for h in range(2):
                    e.memset(acc[:, h, :], 0.0).then_inc(added[h], 1)
                    for n in range(BANKS - 1):
                        e.sem_inc(added[h], 1)

                def prepare(k, s, there):
                    at = bass.ds(k * CREDIT + s * U, U)
                    if heads == 8:
                        e.wait_ge(w_in[s], k * 16 + 16)
                        if not there:
                            e.wait_ge(landed[s], (k - PI) * (16 * U) + 16 * U)
                        v = rows_of(k, s, there)[:, :, 0:D].rearrange("p i (h c) -> p i h c", h=8)
                        e.tensor_tensor(v, v, W[:, s, :, :][:, :, :, None].to_broadcast([P, U, 8, D // 8]),
                                        ALU.mult).then_inc(scaled[s], 1)
                    else:
                        e.wait_ge(summed, k * CREDIT + (s + 1) * U)
                        e.tensor_tensor(OH[:, s, :, :], bc_mid(g.iota_row[:, :], U), bc_last(lrel[:, at], P),
                                        ALU.is_equal).then_inc(hot[s], 1)

                def turn(k, there=False, next_there=False, last=False):
                    for s in range(SETS):
                        if s < SETS - 1:
                            prepare(k, s + 1, there)
                        elif not last:
                            prepare(k + 1, 0, next_there)
                        _, places = nc.values_load_multi_w_load_instructions(
                            base[0:1, bass.ds(k * CREDIT + s * U, U)], engines=[mybir.EngineType.DVE],
                            min_val=0, max_val=NP - 1,
                            skip_runtime_bounds_check_because="a window starts at the node of one of its edges")
                        for i in range(U):
                            t = k * CREDIT + (s * U + i)
                            e.wait_ge(summed, t + (CREDIT + 1))
                            for h in range(2):
                                e.wait_ge(added[h], t + BANKS)
                                w = acc[:, h, bass.ds(places[i], P)]
                                e.tensor_tensor(w, w, g.ps[i % BANKS][:, h * P:(h + 1) * P], ALU.add)\
                                    .then_inc(added[h], 1)

                prepare(0, 0, PI > 0)
                for k in range(PI):
                    turn(k, True, k < PI - 1)
                with e.Fori(PI, WI - 1) as k:
                    turn(k)
                turn(WI - 1, last=True)

            @block.tensor
            def _(e):
                for n in range(CREDIT):
                    e.sem_inc(summed, 1)

                def turn(k, there):
                    for s in range(SETS):
                        e.wait_ge(hot[s], k + 1)
                        if weights is not None:
                            e.wait_ge(scaled[s], k + 1)
                        elif not there:
                            e.wait_ge(landed[s], (k - PI) * (16 * U) + 16 * U)
                        rows = rows_of(k, s, there)
                        for i in range(U):
                            t = k * (SETS * U) + (s * U + i)
                            if not there or t >= BANKS:
                                for h in range(2):
                                    e.wait_ge(added[h], t + 1)
                            for h in range(2):
                                m = e.matmul(g.ps[i % BANKS][:, h * P:(h + 1) * P], lhsT=rows[:, i, h * P:(h + 1) * P],
                                             rhs=OH[:, s, i, :], start=True, stop=True)
                            m.then_inc(summed, 1)
                turns(e, turn)


def stage_update1(nc, env, acc):
    g = env
    loaded, linked, turned, done = g.sem("u1_loaded"), g.sem("u1_linked"), g.sem("u1_turned"), g.sem("u1_done")
    with ExitStack() as own:
        WH = own.enter_context(nc.sbuf_tensor("u1_WH", [P, NT, D], f32))
        lone = own.enter_context(nc.sbuf_tensor("u1_lone", [P, NT], f32))
        with nc.Block() as block:
            @block.sync
            def _(e):
                e.dma_start(WH[:, :, :], g.WHD.rearrange("(j p) d -> p j d", p=P)).then_inc(loaded, 16)

            @block.tensor
            def _(e):
                for j in range(NT):
                    if j >= 4:
                        e.wait_ge(done, j - 3)
                    for h in range(2):
                        m = e.transpose(g.ps[j % 4][:, h * P:(h + 1) * P], acc[:, h, j * P:(j + 1) * P],
                                        g.ident[:, :])
                    m.then_inc(turned, 1)

            @block.vector
            def _(e):
                link = Link(e, linked)
                link(e.tensor_single_scalar(lone[:, :], g.deg_s[:, :], 0.0, ALU.is_equal))
                e.wait_ge(loaded, 16)
                link(e.tensor_tensor(WH[:, :, :], WH[:, :, :], bc_last(lone[:, :], D), ALU.mult))
                link(e.tensor_tensor(g.X[:, :, :], g.X[:, :, :], WH[:, :, :], ALU.add))
                for j in range(NT):
                    e.wait_ge(turned, j + 1)
                    e.tensor_tensor(g.X[:, j, :], g.X[:, j, :], g.ps[j % 4][:, 0:D], ALU.add).then_inc(done, 1)


def stage_update2(nc, env, A, acc):
    g = env
    loaded, linked, product, done, added = (g.sem("u2_loaded"), g.sem("u2_linked"), g.sem("u2_product"),
                                            g.sem("u2_done"), g.sem("u2_added"))
    with ExitStack() as own:
        Wn = own.enter_context(nc.sbuf_tensor("u2_Wn", [P, 2, D], f32))
        Ws = own.enter_context(nc.sbuf_tensor("u2_Ws", [P, 2, D], f32))
        b = own.enter_context(nc.sbuf_tensor("u2_b", [P, D], f32))
        rdeg = own.enter_context(nc.sbuf_tensor("u2_rdeg", [P, NT], f32))
        with nc.Block() as block:
            @block.sync
            def _(e):
                e.dma_start(Wn[:, :, :], A["L2_gnn_W_neigh"].rearrange("(h p) m -> p h m", p=P)).then_inc(loaded, 16)
                e.dma_start(Ws[:, :, :], A["L2_gnn_W_self"].rearrange("(h p) m -> p h m", p=P)).then_inc(loaded, 16)
                e.dma_start(b[:, :], bc_row(A["L2_gnn_b_self"])).then_inc(loaded, 16)

            @block.tensor
            def _(e):
                e.wait_ge(loaded, 48)
                for j in range(NT):
                    at = slice(j * P, (j + 1) * P)
                    if j >= 2:
                        e.wait_ge(done, j - 1)
                    for src, w, o in ((acc, Wn, 0), (g.HT, Ws, 2)):
                        for h in range(2):
                            m = e.matmul(g.ps[o + j % 2][:, 0:D], lhsT=src[:, h, at], rhs=w[:, h, :],
                                         start=h == 0, stop=h == 1)
                    m.then_inc(product, 1)

            @block.vector
            def _(e):
                link = Link(e, linked)
                link(e.tensor_single_scalar(rdeg[:, :], g.deg_d[:, :], 1.0, ALU.max))
                link(e.reciprocal(rdeg[:, :], rdeg[:, :]))
                e.wait_ge(loaded, 48)
                link(e.tensor_tensor(g.X[:, :, :], g.X[:, :, :], bc_mid(b[:, :], NT), ALU.add))
                for j in range(NT):
                    e.wait_ge(product, j + 1)
                    e.scalar_tensor_tensor(g.X[:, j, :], g.ps[j % 2][:, 0:D], rdeg[:, j:j + 1], g.X[:, j, :],
                                           ALU.mult, ALU.add).then_inc(added, 1)
                    e.wait_ge(added, j + 1)
                    e.tensor_tensor(g.X[:, j, :], g.X[:, j, :], g.ps[2 + j % 2][:, 0:D], ALU.add).then_inc(done, 1)



def stage_border(nc, env, T):
    g = env
    zeroed, stored = g.sem("b3_zeroed"), g.sem("b3_stored")
    with nc.Block() as block:
        @block.vector
        def _(e):
            e.memset(T[:, 0, :], 0.0).then_inc(zeroed, 1)

        @block.sync
        def _(e):
            e.wait_ge(zeroed, 1)
            e.dma_start(g.XRD[NP:NP + P, :], T[:, 0, :]).then_inc(stored, 16)
            e.wait_ge(stored, 16)


def stage_scores3(nc, env, A, pre):
    g = env
    sem = g.sem
    landed, free, hot, row_in, win_in, sc_ready, sc_out = (
        [sem(f"s3_{x}{s}") for s in range(SETS)]
        for x in ("landed", "free", "hot", "row", "win", "sc_ready", "sc_out"))
    staged, seen, att_in = sem("s3_staged"), sem("s3_seen"), sem("s3_att")
    summed, drained, weighed = sem("s3_summed"), sem("s3_drained"), sem("s3_weighed")
    BANKS, PER = 8, SETS * U
    with ExitStack() as own:
        def sb(n, shape, dt=f32):
            return own.enter_context(nc.sbuf_tensor("s3_" + n, shape, dt))
        idx = sb("idx", [P, SETS, U], i32)
        G, XR = sb("G", [P, SETS, U, XLW]), sb("XR", [P, SETS, U, XLW])
        rowb, OT = sb("rowb", [P, SETS, U * P], i32), one_hot_view(g)
        R = sb("R", [P, 2, U, D])
        L = sb("L", [P, 2, U, 8])
        att = sb("att", [P, D])
        SC = sb("SC", [P, SETS, U, 8])
        with nc.Block() as block:
            @block.gpsimd
            def _(e):
                def gather(k, first=False):
                    for s in range(SETS):
                        if not first:
                            e.wait_ge(free[s], k + 1)
                        e.tensor_copy(idx[:, s, :], g.src_t[:, bass.ds(k * PER + s * U, U)])\
                            .then_inc(staged, 1)
                        e.wait_ge(staged, (k - 1) * SETS + (s + 1))
                        e.sem_inc(seen, 1)
                        for i in range(U):
                            e.indirect_dma_start(out=G[:, s, i, :], out_offset=None, in_=g.XLD[:, :],
                                                 in_offset=IOA(ap=idx[:, s, i:i + 1], axis=0))\
                                .then_inc(landed[s], 16)

                gather(1, first=True)
                with e.Fori(2, WI) as k:
                    gather(k)

            @block.sync
            def _(e):
                e.dma_start(att[:, :], bc_row(A["L3_gnn_att"].rearrange("h c -> (h c)"))).then_inc(att_in, 16)
                with e.Fori(0, WI) as k:
                    for s in range(SETS):
                        e.wait_ge(free[s], k + 1)
                        e.dma_start(rowb[:, s, :], bc_row(A["dst_row"][bass.ds(k * (PER * P) + s * U * P, U * P)]))\
                            .then_inc(row_in[s], 16)
                        _, places = nc.values_load_multi_w_load_instructions(
                            g.base_d[0:1, bass.ds(k * PER + s * U, U)], engines=[mybir.EngineType.SP],
                            min_val=0, max_val=NP - 1,
                            skip_runtime_bounds_check_because="a window starts at the node of one of its edges")
                        for i in range(U):
                            e.dma_start(XR[:, s, i, :], g.XRD[bass.ds(places[i], P), :]).then_inc(win_in[s], 16)

            @block.scalar
            def _(e):
                sc_t = g.SCD.rearrange("(t p) w -> p t w", p=P)

                def store(k, s):
                    e.wait_ge(sc_ready[s], k * 3 + 3)
                    e.dma_start(sc_t[:, bass.ds(k * PER + s * U, U), :], SC[:, s, :, :]).then_inc(sc_out[s], 16)

                for n in range(BANKS):
                    e.sem_inc(drained, 1)
                with e.Fori(0, WI) as k:
                    for s in range(SETS):
                        e.wait_ge(weighed, k * SETS + (s + 1))
                        for i in range(U):
                            t = k * PER + (s * U + i)
                            bank = g.ps[(s * U + i) % BANKS]
                            e.wait_ge(summed, t + 1)
                            e.activation(L[:, s % 2, i, :], bank[:, D:XLW], ACT.Copy)
                            e.activation(R[:, s % 2, i, :], bank[:, 0:D], ACT.Relu, scale=0.8).then_inc(drained, 1)
                        if s >= 1:
                            store(k, s - 1)
                    store(k, SETS - 1)
                for s in range(SETS):
                    e.wait_ge(sc_out[s], 16 * WI)

            @block.vector
            def _(e):
                e.wait_ge(att_in, 16)

                def one_hot(k, s):
                    e.wait_ge(row_in[s], k * 16 + 16)
                    e.tensor_tensor(OT[:, s, :, :], rowb[:, s, :].rearrange("p (i f) -> p i f", f=P),
                                    bc_last(g.win_d[:, bass.ds(k * PER + s * U, U)], P), ALU.is_equal)\
                        .then_inc(hot[s], 1)

                def finish(k, s, first):
                    e.wait_ge(drained, k * PER + ((s + 1) * U + BANKS))
                    e.sem_inc(free[s], 1)
                    v = R[:, s % 2, :, :]
                    e.tensor_tensor(v, v, bc_mid(att[:, :], U), ALU.mult).then_inc(sc_ready[s], 1)
                    e.wait_ge(sc_ready[s], k * 3 + 1)
                    if not first:
                        e.wait_ge(sc_out[s], k * 16)
                    e.tensor_reduce(SC[:, s, :, :], v.rearrange("p i (h c) -> p i h c", h=8), AX.X, ALU.add)\
                        .then_inc(sc_ready[s], 1)
                    e.wait_ge(sc_ready[s], k * 3 + 2)
                    e.tensor_tensor(SC[:, s, :, :], SC[:, s, :, :], L[:, s % 2, :, :], ALU.add)\
                        .then_inc(sc_ready[s], 1)
                    e.wait_ge(sc_ready[s], k * 3 + 3)
                    e.sem_inc(weighed, 1)

                def turn(k, first=False, last=False):
                    for s in range(SETS):
                        if s < SETS - 1:
                            one_hot(k, s + 1)
                        elif not last:
                            one_hot(k + 1, 0)
                        finish(k, s, first)

                for s in range(SETS):
                    e.sem_inc(free[s], 1)
                for s in range(2):
                    e.sem_inc(weighed, 1)
                one_hot(0, 0)
                turn(0, first=True)
                with e.Fori(1, WI - 1) as k:
                    turn(k)
                turn(WI - 1, last=True)

            @block.tensor
            def _(e):
                def turn(k, there=False):
                    for s in range(SETS):
                        e.wait_ge(hot[s], k + 1)
                        e.wait_ge(win_in[s], k * (16 * U) + 16 * U)
                        if not there:
                            e.wait_ge(landed[s], (k - 1) * (16 * U) + 16 * U)
                        rows = pre[:, s * U:(s + 1) * U, :] if there else G[:, s, :, :]
                        for i in range(U):
                            bank = g.ps[(s * U + i) % BANKS]
                            e.wait_ge(drained, k * PER + (s * U + i + 1))
                            e.matmul(bank[:, 0:XLW], lhsT=OT[:, s, i, :], rhs=XR[:, s, i, :], start=True, stop=False)
                            e.matmul(bank[:, 0:XLW], lhsT=g.ident[:, :], rhs=rows[:, i, :], start=False, stop=True)\
                                .then_inc(summed, 1)

                turn(0, True)
                with e.Fori(1, WI) as k:
                    turn(k)


def stage_softmax3(nc, env, A, pre):
    g = env
    sem = g.sem
    loaded, linked, asked, answered, act_asked, act_done, soft, stored = (
        sem("x3_loaded"), sem("x3_linked"), sem("x3_ask"), sem("x3_answer"), sem("x3_act_ask"), sem("x3_act"),
        sem("x3_soft"), sem("x3_stored"))
    with ExitStack() as own:
        def sb(n, shape):
            return own.enter_context(nc.sbuf_tensor("x3_" + n, shape, f32))
        S, M, V = (sb(x, [P, ET, 8]) for x in ("S", "M", "V"))
        ew, lw, carry = sb("ew", [P, ET]), sb("lw", [P, ET]), sb("carry", [P, 8])
        ahead = Ahead(nc, g, own, "x3", pre.shape[1])
        with nc.Block() as block:
            @block.gpsimd
            def _(e):
                ahead.gather(e, g.src_t[:, 0:ahead.columns], g.XLD[:, :], pre)

            @block.sync
            def _(e):
                e.dma_start(S[:, :, :], g.SCD.rearrange("(p j) w -> p j w", j=ET)).then_inc(loaded, 16)
                e.dma_start(ew[:, :], A["ew"][:, :]).then_inc(loaded, 16)
                e.wait_ge(soft, 1)
                e.dma_start(g.WD.rearrange("(p j) w -> p j w", j=ET), S[:, :, :]).then_inc(stored, 16)
                e.wait_ge(stored, 16)

            @block.scalar
            def _(e):
                e.wait_ge(act_asked, 1)
                e.activation(lw[:, :], lw[:, :], ACT.Ln).then_inc(act_done, 1)
                e.wait_ge(act_asked, 2)
                e.activation(S[:, :, :], S[:, :, :], ACT.Exp).then_inc(act_done, 1)

            @block.vector
            def _(e):
                link = Link(e, linked)
                flip, act = Asks(e, asked, answered), Asks(e, act_asked, act_done)
                e.wait_ge(loaded, 32)
                link(e.tensor_single_scalar(lw[:, :], ew[:, :], 2.0 ** -64, ALU.max))
                act()
                link(e.tensor_tensor(V[:, :, :], S[:, :, :], bc_last(lw[:, :], 8), ALU.add))
                seg_softmax(e, g, link, flip, act, 8, g.od, S, M, V, carry, weight=ew[:, :], eps=1e-16)
                e.sem_inc(soft, 1)

            @block.tensor
            def _(e):
                tensor_flips(e, g, asked, answered, scan_flips(8, 4))


def stage_output(nc, env, A, acc, out):
    g = env
    loaded, linked, turned, done, stored = (g.sem("o_loaded"), g.sem("o_linked"), g.sem("o_turned"),
                                            g.sem("o_done"), g.sem("o_stored"))
    with ExitStack() as own:
        b = own.enter_context(nc.sbuf_tensor("o_b", [P, D], f32))
        with nc.Block() as block:
            @block.sync
            def _(e):
                e.dma_start(b[:, :], bc_row(A["L3_gnn_bias"])).then_inc(loaded, 16)
                o = out.rearrange("(j p) d -> p j d", p=P)
                for n in range(5):
                    e.wait_ge(done, 5 * n + 5)
                    e.dma_start(o[:, 5 * n:5 * n + 5, :], g.X[:, 5 * n:5 * n + 5, :]).then_inc(stored, 16)
                e.wait_ge(stored, 80)

            @block.tensor
            def _(e):
                for j in range(NT):
                    if j >= 4:
                        e.wait_ge(done, j - 3)
                    for h in range(2):
                        m = e.transpose(g.ps[j % 4][:, h * P:(h + 1) * P], acc[:, h, j * P:(j + 1) * P],
                                        g.ident[:, :])
                    m.then_inc(turned, 1)

            @block.vector
            def _(e):
                link = Link(e, linked)
                e.wait_ge(loaded, 16)
                link(e.tensor_tensor(g.X[:, :, :], g.X[:, :, :], bc_mid(b[:, :], NT), ALU.add))
                for j in range(NT):
                    e.wait_ge(turned, j + 1)
                    e.tensor_tensor(g.X[:, j, :], g.X[:, j, :], g.ps[j % 4][:, 0:D], ALU.add).then_inc(done, 1)


def build(nc, A, out):
    with ExitStack() as stack:
        g = Env()

        def run(stage, *args):
            taken = []

            def sem(name):
                taken.append(nc.alloc_semaphore(name=name))
                return taken[-1]

            g.sem = sem
            stage(nc, g, *args)
            nc.all_engine_barrier()
            nc.clear_and_free_semaphores(taken)
            nc.all_engine_barrier()

        def sb(name, shape, dt=f32):
            return stack.enter_context(nc.sbuf_tensor(name, shape, dt))

        def dram(name, shape, dt=f32):
            return nc.dram_tensor(name, shape, dt, kind="Internal").ap()

        g.ps = [stack.enter_context(nc.psum_tensor(f"ps{i}", [P, 512], f32)) for i in range(8)]
        g.iota_row, g.iota_p, g.ones = sb("iota_row", [P, P]), sb("iota_p", [P, 1]), sb("ones", [P, P])
        g.ident, g.before, g.after = sb("ident", [P, P]), sb("before", [P, P]), sb("after", [P, P])
        g.X, g.HT = sb("X", [P, NT, D]), sb("HT", [P, 2, NP])
        g.src_t = sb("src_t_sb", [P, ET], i32)
        g.deg_s, g.deg_d, g.start_s, g.start_d = (sb(x, [P, NT]) for x in ("deg_s", "deg_d", "start_s", "start_d"))
        g.T0, g.RKF = dram("T0", (NP, 16)), dram("RKF", (EP,), i32)
        g.lrel_d, g.win_d = sb("lrel_d", [P, ET]), sb("win_d", [P, ET])
        g.base_d = sb("base_d", [1, ET], i32)
        g.put_d, g.put_s, g.end_d, g.end_s = (sb(x, [P, NT], i32) for x in ("put_d", "put_s", "end_d", "end_s"))
        g.flip_in, g.flip_ex = sb("flip_in", [P, 8]), sb("flip_ex", [8, P + 2])
        g.od = Order(sb, "od")
        g.MSG = sb("MSG", [P, NT, 8])
        g.Z8, g.RECD, g.KEYD = dram("Z8", (EP, 8)), dram("RECD", (EP + 2, NRW)), dram("KEYD", (2, EP))
        g.WHD, g.H2D, g.XLD, g.XRD = (dram("WHD", (NP, D)), dram("H2D", (NP, D)), dram("XLD", (NP, XLW)),
                                      dram("XRD", (NP + P, XLW)))
        g.Z2, g.ALD = dram("Z2", (EP, 2)), dram("ALD", (EP, 2))
        g.SLOW, g.DLOW, g.LSD = dram("SLOW", (EP,), bf16), dram("DLOW", (EP,), bf16), dram("LSD", (EP, 8))
        g.LTD = dram("LTD", (NP, 8))
        g.SCD, g.WD = dram("SCD", (EP, 8)), dram("WD", (EP, 8))
        g.MSD = dram("MSD", (EP, 8))
        with ExitStack() as by_src:
            def by_src_sb(name, shape, dt=f32):
                return by_src.enter_context(nc.sbuf_tensor(name, shape, dt))

            g.os = Order(by_src_sb, "os")
            g.lrel_s, g.dhi_s = by_src_sb("lrel_s", [P, ET]), by_src_sb("dhi_s", [P, ET])
            g.dsts_t, g.base_s = by_src_sb("dsts_t", [P, ET], i32), by_src_sb("base_s", [1, ET], i32)
            with ExitStack() as layer0:
                def layer0_sb(name, shape, dt=f32):
                    return layer0.enter_context(nc.sbuf_tensor(name, shape, dt))

                g.dst_t, g.src_c, g.rank_c, g.dsts_c = (layer0_sb(x, [P, ET], i32)
                                                        for x in ("dst_t_sb", "src_c_sb", "rank_c", "dsts_c"))
                g.shi_c, g.LT = layer0_sb("shi_c", [P, ET]), layer0_sb("LT", [P, NT, 8])
                g.AD = layer0.enter_context(nc.sbuf_tensor("AD", [P, NT, 8], f32))
                g.GAT = layer0.enter_context(nc.sbuf_tensor("GAT", [P, ET, 16], f32))
                run(stage_constants, A)
                run(stage_norm, "n0")
                run(stage_tables0, A)
                run(stage_rank, A)
                g.PD, g.T1, g.T2 = (layer0_sb(x, [P, ET, 8]) for x in ("PD", "T1", "T2"))
                with ExitStack() as own:
                    REC = own.enter_context(nc.sbuf_tensor("REC", [P, ET, NRW], f32))
                    run(stage_edges0, A, REC)
                g.T3 = layer0_sb("T3", [P, ET, 8])
                run(stage_by_src)
                run(stage_messages0)
            run(stage_update0, A)
            run(stage_norm, "n1")
            SN, TN = by_src.enter_context(nc.sbuf_tensor("SN", [P, NT, 2], f32)), \
                by_src.enter_context(nc.sbuf_tensor("TN", [P, NT, 2], f32))
            with ExitStack() as own:
                T = own.enter_context(nc.sbuf_tensor("T_wh", [P, NT, D], f32))
                a = A["L1_gnn_a"]
                run(stage_project, A, "p1", A["L1_gnn_W_w"], A["L1_gnn_W_b"],
                              [[(0, a[0:P]), (P, a[0:P])], [(0, a[P:D]), (P, a[P:D])]], 2, 1.0, T,
                              [SN[:, :, :], TN[:, :, :]], g.WHD[:, :], D)
            pre = by_src.enter_context(nc.sbuf_tensor("pre1", [P, 64, D], f32))
            run(stage_edges1, SN, TN, g.ALD, pre)
            acc = by_src.enter_context(nc.sbuf_tensor("acc1", [P, 2, ACCW], f32))
            run(stage_aggregate, "a1", g.WHD[:, :], D, g.dsts_t, g.lrel_s, g.base_s, acc, g.ALD, 2, pre,
                one_hot_view(g))
            run(stage_update1, acc)
        with ExitStack() as own:
            acc = own.enter_context(nc.sbuf_tensor("acc2", [P, 2, ACCW], f32))
            run(stage_norm, "n2", g.H2D)
            run(stage_aggregate, "a2", g.H2D[:, :], D, g.src_t, g.lrel_d, g.base_d, acc)
            run(stage_update2, A, acc)
        run(stage_norm, "n3")
        att = A["L3_gnn_att"].rearrange("h c -> (h c)")
        with ExitStack() as scores:
          pre = scores.enter_context(nc.sbuf_tensor("pre_scores", [P, SETS * U, XLW], f32))
          with ExitStack() as own:
            T = own.enter_context(nc.sbuf_tensor("T_xl", [P, NT, XLW], f32))
            run(stage_project, A, "p3l", A["L3_gnn_W_l"], A["L3_gnn_b_l"], [[(0, att)]], 8, 0.2, T,
                          [T[:, :, D:XLW]], g.XLD[:, :], XLW)
            run(stage_project, A, "p3r", A["L3_gnn_W_r"], A["L3_gnn_b_r"], [[(0, att)]], 8, 0.2, T,
                          [T[:, :, D:XLW]], g.XRD[0:NP, :], XLW, pre)
            run(stage_border, T)
          run(stage_scores3, A, pre)
        pre = sb("pre3", [P, 64, XLW])
        run(stage_softmax3, A, pre)
        acc = sb("acc3", [P, 2, ACCW])
        run(stage_aggregate, "a3", g.XLD[:, :], XLW, g.src_t, g.lrel_d, g.base_d, acc, g.WD, 8, pre,
            one_hot_view(g))
        run(stage_output, A, acc, out)


def kernel(**inputs):
    import numpy as _np
    import concourse.bacc as _bacc
    from concourse import mybir as _mybir
    from concourse.bass_utils import run_bass_kernel_spmd as _run

    def edges(a, fill):
        padded = _np.full((EP,) + a.shape[1:], fill, a.dtype)
        padded[:NE] = a
        return padded

    src, dst = edges(_np.asarray(inputs["src"]), NP - 1), edges(_np.asarray(inputs["dst"]), NP - 1)
    bordered = _np.concatenate([_np.full(1, -1, dst.dtype), dst, _np.full(1, NP, dst.dtype)])
    x = _np.zeros((NP, D), _np.float32)
    x[:NN] = inputs["x"]
    laid = {
        "x": x,
        "src_t": src.reshape(ET, P).T, "dst_t": dst.reshape(ET, P).T,
        "src_c": src.reshape(P, ET), "dst_c": _np.stack([bordered[ET * p:ET * p + ET + 2] for p in range(P)]),
        "src_row": src, "dst_row": dst,
        "attr": edges(_np.asarray(inputs["edge_attr_16"]), 0).reshape(P, ET // 8, P).transpose(1, 2, 0),
        "ew": edges(_np.asarray(inputs["edge_weight"]), 1).reshape(P, ET),
    }
    for name, a in inputs.items():
        if name.startswith("L"):
            a = _np.asarray(a)
            laid[name] = a.T if name in ("L2_gnn_W_neigh", "L2_gnn_W_self") else a
    nc = _bacc.Bacc("TRN2", target_bir_lowering=False, num_devices=1)
    arrays, args = {}, {}
    for name, a in laid.items():
        a = _np.ascontiguousarray(a)
        arrays[f"in_{name}_dram"] = a
        args[name] = nc.dram_tensor(f"in_{name}_dram", a.shape, _mybir.dt.from_np(a.dtype),
                                    kind="ExternalInput").ap()
    out = nc.dram_tensor("out_0_dram", (NP, D), _mybir.dt.float32, kind="ExternalOutput").ap()
    build(nc, args, out)
    r = _run(nc, [arrays], core_ids=[0])
    return r.results[0]["out_0_dram"][:NN]
```

```python
import concourse.bass as bass
from concourse import mybir
from contextlib import ExitStack

P = 128
NN = 3125
NE = 53125
D = 256
NT = -(-NN // P)
NP = NT * P
ET = -(-NE // (32 * P)) * 32
EP = ET * P
CU = 16
CI = ET // (2 * CU)
U = 8
SETS = 4
WI = ET // (SETS * U)
PRE_AT = (0, WI // 2)
PRE_SCORES = WI // 2
RU = 8
RI = ET // (2 * RU)
LOOKED = 17 * 2 * RU
ACCW = NP + P
TQ = ET // 4
NRW = 10
BIG = 1.0e30
LN_EPS = 1e-5
XLW = D + 8

f32 = mybir.dt.float32
bf16 = mybir.dt.bfloat16
i32 = mybir.dt.int32
ALU = mybir.AluOpType
ACT = mybir.ActivationFunctionType
AX = mybir.AxisListType
IOA = bass.IndirectOffsetOnAxis


class Link:

    def __init__(self, eng, sem):
        self.eng, self.sem, self.n = eng, sem, 0

    def __call__(self, ins):
        ins.then_inc(self.sem, 1)
        self.n += 1
        self.eng.wait_ge(self.sem, self.n)


class Env:
    pass


def bc_mid(ap, n):
    return ap[:, None, :].to_broadcast([ap.shape[0], n, ap.shape[1]])


def bc_last(ap, n):
    return ap[:, :, None].to_broadcast([ap.shape[0], ap.shape[1], n])


def one_hot_view(g):
    return g.HT[:, :, :].rearrange("p h n -> p (h n)")[:, 0:SETS * U * P]\
        .rearrange("p (s i f) -> p s i f", s=SETS, f=P)


def bc_row(ap, n=P):
    return ap[None, :].to_broadcast([n, ap.shape[0]])



def stage_constants(nc, env, A):
    g = env
    ready, zero, zeroed = g.sem("const_ready"), g.sem("const_zero"), g.sem("const_zeroed")
    none = g.HT[:, :, :].rearrange("p h n -> p (h n)")
    loaded = g.sem("index_loaded")
    with nc.Block() as block:
        @block.gpsimd
        def _(e):
            e.iota(g.iota_row[:, :], [[1, P]], base=0, channel_multiplier=0,
                   allow_small_or_imprecise_dtypes=True)
            e.iota(g.iota_p[:, :], [[0, 1]], base=0, channel_multiplier=1,
                   allow_small_or_imprecise_dtypes=True)
            e.memset(g.ones[:, :], 1.0)
            e.memset(g.ident[:, :], 0.0).then_inc(ready, 1)
            e.wait_ge(ready, 1)
            e.affine_select(out=g.ident[:, :], in_=g.ident[:, :], compare_op=ALU.not_equal, fill=1.0,
                            base=0, pattern=[[-1, P]], channel_multiplier=1)
            e.affine_select(out=g.before[:, :], in_=g.ones[:, :], compare_op=ALU.is_ge, fill=0.0,
                            base=-1, pattern=[[-1, P]], channel_multiplier=1)
            e.affine_select(out=g.after[:, :], in_=g.ones[:, :], compare_op=ALU.is_ge, fill=0.0,
                            base=-1, pattern=[[1, P]], channel_multiplier=-1).then_inc(ready, 1)

        @block.vector
        def _(e):
            e.memset(none[:, 0:8 * ET], 0.0).then_inc(zero, 1)

        @block.scalar
        def _(e):
            e.wait_ge(zero, 1)
            e.dma_start(g.Z8.rearrange("(p j) w -> p (j w)", j=ET), none[:, 0:8 * ET]).then_inc(zeroed, 16)
            e.dma_start(g.Z2.rearrange("(p j) w -> p (j w)", j=ET), none[:, 0:2 * ET]).then_inc(zeroed, 16)
            e.dma_start(g.XRD[NP:NP + P, :], none[:, 0:XLW]).then_inc(zeroed, 16)
            e.wait_ge(zeroed, 48)

        @block.sync
        def _(e):
            e.dma_start(g.X[:, :, :], A["x"].rearrange("(j p) d -> p j d", p=P)).then_inc(loaded, 16)
            e.dma_start(g.src_t[:, :], A["src_t"][:, :]).then_inc(loaded, 16)
            e.dma_start(g.dst_t[:, :], A["dst_t"][:, :]).then_inc(loaded, 16)
            e.dma_start(g.src_c[:, :], A["src_c"][:, :]).then_inc(loaded, 16)
            e.wait_ge(loaded, 64)



class Norm:

    def __init__(self, nc, g, own, name, rows=None):
        self.g, self.rows = g, rows
        (self.moments, self.root, self.linked, self.h_ready, self.flipped, self.kept, self.stored) = (
            g.sem(name + x) for x in ("_moments", "_root", "_linked", "_h_ready", "_flipped", "_kept", "_stored"))
        self.H = own.enter_context(nc.sbuf_tensor(name + "_H", [P, NT, D], f32))
        self.stats = own.enter_context(nc.sbuf_tensor(name + "_stats", [P, NT, 6], f32))
        self.mv = own.enter_context(nc.sbuf_tensor(name + "_mv", [P, NT, 2], f32))
        self.rstd = own.enter_context(nc.sbuf_tensor(name + "_rstd", [P, NT], f32))
        self.shift = own.enter_context(nc.sbuf_tensor(name + "_shift", [P, NT], f32))

    def vector(self, e):
        g, stats, mv, rstd, shift = self.g, self.stats, self.mv, self.rstd, self.shift
        link = Link(e, self.linked)
        for j in range(NT - 1):
            e.bn_stats(stats[:, j, :], g.X[:, j, :])
        link(e.bn_stats(stats[:, NT - 1, :], g.X[:, NT - 1, :]))
        for j in range(NT - 1):
            e.bn_aggr(mv[:, j, :], stats[:, j, :])
        link(e.bn_aggr(mv[:, NT - 1, :], stats[:, NT - 1, :]))
        e.tensor_scalar(rstd[:, :], mv[:, :, 1], LN_EPS, None, ALU.add).then_inc(self.moments, 1)
        e.wait_ge(self.root, 1)
        link(e.reciprocal(rstd[:, :], rstd[:, :]))
        e.scalar_tensor_tensor(shift[:, :], mv[:, :, 0], -1.0, rstd[:, :], ALU.mult, ALU.mult)\
            .then_inc(self.moments, 1)
        for j in range(NT):
            e.wait_ge(self.flipped, j + 1)
            e.tensor_copy(g.HT[:, :, j * P:(j + 1) * P],
                          g.ps[j % 4][:, 0:D].rearrange("p (h n) -> p h n", h=2)).then_inc(self.kept, 1)

    def scalar(self, e):
        e.wait_ge(self.moments, 1)
        e.activation(self.rstd[:, :], self.rstd[:, :], ACT.Sqrt).then_inc(self.root, 1)
        e.wait_ge(self.moments, 2)
        for j in range(NT):
            e.activation(self.H[:, j, :], self.g.X[:, j, :], ACT.Relu, bias=self.shift[:, j:j + 1],
                         scale=self.rstd[:, j:j + 1]).then_inc(self.h_ready, 1)

    def tensor(self, e):
        g = self.g
        for j in range(NT):
            e.wait_ge(self.h_ready, j + 1)
            if j >= 4:
                e.wait_ge(self.kept, j - 3)
            e.transpose(g.ps[j % 4][:, 0:P], self.H[:, j, 0:P], g.ident[:, :])
            e.transpose(g.ps[j % 4][:, P:D], self.H[:, j, P:D], g.ident[:, :]).then_inc(self.flipped, 1)

    def sync(self, e):
        if self.rows is not None:
            e.wait_ge(self.h_ready, NT)
            e.dma_start(self.rows.rearrange("(j p) d -> p j d", p=P), self.H[:, :, :]).then_inc(self.stored, 16)
            e.wait_ge(self.stored, 16)


def stage_tables0(nc, env, A):
    g = env
    loaded, product, kept, stored = (g.sem("t0_loaded"), g.sem("t0_product"), g.sem("t0_kept"),
                                     g.sem("t0_stored"))
    with ExitStack() as own:
        W = own.enter_context(nc.sbuf_tensor("t0_W", [P, 2, 24], f32))
        T = own.enter_context(nc.sbuf_tensor("t0_T", [P, NT, 16], f32))
        norm = Norm(nc, g, own, "n0")
        with nc.Block() as block:
            @block.sync
            def _(e):
                for n, name in enumerate(("L0_gnn_W_attn_src", "L0_gnn_W_prop_src", "L0_gnn_W_attn_dst")):
                    e.dma_start(W[:, :, 8 * n:8 * n + 8],
                                A[name].rearrange("(h p) m -> p h m", p=P)).then_inc(loaded, 16)
                e.wait_ge(kept, NT)
                e.dma_start(g.T0.rearrange("(j p) w -> p j w", p=P), T[:, :, :]).then_inc(stored, 16)
                e.wait_ge(stored, 16)

            @block.tensor
            def _(e):
                norm.tensor(e)
                e.wait_ge(loaded, 48)
                for j in range(NT):
                    e.wait_ge(norm.kept, j + 1)
                    if j >= 4:
                        e.wait_ge(kept, j - 3)
                    for h in range(2):
                        m = e.matmul(g.ps[4 + j % 4][:, 0:24], lhsT=g.HT[:, h, j * P:(j + 1) * P], rhs=W[:, h, :],
                                     start=h == 0, stop=h == 1)
                    m.then_inc(product, 1)

            @block.vector
            def _(e):
                norm.vector(e)

            @block.scalar
            def _(e):
                norm.scalar(e)
                for j in range(NT):
                    e.wait_ge(product, j + 1)
                    e.activation(T[:, j, :], g.ps[4 + j % 4][:, 0:16], ACT.Copy)
                    e.activation(g.AD[:, j, :], g.ps[4 + j % 4][:, 16:24], ACT.Copy).then_inc(kept, 1)



class Narrow:

    def __init__(self, g, nc, own, name, w):
        self.idx = own.enter_context(nc.sbuf_tensor(name + "_idx", [P, 2, CU], i32))
        self.rows = own.enter_context(nc.sbuf_tensor(name + "_rows", [P, 2, CU, w], f32))
        self.landed = [g.sem(f"{name}_landed{s}") for s in range(2)]
        self.staged, self.seen = g.sem(name + "_staged"), g.sem(name + "_seen")
        self.collected = g.sem(name + "_collected")


def pool_gather(e, n, index, table, out):

    def issue(turn, s):
        at = turn * (2 * CU) + s * CU
        e.tensor_copy(n.idx[:, s, :], index[:, bass.ds(at, CU)]).then_inc(n.staged, 1)
        e.wait_ge(n.staged, turn * 2 + (s + 1))
        e.sem_inc(n.seen, 1)
        for c in range(CU):
            e.indirect_dma_start(out=n.rows[:, s, c, :], out_offset=None, in_=table,
                                 in_offset=IOA(ap=n.idx[:, s, c:c + 1], axis=0)).then_inc(n.landed[s], 16)

    def collect(turn, s):
        at = turn * (2 * CU) + s * CU
        e.wait_ge(n.landed[s], turn * (16 * CU) + 16 * CU)
        e.tensor_copy(out[:, bass.ds(at, CU), :], n.rows[:, s, :, :]).then_inc(n.collected, 1)
        e.wait_ge(n.collected, turn * 2 + (s + 1))
        e.sem_inc(n.seen, 1)

    issue(0, 0)
    with e.Fori(0, CI - 1) as k:
        issue(k, 1)
        collect(k, 0)
        issue(k + 1, 0)
        collect(k, 1)
    issue(CI - 1, 1)
    collect(CI - 1, 0)
    collect(CI - 1, 1)


def pool_scatter(e, n, index, rows, table):

    def issue(turn, s):
        at = turn * (2 * CU) + s * CU
        e.tensor_copy(n.idx[:, s, :], index[:, bass.ds(at, CU)])
        e.tensor_copy(n.rows[:, s, :, :], rows[:, bass.ds(at, CU), :]).then_inc(n.staged, 1)
        e.wait_ge(n.staged, turn * 2 + (s + 1))
        e.sem_inc(n.seen, 1)
        for c in range(CU):
            e.indirect_dma_start(out=table, out_offset=IOA(ap=n.idx[:, s, c:c + 1], axis=0),
                                 in_=n.rows[:, s, c, :], in_offset=None).then_inc(n.landed[s], 16)

    issue(0, 0)
    issue(0, 1)
    with e.Fori(0, CI - 1) as k:
        for s in range(2):
            e.wait_ge(n.landed[s], k * (16 * CU) + 16 * CU)
            issue(k + 1, s)
    for s in range(2):
        e.wait_ge(n.landed[s], 16 * CU * CI)



def stage_rank(nc, env, A):
    g = env
    sem = g.sem
    linked, digits = sem("rk_linked"), sem("rk_digits")
    hot = [sem(f"rk_hot{s}") for s in range(2)]
    counted, count_kept, zero_ready = sem("rk_counted"), sem("rk_count_kept"), sem("rk_zero")
    picked = sem("rk_picked")
    deg_ready, prefixed, starts = sem("rk_deg_ready"), sem("rk_prefixed"), sem("rk_starts")
    row_in = [sem(f"rk_row_in{s}") for s in range(2)]
    row_free = [sem(f"rk_row_free{s}") for s in range(2)]
    base_in = [sem(f"rk_base_in{s}") for s in range(2)]
    base_free = [sem(f"rk_base_free{s}") for s in range(2)]
    onehot_t, looked, looked_free = sem("rk_onehot_t"), sem("rk_looked"), sem("rk_looked_free")
    ranked, turned, out_ready, stored, back = (sem("rk_ranked"), sem("rk_turned"), sem("rk_out_ready"),
                                               sem("rk_stored"), sem("rk_back"))
    with ExitStack() as own:
        def sb(n, shape, dt=f32):
            return own.enter_context(nc.sbuf_tensor("rk_" + n, shape, dt))
        n = Narrow(g, nc, own, "g0", 16)
        di = g.dsts_c
        slo, shi, dlo, dhi = g.od.fm, g.od.fneg, g.od.last, g.od.gm
        junk = sb("junk", [P, RU * P], bf16)
        onehots = sb("onehots", [P, 4 * RU * P], bf16)
        hot4 = onehots[:, :].rearrange("p (o s i f) -> p o s i f", o=2, s=2, f=P)
        hlo, glo = hot4[:, 0], hot4[:, 1]
        hhi = sb("hhi", [P, 2, RU, NT], bf16)
        ghi = sb("ghi", [P, 2, RU, NT], bf16)
        cnt = sb("cnt", [P, NT, ET], bf16)
        upto = sb("upto", [P, NT, ET])
        unit = g.os.fm
        tot = sb("tot", [P, 2, NT])
        run = sb("run", [P, 2, NT])
        row = sb("row", [P, 2, RU * P], i32)
        rlo = sb("rlo", [P, RU * P], i32)
        base = g.win_d[:, 0:2 * RU * NT].rearrange("p (s i c) -> p s i c", s=2, c=NT)
        srcf = g.lrel_s
        match = junk[:, :].rearrange("p (i f) -> p i f", f=P)
        look = g.shi_c[:, 0:RU * NT].rearrange("p (i c) -> p i c", c=NT)
        r2 = sb("r2", [P, 2, RU])
        zero = g.dhi_s[:, 0:P // 2].bitcast(bf16)
        r1 = sb("r1", [P, RU])
        rank = g.os.fneg
        oht = onehots[:, :].bitcast(f32).rearrange("p (s i f) -> p s i f", s=2, f=P)
        out = rlo[0:TQ, 0:4 * P].rearrange("q (i f) -> q i f", f=P)
        with nc.Block() as block:
            @block.gpsimd
            def _(e):
                pool_gather(e, n, g.src_c, g.T0[:, :], g.GAT)

            @block.sync
            def _(e):
                for s in range(2):
                    e.dma_start(row[:, s, :], bc_row(A["src_row"][s * RU * P:(s + 1) * RU * P]))\
                        .then_inc(row_in[s], 16)
                with e.Fori(0, RI - 1) as k:
                    for s in range(2):
                        e.wait_ge(row_free[s], k + 1)
                        e.dma_start(row[:, s, :],
                                    bc_row(A["src_row"][bass.ds(k * (2 * RU * P) + (2 + s) * RU * P, RU * P)]))\
                            .then_inc(row_in[s], 16)
                e.wait_ge(out_ready, 4)
                e.dma_start(g.RKF.rearrange("(i q p) -> q i p", i=4, p=P), out[:, :, :]).then_inc(stored, 16)
                e.wait_ge(stored, 16)
                e.dma_start(g.rank_c[:, :], g.RKF.rearrange("(p j) -> p j", j=ET)).then_inc(back, 16)
                e.wait_ge(back, 16)

            @block.scalar
            def _(e):
                with e.Fori(0, RI) as k:
                    for s in range(2):
                        e.wait_ge(counted, k * 2 + (s + 1))
                        e.activation(cnt[:, :, bass.ds(k * (2 * RU) + s * RU, RU)],
                                     g.ps[s][:, 0:RU * NT].rearrange("p (i c) -> p c i", c=NT), ACT.Copy)\
                            .then_inc(count_kept, 1)
                e.wait_ge(starts, 1)
                with e.Fori(0, RI) as k:
                    for s in range(2):
                        e.wait_ge(base_free[s], k + 1)
                        e.activation(base[:, s, :, :],
                                     upto[:, :, bass.ds(k * (2 * RU) + s * RU, RU)].rearrange("p c i -> p i c"),
                                     ACT.Copy).then_inc(base_in[s], 1)

            @block.vector
            def _(e):
                link = Link(e, linked)
                for src, lo, hi in ((g.src_t, slo, shi), (g.dst_t, dlo, dhi)):
                    link(e.tensor_single_scalar(di[:, :], src[:, :], P - 1, ALU.bitwise_and))
                    link(e.tensor_copy(lo[:, :], di[:, :]))
                    link(e.tensor_single_scalar(di[:, :], src[:, :], 7, ALU.arith_shift_right))
                    link(e.tensor_copy(hi[:, :], di[:, :]))
                e.memset(unit[:, :], 1.0)
                e.memset(zero[:, :], 0.0)
                link(e.tensor_copy(srcf[:, :], g.src_t[:, :]))
                e.sem_inc(zero_ready, 1)
                with e.Fori(0, RI) as k:
                    for s in range(2):
                        at = bass.ds(k * (2 * RU) + s * RU, RU)
                        e.wait_ge(digits, k * 2 + (s + 1))
                        e.tensor_tensor(hlo[:, s, :, :], bc_mid(g.iota_row[:, :], RU), bc_last(slo[:, at], P),
                                        ALU.is_equal)
                        e.tensor_tensor(hhi[:, s, :, :], bc_mid(g.iota_row[:, 0:NT], RU),
                                        bc_last(shi[:, at], NT), ALU.is_equal)
                        e.tensor_tensor(glo[:, s, :, :], bc_mid(g.iota_row[:, :], RU), bc_last(dlo[:, at], P),
                                        ALU.is_equal)
                        e.tensor_tensor(ghi[:, s, :, :], bc_mid(g.iota_row[:, 0:NT], RU),
                                        bc_last(dhi[:, at], NT), ALU.is_equal).then_inc(hot[s], 1)
                e.wait_ge(count_kept, 2 * RI + 2)
                e.wait_ge(counted, 2 * RI + 1)
                link(e.tensor_copy(g.deg_d[:, :], g.ps[4][:, 0:NT]))
                for c in range(NT - 1):
                    e.tensor_tensor_scan(upto[:, c, :], unit[:, :], cnt[:, c, :], 0.0, ALU.mult, ALU.add)
                link(e.tensor_tensor_scan(upto[:, NT - 1, :], unit[:, :], cnt[:, NT - 1, :], 0.0,
                                          ALU.mult, ALU.add))
                link(e.tensor_copy(g.deg_s[:, :], upto[:, :, ET - 1]))
                link(e.tensor_tensor(upto[:, :, :], upto[:, :, :], cnt[:, :, :], ALU.subtract))
                e.sem_inc(deg_ready, 1)
                e.wait_ge(prefixed, 1)
                for o, start in ((0, g.start_s), (1, g.start_d)):
                    link(e.tensor_copy(tot[:, o, :], g.ps[5][:, (2 * o + 1) * NT:(2 * o + 2) * NT]))
                    link(e.tensor_tensor_scan(run[:, o, :], unit[:, 0:NT], tot[:, o, :], 0.0, ALU.mult, ALU.add))
                    link(e.tensor_tensor(run[:, o, :], run[:, o, :], tot[:, o, :], ALU.subtract))
                    link(e.tensor_tensor(start[:, :], run[:, o, :], g.ps[5][:, 2 * o * NT:(2 * o + 1) * NT],
                                         ALU.add))
                link(e.tensor_tensor(upto[:, :, :], upto[:, :, :], bc_last(g.start_s[:, :], ET), ALU.add))
                e.sem_inc(starts, 1)
                for s in range(2):
                    e.sem_inc(base_free[s], 1)

                def prepare(k, s):
                    at = bass.ds(k * (2 * RU) + s * RU, RU)
                    e.wait_ge(row_in[s], k * 16 + 16)
                    e.tensor_single_scalar(rlo[:, :], row[:, s, :], P - 1, ALU.bitwise_and).then_inc(ranked, 1)
                    for i in range(RU):
                        ins = e.scalar_tensor_tensor(match[:, i, :], row[:, s, i * P:(i + 1) * P],
                                                     srcf[:, bass.ds(k * (2 * RU) + (s * RU + i), 1)],
                                                     g.before[:, :], ALU.is_equal, ALU.mult,
                                                     accum_out=r2[:, s, i:i + 1])
                    ins.then_inc(ranked, 1)
                    e.tensor_tensor(hhi[:, s, :, :], bc_mid(g.iota_row[:, 0:NT], RU), bc_last(shi[:, at], NT),
                                    ALU.is_equal)
                    e.wait_ge(ranked, k * 4 + (2 * s + 2))
                    e.tensor_scalar(oht[:, s, :, :].rearrange("p i f -> p (i f)"), rlo[:, :], g.iota_p[:, 0:1],
                                    None, ALU.is_equal).then_inc(onehot_t, 1)
                    e.wait_ge(onehot_t, k * 2 + (s + 1))
                    e.sem_inc(row_free[s], 1)

                def finish(k, s):
                    at = bass.ds(k * (2 * RU) + s * RU, RU)
                    e.wait_ge(looked, k * 2 + (s + 1))
                    e.tensor_tensor(look[:, :, :], g.ps[s][:, 0:RU * NT].rearrange("p (i c) -> p i c", c=NT),
                                    hhi[:, s, :, :], ALU.mult).then_inc(picked, 1)
                    e.wait_ge(picked, k * 4 + (2 * s + 1))
                    e.sem_inc(base_free[s], 1)
                    e.tensor_reduce(r1[:, :], look[:, :, :], AX.X, ALU.add).then_inc(picked, 1)
                    e.wait_ge(picked, k * 4 + (2 * s + 2))
                    e.scalar_tensor_tensor(rank[:, at], r1[:, :], 1.0, r2[:, s, :], ALU.add, ALU.add)\
                        .then_inc(looked_free, 1)
                    e.wait_ge(looked_free, k * 2 + (s + 1))

                prepare(0, 0)
                prepare(0, 1)
                with e.Fori(0, RI - 1) as k:
                    for s in range(2):
                        finish(k, s)
                        prepare(k + 1, s)
                finish(RI - 1, 0)
                finish(RI - 1, 1)
                e.wait_ge(looked_free, 2 * RI)
                for i in range(4):
                    e.wait_ge(turned, i + 1)
                    e.tensor_copy(out[:, i, :], g.ps[i][0:TQ, 0:P]).then_inc(out_ready, 1)
                e.wait_ge(out_ready, 4)

            @block.tensor
            def _(e):
                for s in range(2):
                    e.sem_inc(digits, 1)
                for s in range(2):
                    e.sem_inc(count_kept, 1)
                e.wait_ge(zero_ready, 1)
                e.matmul(g.ps[4][:, 0:NT], lhsT=zero[:, :], rhs=zero[:, 0:NT], start=True, stop=False)
                with e.Fori(0, RI) as k:
                    for s in range(2):
                        e.wait_ge(hot[s], k + 1)
                        e.wait_ge(count_kept, k * 2 + (s + 1))
                        for i in range(RU):
                            e.matmul(g.ps[s][:, i * NT:(i + 1) * NT], lhsT=hlo[:, s, i, :], rhs=hhi[:, s, i, :],
                                     start=True, stop=True)
                        for i in range(RU):
                            m = e.matmul(g.ps[4][:, 0:NT], lhsT=glo[:, s, i, :], rhs=ghi[:, s, i, :],
                                         start=False, stop=False)
                        m.then_inc(counted, 1)
                        e.wait_ge(counted, k * 2 + (s + 1))
                        e.sem_inc(digits, 1)
                e.matmul(g.ps[4][:, 0:NT], lhsT=zero[:, :], rhs=zero[:, 0:NT], start=False, stop=True)\
                    .then_inc(counted, 1)
                e.wait_ge(deg_ready, 1)
                for o, deg in ((0, g.deg_s), (1, g.deg_d)):
                    e.matmul(g.ps[5][:, 2 * o * NT:(2 * o + 1) * NT], lhsT=g.after[:, :], rhs=deg[:, :],
                             start=True, stop=True)
                    m = e.matmul(g.ps[5][:, (2 * o + 1) * NT:(2 * o + 2) * NT], lhsT=g.ones[:, :], rhs=deg[:, :],
                                 start=True, stop=True)
                m.then_inc(prefixed, 1)
                with e.Fori(0, RI) as k:
                    for s in range(2):
                        e.wait_ge(onehot_t, k * 2 + (s + 1))
                        e.wait_ge(base_in[s], k + 1)
                        for i in range(RU):
                            m = e.matmul(g.ps[s][:, i * NT:(i + 1) * NT], lhsT=oht[:, s, i, :],
                                         rhs=base[:, s, i, :], start=True, stop=True)
                        m.then_inc(looked, 1)
                e.wait_ge(looked_free, 2 * RI)
                for i in range(4):
                    e.transpose(g.ps[i][0:TQ, 0:P], rank[:, i * TQ:(i + 1) * TQ], g.ident[:, :])\
                        .then_inc(turned, 1)



class Order:

    def __init__(self, sb, name):
        self.fm, self.fneg, self.last, self.gm = (sb(f"{name}_{x}", [P, ET]) for x in ("fm", "fneg", "last", "gm"))
        self.fmT, self.fnegT, self.gmT = (sb(f"{name}_{x}", [8, P]) for x in ("fmT", "fnegT", "gmT"))


class Asks:

    def __init__(self, e, asked, answered):
        self.e, self.asked, self.answered, self.n = e, asked, answered, 0

    def __call__(self):
        self.e.sem_inc(self.asked, 1)
        self.n += 1
        self.e.wait_ge(self.answered, self.n)


def tensor_flips(e, g, asked, answered, kinds):
    for n, (kind, w) in enumerate(kinds):
        e.wait_ge(asked, n + 1)
        if kind == "in":
            e.transpose(g.ps[6][0:w, 0:P], g.flip_in[:, 0:w], g.ident[:, :]).then_inc(answered, 1)
        else:
            e.transpose(g.ps[7][:, 0:w], g.flip_ex[0:w, 1:P + 1], g.ident[0:w, 0:w]).then_inc(answered, 1)


ORDER_FLIPS = [("in", 8)] * 3


def scan_flips(w, scans):
    return [("in", w), ("ex", w)] * scans


def order_masks(e, g, link, flip, o, key, any_):
    link(e.tensor_tensor(o.last[:, :], key[:, 1:ET + 1], key[:, 2:ET + 2], ALU.not_equal))
    link(e.tensor_tensor(o.fneg[:, :], key[:, 1:ET + 1], key[:, 0:ET], ALU.not_equal))
    link(e.tensor_scalar(o.fm[:, :], o.fneg[:, :], -1.0, 1.0, ALU.mult, ALU.add))
    link(e.tensor_scalar(o.gm[:, :], o.last[:, :], -1.0, 1.0, ALU.mult, ALU.add))
    link(e.tensor_single_scalar(o.fneg[:, :], o.fneg[:, :], -BIG, ALU.mult))
    for mask, row in ((o.fm, o.fmT), (o.fneg, o.fnegT), (o.gm, o.gmT)):
        link(e.tensor_reduce(any_[:, :], mask[:, :], AX.X, ALU.min))
        link(e.tensor_copy(g.flip_in[:, 0:8], any_[:, 0:1].to_broadcast([P, 8])))
        flip()
        link(e.tensor_copy(row[:, :], g.ps[6][0:8, 0:P]))


def seg_scan(e, g, link, flip, w, backward, op0, op1, mask, mask_row, neutral, data, out, carry):

    def rows(first):
        for h in range(w):
            step = slice(None, None, -1) if backward else slice(None)
            ins = e.tensor_tensor_scan(out[:, step, h], mask[:, step], data[:, step, h],
                                       neutral if first else carry[:, h:h + 1], op0, op1)
            if h == w - 1:
                link(ins)

    rows(True)
    link(e.tensor_copy(g.flip_in[:, 0:w], out[:, 0 if backward else ET - 1, 0:w]))
    flip()
    if backward:
        e.memset(g.flip_ex[0:w, P:P + 1], neutral)
        link(e.tensor_tensor_scan(g.flip_ex[0:w, 0:P][:, ::-1], mask_row[0:w, ::-1],
                                  g.ps[6][0:w, 0:P][:, ::-1], neutral, op0, op1))
    else:
        link(e.tensor_tensor_scan(g.flip_ex[0:w, 2:P + 2], mask_row[0:w, :], g.ps[6][0:w, 0:P], neutral,
                                  op0, op1))
        link(e.memset(g.flip_ex[0:w, 1:2], neutral))
    flip()
    link(e.tensor_copy(carry[:, 0:w], g.ps[7][:, 0:w]))
    rows(False)


def seg_softmax(e, g, link, flip, exp, w, o, S, M, V, carry, weight=None, eps=None):
    seg_scan(e, g, link, flip, w, False, ALU.add, ALU.max, o.fneg, o.fnegT, -BIG, S if weight is None else V,
             M, carry)
    link(e.tensor_tensor(V[:, :, :], M[:, :, :], bc_last(o.last[:, :], w), ALU.mult))
    seg_scan(e, g, link, flip, w, True, ALU.mult, ALU.add, o.gm, o.gmT, 0.0, V, M, carry)
    link(e.tensor_tensor(S[:, :, :], S[:, :, :], M[:, :, :], ALU.subtract))
    exp()
    if weight is not None:
        link(e.tensor_tensor(S[:, :, :], S[:, :, :], bc_last(weight, w), ALU.mult))
    seg_scan(e, g, link, flip, w, False, ALU.mult, ALU.add, o.fm, o.fmT, 0.0, S, M, carry)
    link(e.tensor_tensor(V[:, :, :], M[:, :, :], bc_last(o.last[:, :], w), ALU.mult))
    seg_scan(e, g, link, flip, w, True, ALU.mult, ALU.add, o.gm, o.gmT, 0.0, V, M, carry)
    if eps is not None:
        link(e.tensor_single_scalar(M[:, :, :], M[:, :, :], eps, ALU.add))
    link(e.reciprocal(M[:, :, :], M[:, :, :]))
    link(e.tensor_tensor(S[:, :, :], S[:, :, :], M[:, :, :], ALU.mult))



class Ahead:

    def __init__(self, nc, g, own, name, columns):
        self.columns = columns
        self.staged, self.seen, self.landed = (g.sem(name + x) for x in ("_pre_staged", "_pre_seen", "_pre_landed"))
        self.idx = own.enter_context(nc.sbuf_tensor(name + "_pre_idx", [P, columns], i32))

    def gather(self, e, index, table, rows):
        at = 0
        for part in index:
            e.tensor_copy(self.idx[:, at:at + part.shape[1]], part).then_inc(self.staged, 1)
            at += part.shape[1]
        e.wait_ge(self.staged, len(index))
        e.sem_inc(self.seen, 1)
        for c in range(self.columns):
            e.indirect_dma_start(out=rows[:, c, :], out_offset=None, in_=table,
                                 in_offset=IOA(ap=self.idx[:, c:c + 1], axis=0)).then_inc(self.landed, 16)
        e.wait_ge(self.landed, 16 * self.columns)


class Lookup:

    def __init__(self, g, sb, name, w, turns=RI):
        self.turns = turns
        self.w, self.per = w, 8 if w <= 2 else 2
        self.banks = RU // self.per
        self.parts = sb(name + "_parts", [P, 3, w, NT], bf16)
        self.rest = sb(name + "_rest", [P, w, NT])
        self.row = sb(name + "_row", [P, 2, RU * P], bf16)
        self.hot = sb(name + "_hot", [P, 2, RU * P], bf16)
        self.high = sb(name + "_high", [P, 2, RU, NT])
        self.picked = sb(name + "_picked", [P, RU, w, NT])
        self.split = g.sem(name + "_split")
        self.row_in, self.hot_ready, self.high_ready, self.looked, self.masked, self.read = (
            [g.sem(f"{name}_{x}{s}") for s in range(2)] for x in ("row_in", "hot", "high", "looked", "masked", "read"))

    def load_rows(self, e, digits):
        for s in range(2):
            e.dma_start(self.row[:, s, :], bc_row(digits[s * RU * P:(s + 1) * RU * P])).then_inc(self.row_in[s], 16)
        with e.Fori(0, self.turns - 1) as k:
            for s in range(2):
                e.wait_ge(self.hot_ready[s], k + 1)
                e.dma_start(self.row[:, s, :],
                            bc_row(digits[bass.ds(k * (2 * RU * P) + (2 + s) * RU * P, RU * P)]))\
                    .then_inc(self.row_in[s], 16)

    def split_table(self, e, link, table):
        t = table.rearrange("p c w -> p w c")
        link(e.tensor_copy(self.parts[:, 0], t))
        link(e.tensor_tensor(self.rest[:, :, :], t, self.parts[:, 0], ALU.subtract))
        link(e.tensor_copy(self.parts[:, 1], self.rest[:, :, :]))
        link(e.tensor_tensor(self.rest[:, :, :], self.rest[:, :, :], self.parts[:, 1], ALU.subtract))
        link(e.tensor_copy(self.parts[:, 2], self.rest[:, :, :]))
        e.sem_inc(self.split, 1)

    def vector(self, e, g, high, out):

        def make_hot(k, s):
            e.wait_ge(self.row_in[s], k * 16 + 16)
            e.wait_ge(self.looked[s], k + 1)
            e.tensor_scalar(self.hot[:, s, :], self.row[:, s, :], g.iota_p[:, 0:1], None, ALU.is_equal)\
                .then_inc(self.hot_ready[s], 1)

        def make_high(k, s):
            at = bass.ds(k * (2 * RU) + s * RU, RU)
            e.tensor_tensor(self.high[:, s, :, :], bc_mid(g.iota_row[:, 0:NT], RU), bc_last(high[:, at], NT),
                            ALU.is_equal).then_inc(self.high_ready[s], 1)

        def finish(k, s, more=True):
            e.wait_ge(self.looked[s], k + 2)
            e.wait_ge(self.high_ready[s], k + 1)
            e.wait_ge(self.masked[1 - s], k * 2 + (1 + s))
            for b in range(self.banks):
                t = slice(b * self.per, (b + 1) * self.per)
                ps = g.ps[s * 4 + b][:, 0:self.per * self.w * NT].rearrange("p (i w c) -> p i w c", w=self.w, c=NT)
                h = self.high[:, s, t, :][:, :, None, :].to_broadcast([P, self.per, self.w, NT])
                ins = e.tensor_tensor(self.picked[:, t, :, :], ps, h, ALU.mult)
            ins.then_inc(self.masked[s], 1)
            if more:
                make_hot(k + 1, s)
            e.wait_ge(self.masked[s], k * 2 + (2 if s else 1))
            e.sem_inc(self.read[s], 1)
            e.tensor_reduce(out[:, bass.ds(k * (2 * RU) + s * RU, RU), :], self.picked[:, :, :, :], AX.X, ALU.add)\
                .then_inc(self.masked[s], 1)
            if more:
                make_high(k + 1, s)

        e.sem_inc(self.masked[1], 1)
        for s in range(2):
            e.sem_inc(self.looked[s], 1)
            e.sem_inc(self.read[s], 1)
        for s in range(2):
            make_hot(0, s)
            make_high(0, s)
        with e.Fori(0, self.turns - 1) as k:
            for s in range(2):
                finish(k, s)
        finish(self.turns - 1, 0, more=False)
        finish(self.turns - 1, 1, more=False)

    def tensor(self, e, g):
        e.wait_ge(self.split, 1)
        with e.Fori(0, self.turns) as k:
            for s in range(2):
                e.wait_ge(self.hot_ready[s], k + 1)
                e.wait_ge(self.read[s], k + 1)
                for i in range(RU):
                    n = self.w * NT
                    o = g.ps[s * 4 + i // self.per][:, (i % self.per) * n:(i % self.per + 1) * n]
                    for part in range(3):
                        m = e.matmul(o, lhsT=self.hot[:, s, i * P:(i + 1) * P],
                                     rhs=self.parts[:, part].rearrange("p w c -> p (w c)"),
                                     start=part == 0, stop=part == 2)
                m.then_inc(self.looked[s], 1)



def stage_edges0(nc, env, A, REC):
    g = env
    sem = g.sem
    loaded, linked, idx_ready, marked = sem("e0_loaded"), sem("e0_linked"), sem("e0_idx"), sem("e0_marked")
    filled, expanded = sem("e0_filled"), sem("e0_expanded")
    w_zeroed, attr_in, product, kept = sem("e0_w_zeroed"), sem("e0_attr_in"), sem("e0_product"), sem("e0_kept")
    BANKS = 5
    asked, answered, exp_asked, exp_done = sem("e0_ask"), sem("e0_answer"), sem("e0_exp_ask"), sem("e0_exp")
    rec_ready, based, border = sem("e0_rec"), sem("e0_based"), sem("e0_border")
    with ExitStack() as own:
        n = Narrow(g, nc, own, "s0", NRW)
        key = own.enter_context(nc.sbuf_tensor("e0_key", [P, ET + 2], i32))
        any_ = own.enter_context(nc.sbuf_tensor("e0_any", [P, 1], f32))
        carry = own.enter_context(nc.sbuf_tensor("e0_carry", [P, 8], f32))
        fsum = own.enter_context(nc.sbuf_tensor("e0_fsum", [P, NT], f32))
        keyf = own.enter_context(nc.sbuf_tensor("e0_keyf", [P, ET], f32))
        mark = own.enter_context(nc.sbuf_tensor("e0_mark", [2, 2], f32))
        half = ET // 16
        attr = [g.PD[:, :, :].rearrange("p j h -> p (j h)").rearrange("p (g q) -> p g q", q=P),
                own.enter_context(nc.sbuf_tensor("e0_attr", [P, half, P], f32))]
        W = own.enter_context(nc.sbuf_tensor("e0_W", [P, 64], f32))
        Wd = attr[1][:, 0:2 * D // P, :].rearrange("p a q -> p (a q)").rearrange("p (h m) -> p h m", h=2)
        wd_in, own_product, own_kept = sem("e0_wd_in"), sem("e0_own_product"), sem("e0_own_kept")
        with nc.Block() as block:
            @block.sync
            def _(e):
                e.dma_start(key[:, :], A["dst_c"][:, :]).then_inc(loaded, 16)
                e.wait_ge(w_zeroed, 1)
                for n in range(8):
                    e.dma_start(W[16 * n:16 * n + 16, 8 * n:8 * n + 8], A["L0_gnn_W_attn_edge"][:, :])\
                        .then_inc(attr_in, 16)
                for i in range(2):
                    e.dma_start(attr[i][:, :, :], A["attr"][i * half:(i + 1) * half].rearrange("g r p -> r g p"))\
                        .then_inc(attr_in, 16)
                e.wait_ge(marked, 1)
                e.dma_start(g.RECD[0:1, 0:2], mark[0:1, :]).then_inc(border, 16)
                e.dma_start(g.RECD[EP + 1:EP + 2, 0:2], mark[1:2, :]).then_inc(border, 16)
                e.wait_ge(filled, 16 * NT)
                e.dma_start(g.T2[:, :, :], g.Z8.rearrange("(p j) w -> p j w", j=ET)).then_inc(expanded, 16)
                e.wait_ge(product, -(-ET // 64))
                e.dma_start(Wd, A["L0_gnn_W_apply_dst"].rearrange("(h p) m -> p h m", p=P)).then_inc(wd_in, 16)
                e.wait_ge(expanded, 16)
                e.wait_ge(border, 32)
                e.wait_ge(wd_in, 16)

            @block.gpsimd
            def _(e):
                e.wait_ge(idx_ready, 1)
                for j in range(NT):
                    e.indirect_dma_start(out=g.Z8[:, :], out_offset=IOA(ap=g.put_d[:, j:j + 1], axis=0),
                                         in_=g.AD[:, j, :], in_offset=None, bounds_check=EP - 1,
                                         oob_is_err=False).then_inc(filled, 16)
                e.wait_ge(rec_ready, 1)
                pool_scatter(e, n, g.rank_c, REC, g.RECD[:, :])

            @block.scalar
            def _(e):
                e.wait_ge(exp_asked, 1)
                e.activation(g.PD[:, :, :], g.PD[:, :, :], ACT.Exp).then_inc(exp_done, 1)
                for j in range(NT):
                    e.wait_ge(own_product, j + 1)
                    e.activation(g.HT[:, :, j * P:(j + 1) * P],
                                 g.ps[j % 4][:, 0:D].rearrange("p (h n) -> p h n", h=2), ACT.Copy)\
                        .then_inc(own_kept, 1)

            @block.vector
            def _(e):
                link = Link(e, linked)
                flip, exp = Asks(e, asked, answered), Asks(e, exp_asked, exp_done)
                e.memset(W[:, :], 0.0).then_inc(w_zeroed, 1)
                e.memset(mark[:, :], -1.0).then_inc(marked, 1)
                for deg, start, put, end in ((g.deg_d, g.start_d, g.put_d, g.end_d),
                                             (g.deg_s, g.start_s, g.put_s, g.end_s)):
                    link(e.tensor_single_scalar(fsum[:, :], deg[:, :], 0.0, ALU.is_equal))
                    link(e.scalar_tensor_tensor(fsum[:, :], fsum[:, :], float(EP), start[:, :], ALU.mult, ALU.add))
                    link(e.tensor_copy(put[:, :], fsum[:, :]))
                    link(e.scalar_tensor_tensor(fsum[:, :], start[:, :], -1.0, deg[:, :], ALU.add, ALU.add))
                    link(e.tensor_single_scalar(fsum[:, :], fsum[:, :], 0.0, ALU.max))
                    link(e.tensor_copy(end[:, :], fsum[:, :]))
                e.sem_inc(idx_ready, 1)
                e.wait_ge(loaded, 16)
                order_masks(e, g, link, flip, g.od, key, any_)
                link(e.tensor_copy(keyf[:, :], g.dst_t[:, :]))
                link(e.tensor_copy(g.base_d[0:1, :], g.dst_t[0:1, :]))
                flip()
                link(e.tensor_tensor(g.lrel_d[:, :], keyf[:, :], g.ps[5][:, 0:ET], ALU.subtract))
                link(e.tensor_scalar(g.win_d[:, :], g.ps[5][:, 0:ET], g.iota_p[:, 0:1], None, ALU.add))
                for n in range(-(-ET // 64)):
                    m = min(64, ET - 64 * n)
                    e.wait_ge(product, n + 1)
                    e.tensor_copy(REC[:, 64 * n:64 * n + m, 2:10],
                                  g.ps[n % BANKS][:, 0:8 * m].rearrange("p (j h) -> p j h", h=8)).then_inc(kept, 1)
                e.wait_ge(kept, -(-ET // 64))
                link(e.tensor_copy(REC[:, :, 0], g.src_c[:, :]))
                link(e.tensor_copy(REC[:, :, 1], key[:, 1:ET + 1]))
                e.wait_ge(expanded, 16)
                seg_scan(e, g, link, flip, 8, False, ALU.mult, ALU.add, g.od.fm, g.od.fmT, 0.0, g.T2, g.T1, carry)
                E = REC[:, :, 2:10]
                link(e.tensor_tensor(E, E, g.GAT[:, :, 0:8], ALU.add))
                link(e.tensor_tensor(E, E, g.T1[:, :, :], ALU.add))
                link(e.scalar_tensor_tensor(E, E, 0.2, E, ALU.mult, ALU.max))
                e.sem_inc(rec_ready, 1)
                link(e.tensor_copy(g.PD[:, :, :], E))
                link(e.tensor_copy(g.GAT[:, :, 0:8], E))
                seg_softmax(e, g, link, flip, exp, 8, g.od, g.PD, g.T1, g.T2, carry)

            @block.tensor
            def _(e):
                kinds = ORDER_FLIPS + [("base", 0)] + scan_flips(8, 5)
                for k, (kind, w) in enumerate(kinds):
                    if k == len(ORDER_FLIPS) + 1:
                        e.wait_ge(attr_in, 16 * 10)
                        for n in range(-(-ET // 64)):
                            if n >= BANKS:
                                e.wait_ge(kept, n - BANKS + 1)
                            for q in range(8 * n, min(8 * n + 8, ET // 8)):
                                last = e.matmul(g.ps[n % BANKS][:, 64 * (q % 8):64 * (q % 8) + 64],
                                                lhsT=attr[q // half][:, q % half, :], rhs=W[:, :],
                                                start=True, stop=True)
                            last.then_inc(product, 1)
                    e.wait_ge(asked, k + 1)
                    if kind == "base":
                        e.matmul(g.ps[5][:, 0:ET], lhsT=g.ones[0:1, :], rhs=keyf[0:1, :], start=True, stop=True)\
                            .then_inc(answered, 1)
                    elif kind == "in":
                        e.transpose(g.ps[6][0:w, 0:P], g.flip_in[:, 0:w], g.ident[:, :]).then_inc(answered, 1)
                    else:
                        e.transpose(g.ps[7][:, 0:w], g.flip_ex[0:w, 1:P + 1], g.ident[0:w, 0:w])\
                            .then_inc(answered, 1)
                e.wait_ge(wd_in, 16)
                for j in range(NT):
                    if j >= 4:
                        e.wait_ge(own_kept, j - 3)
                    for h in range(2):
                        m = e.matmul(g.ps[j % 4][:, 0:D], lhsT=g.HT[:, h, j * P:(j + 1) * P], rhs=Wd[:, h, :],
                                     start=h == 0, stop=h == 1)
                    m.then_inc(own_product, 1)


def stage_by_src(nc, env):
    g = env
    sem = g.sem
    loaded, linked, asked, answered = sem("bs_loaded"), sem("bs_linked"), sem("bs_ask"), sem("bs_answer")
    exp_asked, exp_done, keys_ready, keys_out = sem("bs_exp_ask"), sem("bs_exp"), sem("bs_keys"), sem("bs_out")
    slices, turned, based, soft, stored = (sem("bs_slices"), sem("bs_turned"), sem("bs_based"), sem("bs_soft"),
                                           sem("bs_stored"))
    with ExitStack() as own:
        def sb(name, shape, dt=f32):
            return own.enter_context(nc.sbuf_tensor("bs_" + name, shape, dt))
        RC = sb("RC", [P, ET + 2, NRW])
        keys = sb("keys", [P, 2, ET])
        part = sb("part", [TQ, 2, 4, P])
        tiles = sb("tiles", [P, 2, ET])
        any_, carry = sb("any", [P, 1]), sb("carry", [P, 8])
        di = sb("di", [P, ET], i32)
        low = sb("low", [P, 2, ET])
        lowt = sb("lowt", [TQ, 2, 4, P], bf16)
        flat, digits_out, ends = sem("bs_flat"), sem("bs_digits_out"), sem("bs_ends")
        with nc.Block() as block:
            @block.gpsimd
            def _(e):
                e.wait_ge(stored, 16)
                for j in range(NT):
                    e.indirect_dma_start(out=g.LT[:, j, :], out_offset=None, in_=g.LSD[:, :],
                                         in_offset=IOA(ap=g.end_s[:, j:j + 1], axis=0)).then_inc(ends, 16)
                e.wait_ge(ends, 16 * NT)

            @block.sync
            def _(e):
                e.dma_start(RC[:, 1:ET + 1, :], g.RECD[1:EP + 1, :].rearrange("(p j) w -> p j w", j=ET))\
                    .then_inc(loaded, 16)
                e.dma_start(RC[:, 0:1, 0:2], g.RECD[0:EP, :].rearrange("(p j) w -> p j w", j=ET)[:, 0:1, 0:2])\
                    .then_inc(loaded, 16)
                e.dma_start(RC[:, ET + 1:ET + 2, 0:2],
                            g.RECD[2:EP + 2, :].rearrange("(p j) w -> p j w", j=ET)[:, ET - 1:ET, 0:2])\
                    .then_inc(loaded, 16)
                e.wait_ge(keys_ready, 1)
                e.dma_start(g.KEYD.rearrange("n (p j) -> p n j", j=ET), keys[:, :, :]).then_inc(keys_out, 16)
                e.wait_ge(keys_out, 16)
                for m in range(2):
                    e.dma_start(part[:, m, :, :], g.KEYD[m, :].rearrange("(i q p) -> q i p", i=4, p=P))\
                        .then_inc(slices, 16)
                e.wait_ge(soft, 1)
                e.dma_start(g.LSD.rearrange("(p j) w -> p j w", j=ET), g.T1[:, :, :]).then_inc(stored, 16)
                for m, flat_row in ((0, g.SLOW), (1, g.DLOW)):
                    e.wait_ge(flat, m + 1)
                    e.dma_start(flat_row.rearrange("(i q p) -> q i p", i=4, p=P), lowt[:, m, :, :])\
                        .then_inc(digits_out, 16)
                e.wait_ge(digits_out, 32)
                e.wait_ge(stored, 16)

            @block.scalar
            def _(e):
                e.wait_ge(exp_asked, 1)
                e.activation(g.T3[:, :, :], g.T3[:, :, :], ACT.Exp).then_inc(exp_done, 1)
                e.wait_ge(exp_asked, 2)
                e.activation(g.T2[:, :, :], g.T2[:, :, :], ACT.Ln).then_inc(exp_done, 1)

            @block.vector
            def _(e):
                link = Link(e, linked)
                flip, exp = Asks(e, asked, answered), Asks(e, exp_asked, exp_done)
                e.wait_ge(loaded, 48)
                e.tensor_copy(keys[:, 0, :], RC[:, 1:ET + 1, 0])
                link(e.tensor_copy(keys[:, 1, :], RC[:, 1:ET + 1, 1]))
                e.sem_inc(keys_ready, 1)
                link(e.tensor_copy(g.dsts_c[:, :], keys[:, 1, :]))
                order_masks(e, g, link, flip, g.os, RC[:, :, 0], any_)
                S, M, V, o = g.T3, g.T1, g.T2, g.os
                link(e.tensor_copy(S[:, :, :], RC[:, 1:ET + 1, 2:10]))
                seg_scan(e, g, link, flip, 8, False, ALU.add, ALU.max, o.fneg, o.fnegT, -BIG, S, M, carry)
                link(e.tensor_tensor(V[:, :, :], M[:, :, :], bc_last(o.last[:, :], 8), ALU.mult))
                seg_scan(e, g, link, flip, 8, True, ALU.mult, ALU.add, o.gm, o.gmT, 0.0, V, M, carry)
                link(e.tensor_tensor(S[:, :, :], S[:, :, :], M[:, :, :], ALU.subtract))
                exp()
                seg_scan(e, g, link, flip, 8, False, ALU.mult, ALU.add, o.fm, o.fmT, 0.0, S, V, carry)
                link(e.tensor_single_scalar(V[:, :, :], V[:, :, :], 1.0, ALU.max))
                exp()
                link(e.tensor_tensor(M[:, :, :], M[:, :, :], V[:, :, :], ALU.add))
                e.sem_inc(soft, 1)
                for m in range(2):
                    e.wait_ge(turned, 2)
                    for i in range(4):
                        ins = e.tensor_copy(tiles[:, m, i * TQ:(i + 1) * TQ], g.ps[i][:, m * P:m * P + TQ])
                    link(ins)
                link(e.tensor_copy(g.dsts_t[:, :], tiles[:, 1, :]))
                link(e.tensor_copy(g.base_s[0:1, :], tiles[0:1, 0, :]))
                flip()
                link(e.tensor_tensor(g.lrel_s[:, :], tiles[:, 0, :], g.ps[5][:, 0:ET], ALU.subtract))
                for m, index, high in ((0, g.src_c, g.shi_c), (1, g.dsts_c, g.dhi_s)):
                    link(e.tensor_single_scalar(di[:, :], index[:, :], P - 1, ALU.bitwise_and))
                    link(e.tensor_copy(low[:, m, :], di[:, :]))
                    link(e.tensor_single_scalar(di[:, :], index[:, :], 7, ALU.arith_shift_right))
                    link(e.tensor_copy(high[:, :], di[:, :]))
                    flip()
                    for i in range(4):
                        ins = e.tensor_copy(lowt[:, m, i, :], g.ps[i][0:TQ, 0:P])
                    link(ins)
                    e.sem_inc(flat, 1)

            @block.tensor
            def _(e):
                def turn(m):
                    e.wait_ge(slices, 16 * (m + 1) if m else 32)
                    for i in range(4):
                        ins = e.transpose(g.ps[i][:, m * P:m * P + TQ], part[:, m, i, :], g.ident[0:TQ, 0:TQ])
                    ins.then_inc(turned, 1)

                kinds = ORDER_FLIPS + scan_flips(8, 3) + [("base", 0), ("low", 0), ("low", 1)]
                for k, (kind, w) in enumerate(kinds):
                    if kind == "base":
                        turn(0)
                        turn(1)
                    e.wait_ge(asked, k + 1)
                    if kind == "base":
                        e.matmul(g.ps[5][:, 0:ET], lhsT=g.ones[0:1, :], rhs=tiles[0:1, 0, :],
                                 start=True, stop=True).then_inc(answered, 1)
                    elif kind == "low":
                        for i in range(4):
                            ins = e.transpose(g.ps[i][0:TQ, 0:P], low[:, w, i * TQ:(i + 1) * TQ], g.ident[:, :])
                        ins.then_inc(answered, 1)
                    elif kind == "in":
                        e.transpose(g.ps[6][0:w, 0:P], g.flip_in[:, 0:w], g.ident[:, :]).then_inc(answered, 1)
                    else:
                        e.transpose(g.ps[7][:, 0:w], g.flip_ex[0:w, 1:P + 1], g.ident[0:w, 0:w])\
                            .then_inc(answered, 1)


def stage_messages0(nc, env):
    g = env
    sem = g.sem
    linked, asked, answered = sem("m0_linked"), sem("m0_ask"), sem("m0_answer")
    root_asked, root_done, summed, stored, rows_in = (sem("m0_root_ask"), sem("m0_root"), sem("m0_summed"),
                                                      sem("m0_stored"), sem("m0_rows"))
    table_out = sem("m0_table_out")
    with ExitStack() as own:
        look = Lookup(g, lambda x, shape, dt=f32: own.enter_context(nc.sbuf_tensor(x, shape, dt)), "lk0", 8,
                      LOOKED // (2 * RU))
        ahead = Ahead(nc, g, own, "m0", ET - LOOKED)
        carry = own.enter_context(nc.sbuf_tensor("m0_carry", [P, 8], f32))
        with nc.Block() as block:
            @block.gpsimd
            def _(e):
                e.wait_ge(table_out, 16)
                ahead.gather(e, [g.src_c[:, LOOKED:ET]], g.LTD[:, :], g.T3[:, LOOKED:ET, :])
                e.wait_ge(stored, 16)
                for j in range(NT):
                    e.indirect_dma_start(out=g.MSG[:, j, :], out_offset=None, in_=g.MSD[:, :],
                                         in_offset=IOA(ap=g.end_d[:, j:j + 1], axis=0)).then_inc(rows_in, 16)
                e.wait_ge(rows_in, 16 * NT)

            @block.scalar
            def _(e):
                e.wait_ge(root_asked, 1)
                e.activation(g.T3[:, :, :], g.T3[:, :, :], ACT.Exp).then_inc(root_done, 1)
                e.wait_ge(root_asked, 2)
                e.activation(g.PD[:, :, :], g.PD[:, :, :], ACT.Sqrt).then_inc(root_done, 1)

            @block.vector
            def _(e):
                link = Link(e, linked)
                flip, root = Asks(e, asked, answered), Asks(e, root_asked, root_done)
                link(e.tensor_single_scalar(g.PD[:, :, :], g.PD[:, :, :], 1e-9, ALU.max))
                look.split_table(e, link, g.LT[:, :, :])
                look.vector(e, g, g.shi_c, g.T3)
                e.wait_ge(look.masked[1], 2 * look.turns + 1)
                e.wait_ge(ahead.landed, 16 * ahead.columns)
                link(e.tensor_tensor(g.T3[:, :, :], g.GAT[:, :, 0:8], g.T3[:, :, :], ALU.subtract))
                root()
                link(e.scalar_tensor_tensor(g.PD[:, :, :], g.T3[:, :, :], 1e-9, g.PD[:, :, :], ALU.max, ALU.mult))
                root()
                link(e.tensor_tensor(g.PD[:, :, :], g.PD[:, :, :], g.GAT[:, :, 8:16], ALU.mult))
                seg_scan(e, g, link, flip, 8, False, ALU.mult, ALU.add, g.od.fm, g.od.fmT, 0.0, g.PD, g.T1, carry)
                e.sem_inc(summed, 1)
                e.wait_ge(rows_in, 16 * NT)
                link(e.tensor_single_scalar(g.T3[:, 0:NT, 0], g.deg_d[:, :], 0.0, ALU.is_gt))
                link(e.tensor_tensor(g.MSG[:, :, :], g.MSG[:, :, :], bc_last(g.T3[:, 0:NT, 0], 8), ALU.mult))

            @block.sync
            def _(e):
                e.dma_start(g.LTD.rearrange("(j p) w -> p j w", p=P), g.LT[:, :, :]).then_inc(table_out, 16)
                look.load_rows(e, g.SLOW)
                e.wait_ge(summed, 1)
                e.dma_start(g.MSD.rearrange("(p j) w -> p j w", j=ET), g.T1[:, :, :]).then_inc(stored, 16)
                e.wait_ge(stored, 16)

            @block.tensor
            def _(e):
                look.tensor(e, g)
                tensor_flips(e, g, asked, answered, scan_flips(8, 1))



def stage_update0(nc, env, A):
    g = env
    sem = g.sem
    loaded, flipped, kept, linked, asked, root_done = (sem("u0_loaded"), sem("u0_flipped"), sem("u0_kept"),
                                                       sem("u0_linked"), sem("u0_ask"), sem("u0_root"))
    ready, first, act_in, turned, act_t, second, done = (sem("u0_ready"), sem("u0_first"), sem("u0_act"),
                                                         sem("u0_turned"), sem("u0_act_t"), sem("u0_second"),
                                                         sem("u0_done"))
    biased = sem("u0_biased")
    with ExitStack() as own:
        def sb(name, shape):
            return own.enter_context(nc.sbuf_tensor("u0_" + name, shape, f32))
        M = sb("M", [8, NP])
        BN = next(n for n in range(512, 0, -1) if NN % n == 0)
        stats = sb("stats", [8, NN // BN, 6])
        st = sb("st", [8, 8])
        Wa, Wo = sb("Wa", [8, D]), sb("Wo", [P, 2, D])
        b1, b2, bo = sb("b1", [P, D]), sb("b2", [P, D]), sb("bo", [P, D])
        R, Q, RT = sb("R", [P, 2, D]), sb("Q", [P, 2, D]), sb("RT", [P, 2, D])
        with nc.Block() as block:
            @block.sync
            def _(e):
                e.dma_start(Wa[:, :], A["L0_gnn_W_agg"][:, :]).then_inc(loaded, 16)
                e.dma_start(Wo[:, :, :], A["L0_gnn_W_apply"].rearrange("(h p) m -> p h m", p=P))\
                    .then_inc(loaded, 16)
                e.dma_start(b1[:, :], bc_row(A["L0_gnn_b_agg"])).then_inc(loaded, 16)
                e.dma_start(b2[:, :], bc_row(A["L0_gnn_b_apply_dst"])).then_inc(loaded, 16)
                e.dma_start(bo[:, :], bc_row(A["L0_gnn_b_apply"])).then_inc(loaded, 16)
                e.dma_start(st[:, 6:7], A["L0_gnn_bn_gamma"][:, None]).then_inc(loaded, 16)
                e.dma_start(st[:, 7:8], A["L0_gnn_bn_beta"][:, None]).then_inc(loaded, 16)

            @block.gpsimd
            def _(e):
                e.wait_ge(loaded, 112)
                e.tensor_tensor(b1[:, :], b1[:, :], b2[:, :], ALU.add).then_inc(biased, 1)
                e.wait_ge(biased, 1)
                v = g.HT[:, :, :].rearrange("p h (j c) -> p h j c", c=P)
                e.tensor_tensor(v, v, b1[:, :].rearrange("p (h c) -> p h c", h=2)[:, :, None, :]
                                .to_broadcast([P, 2, NT, P]), ALU.add).then_inc(biased, 1)
                e.tensor_tensor(g.X[:, :, :], g.X[:, :, :], bc_mid(bo[:, :], NT), ALU.add).then_inc(biased, 1)

            @block.scalar
            def _(e):
                e.wait_ge(asked, 1)
                e.activation(st[:, 2:3], st[:, 1:2], ACT.Sqrt).then_inc(root_done, 1)
                for j in range(NT):
                    e.wait_ge(turned, j + 1)
                    if j >= 2:
                        e.wait_ge(second, j - 1)
                    e.activation(RT[:, j % 2, :], g.ps[2 + j % 2][:, 0:D], ACT.Copy).then_inc(act_t, 1)

            @block.vector
            def _(e):
                link = Link(e, linked)
                for q in range(7):
                    e.wait_ge(flipped, q + 1)
                    m = min(4, NT - 4 * q)
                    link(e.tensor_copy(M[:, q * 4 * P:(q * 4 + m) * P], g.ps[q][0:8, 0:m * P]))
                for q in range(NN // BN):
                    ins = e.bn_stats(stats[:, q, :], M[:, q * BN:(q + 1) * BN])
                link(ins)
                link(e.bn_aggr(st[:, 0:2], stats[:, :, :]))
                link(e.tensor_single_scalar(st[:, 1:2], st[:, 1:2], LN_EPS, ALU.add))
                e.wait_ge(loaded, 112)
                e.sem_inc(asked, 1)
                e.wait_ge(root_done, 1)
                link(e.reciprocal(st[:, 3:4], st[:, 2:3]))
                link(e.tensor_tensor(st[:, 4:5], st[:, 3:4], st[:, 6:7], ALU.mult))
                link(e.tensor_scalar(M[:, :], M[:, :], st[:, 0:1], None, ALU.subtract))
                link(e.tensor_scalar(M[:, :], M[:, :], st[:, 4:5], st[:, 7:8], ALU.mult, ALU.add))
                e.sem_inc(ready, 1)
                e.wait_ge(biased, 3)
                for j in range(NT + 2):
                    if j < NT:
                        e.wait_ge(first, j + 1)
                        link(e.tensor_tensor(Q[:, j % 2, :].rearrange("p (h c) -> p h c", h=2),
                                             g.ps[j % 2][:, 0:D].rearrange("p (h c) -> p h c", h=2),
                                             g.HT[:, :, j * P:(j + 1) * P], ALU.add))
                        if j >= 2:
                            e.wait_ge(turned, j - 1)
                        e.scalar_tensor_tensor(R[:, j % 2, :], Q[:, j % 2, :], 0.2, Q[:, j % 2, :], ALU.mult,
                                               ALU.max).then_inc(act_in, 1)
                    if j >= 2:
                        i = j - 2
                        e.wait_ge(second, i + 1)
                        e.tensor_tensor(g.X[:, i, :], g.X[:, i, :], g.ps[4 + i % 2][:, 0:D], ALU.add)\
                            .then_inc(done, 1)

            @block.tensor
            def _(e):
                for q in range(7):
                    m = min(4, NT - 4 * q)
                    for i in range(m):
                        last = e.transpose(g.ps[q][0:8, i * P:(i + 1) * P], g.MSG[:, 4 * q + i, :], g.ident[:, :])
                    last.then_inc(flipped, 1)
                e.wait_ge(ready, 1)
                for j in range(NT + 2):
                    if j < NT:
                        if j >= 2:
                            e.wait_ge(act_in, j - 1)
                        at = slice(j * P, (j + 1) * P)
                        e.matmul(g.ps[j % 2][:, 0:D], lhsT=M[:, at], rhs=Wa[:, :], start=True, stop=True)\
                            .then_inc(first, 1)
                    if 1 <= j <= NT:
                        i = j - 1
                        e.wait_ge(act_in, i + 1)
                        if i >= 2:
                            e.wait_ge(act_t, i - 1)
                        e.transpose(g.ps[2 + i % 2][:, 0:P], R[:, i % 2, 0:P], g.ident[:, :])
                        e.transpose(g.ps[2 + i % 2][:, P:D], R[:, i % 2, P:D], g.ident[:, :]).then_inc(turned, 1)
                    if j >= 2:
                        i = j - 2
                        e.wait_ge(act_t, i + 1)
                        if i >= 2:
                            e.wait_ge(done, i - 1)
                        e.matmul(g.ps[4 + i % 2][:, 0:D], lhsT=RT[:, i % 2, 0:P], rhs=Wo[:, 0, :], start=True,
                                 stop=False)
                        e.matmul(g.ps[4 + i % 2][:, 0:D], lhsT=RT[:, i % 2, P:D], rhs=Wo[:, 1, :], start=False,
                                 stop=True).then_inc(second, 1)



class Project:

    def __init__(self, nc, g, own, name, weight, bias, vec, groups, scale, T, V, table, row, tmp, bank):
        self.g, self.weight, self.bias, self.vec, self.groups, self.scale = g, weight, bias, vec, groups, scale
        self.T, self.V, self.table, self.row, self.tmp, self.bank = T, V, table, row, tmp, bank
        self.loaded, self.product, self.kept, self.linked, self.ready, self.stored = (
            g.sem(name + x) for x in ("_loaded", "_product", "_kept", "_linked", "_ready", "_stored"))
        self.W = own.enter_context(nc.sbuf_tensor(name + "_W", [P, 2, D], f32))
        self.b = own.enter_context(nc.sbuf_tensor(name + "_b", [P, D], f32))
        self.v = own.enter_context(nc.sbuf_tensor(name + "_v", [P, len(vec), D], f32))
        self.loads = 2 + sum(len(parts) for parts in vec)

    def load(self, e):
        e.dma_start(self.W[:, :, :], self.weight.rearrange("(h p) m -> p h m", p=P)).then_inc(self.loaded, 16)
        e.dma_start(self.b[:, :], bc_row(self.bias)).then_inc(self.loaded, 16)
        for q, parts in enumerate(self.vec):
            for at, part in parts:
                e.dma_start(self.v[:, q, at:at + part.shape[0]], bc_row(part)).then_inc(self.loaded, 16)

    def store(self, e):
        e.wait_ge(self.ready, 1)
        e.dma_start(self.table.rearrange("(j p) d -> p j d", p=P), self.T[:, :, 0:self.row])\
            .then_inc(self.stored, 16)
        e.wait_ge(self.stored, 16)

    def tensor(self, e, in_ht):
        g = self.g
        e.wait_ge(self.loaded, 16 * self.loads)
        for j in range(NT):
            e.wait_ge(in_ht, j + 1)
            if j >= 4:
                e.wait_ge(self.kept, j - 3)
            for h in range(2):
                m = e.matmul(g.ps[self.bank + j % 4][:, 0:D], lhsT=g.HT[:, h, j * P:(j + 1) * P],
                             rhs=self.W[:, h, :], start=h == 0, stop=h == 1)
            m.then_inc(self.product, 1)

    def vector(self, e, turned):
        g, T, V, tmp, v = self.g, self.T, self.V, self.tmp, self.v
        link = Link(e, self.linked)
        e.wait_ge(self.loaded, 16 * self.loads)
        e.wait_ge(turned, NT)
        for j in range(NT + 1):
            if j < NT:
                e.wait_ge(self.product, j + 1)
                e.tensor_tensor(T[:, j, 0:D], g.ps[self.bank + j % 4][:, 0:D], self.b[:, :], ALU.add)\
                    .then_inc(self.kept, 1)
            if j > 0:
                e.wait_ge(self.kept, j)
                ins = e.tensor_tensor(tmp[:, j - 1, :], T[:, j - 1, 0:D], v[:, 0, :], ALU.mult)
        link(ins)
        for q in range(len(self.vec)):
            if q:
                link(e.tensor_tensor(tmp[:, :, :], T[:, :, 0:D], bc_mid(v[:, q, :], NT), ALU.mult))
            link(e.tensor_reduce(V[q], tmp[:, :, :].rearrange("p j (n c) -> p j n c", n=self.groups), AX.X,
                                 ALU.add))
            if self.scale != 1.0:
                link(e.tensor_single_scalar(V[q], V[q], self.scale, ALU.mult))
        e.sem_inc(self.ready, 1)


def stage_norm_project(nc, env, name, projections, ahead_of=None, lone=None):
    g = env
    with ExitStack() as own:
        norm = Norm(nc, g, own, name)
        projects = [Project(nc, g, own, *p, norm.H, 4 * (1 - i)) for i, p in enumerate(projections)]
        if ahead_of is not None:
            ahead = Ahead(nc, g, own, name, ahead_of[2].shape[1])
        if lone is not None:
            alone, found = own.enter_context(nc.sbuf_tensor(name + "_alone", [P, NT], f32)), g.sem(name + "_found")
        with nc.Block() as block:
            @block.vector
            def _(e):
                norm.vector(e)
                for p in projects:
                    p.vector(e, norm.flipped)
                if lone is not None:
                    T = projects[0].T
                    e.tensor_single_scalar(alone[:, :], lone[:, :], 0.0, ALU.is_equal).then_inc(found, 1)
                    e.wait_ge(found, 1)
                    for j in range(NT):
                        e.scalar_tensor_tensor(g.X[:, j, :], T[:, j, 0:D], alone[:, j:j + 1], g.X[:, j, :],
                                               ALU.mult, ALU.add)

            @block.scalar
            def _(e):
                norm.scalar(e)

            @block.tensor
            def _(e):
                norm.tensor(e)
                for p in projects:
                    p.tensor(e, norm.kept)

            @block.sync
            def _(e):
                for p in projects:
                    p.load(e)
                for p in projects:
                    p.store(e)

            if ahead_of is not None:
                @block.gpsimd
                def _(e):
                    e.wait_ge(projects[0].stored, 16)
                    ahead.gather(e, *ahead_of)



def stage_edges1(nc, env, SN, TN, AL, pre):
    g = env
    sem = g.sem
    linked, asked, answered, exp_asked, exp_done = (sem("e1_linked"), sem("e1_ask"), sem("e1_answer"),
                                                    sem("e1_exp_ask"), sem("e1_exp"))
    filled, expanded, soft, stored = (
        sem("e1_filled"), sem("e1_expanded"), sem("e1_soft"), sem("e1_stored"))
    with ExitStack() as own:
        def sb(name, shape, dt=f32):
            return own.enter_context(nc.sbuf_tensor("e1_" + name, shape, dt))
        look = Lookup(g, sb, "lk1", 2)
        ahead = Ahead(nc, g, own, "e1", pre.shape[1])
        S, M, V, TG = (sb(x, [P, ET, 2]) for x in ("S", "M", "V", "TG"))
        carry = sb("carry", [P, 8])
        with nc.Block() as block:
            @block.sync
            def _(e):
                look.load_rows(e, g.DLOW)
                e.wait_ge(filled, 16 * NT)
                e.dma_start(M[:, :, :], g.Z2.rearrange("(p j) w -> p j w", j=ET)).then_inc(expanded, 16)
                e.wait_ge(soft, 1)
                e.dma_start(AL.rearrange("(p j) w -> p j w", j=ET), TG[:, :, :]).then_inc(stored, 16)
                e.wait_ge(stored, 16)

            @block.gpsimd
            def _(e):
                for j in range(NT):
                    e.indirect_dma_start(out=g.Z2[:, :], out_offset=IOA(ap=g.put_s[:, j:j + 1], axis=0),
                                         in_=SN[:, j, :], in_offset=None, bounds_check=EP - 1,
                                         oob_is_err=False).then_inc(filled, 16)
                ahead.gather(e, [g.dsts_t[:, k * SETS * U:(k + 1) * SETS * U] for k in PRE_AT], g.WHD[:, :], pre)

            @block.scalar
            def _(e):
                e.wait_ge(exp_asked, 1)
                e.activation(TG[:, :, :], TG[:, :, :], ACT.Exp).then_inc(exp_done, 1)

            @block.vector
            def _(e):
                link = Link(e, linked)
                flip, exp = Asks(e, asked, answered), Asks(e, exp_asked, exp_done)
                look.split_table(e, link, TN[:, :, :])
                look.vector(e, g, g.dhi_s, TG)
                e.wait_ge(look.masked[1], 2 * RI + 1)
                e.wait_ge(expanded, 16)
                seg_scan(e, g, link, flip, 2, False, ALU.mult, ALU.add, g.os.fm, g.os.fmT, 0.0, M, S, carry)
                link(e.tensor_tensor(TG[:, :, :], TG[:, :, :], S[:, :, :], ALU.add))
                link(e.scalar_tensor_tensor(TG[:, :, :], TG[:, :, :], 0.2, TG[:, :, :], ALU.mult, ALU.max))
                seg_softmax(e, g, link, flip, exp, 2, g.os, TG, M, V, carry)
                e.sem_inc(soft, 1)

            @block.tensor
            def _(e):
                look.tensor(e, g)
                tensor_flips(e, g, asked, answered, scan_flips(2, 5))



def stage_aggregate(nc, env, name, table, row, index, lrel, base, acc, weights=None, heads=0, pre=None, OH=None,
                    own_part=None):
    g = env
    sem = g.sem
    landed, hot, scaled, w_in = ([sem(f"{name}_{x}{s}") for s in range(SETS)]
                                 for x in ("landed", "hot", "scaled", "w_in"))
    staged, seen, spread = sem(name + "_staged"), sem(name + "_seen"), sem(name + "_spread")
    summed, added = sem(name + "_summed"), sem(name + "_added")
    CREDIT, BANKS = SETS * U, 8
    pre_at = () if pre is None else PRE_AT
    with ExitStack() as own:
        def sb(n, shape, dt=f32):
            return own.enter_context(nc.sbuf_tensor(f"{name}_{n}", shape, dt))
        idx = sb("idx", [P, SETS, U], i32)
        G = sb("G", [P, SETS, U, row])
        if OH is None:
            OH = sb("OH", [P, SETS, U, P])
        W = sb("W", [P, SETS, U, max(heads, 1)])
        if own_part is not None:
            own_part = OwnPart(nc, g, own, own_part)

        def rows_of(s, slot):
            return G[:, s, :, :] if slot is None else pre[:, slot * CREDIT + s * U:slot * CREDIT + (s + 1) * U, :]

        def turns(e, turn):
            at = 0
            for n, k in enumerate(pre_at + (WI,)):
                if at < k:
                    with e.Fori(at, k) as r:
                        turn(r, None, n)
                if k < WI:
                    turn(k, n, n)
                at = k + 1

        with nc.Block() as block:
            @block.gpsimd
            def _(e):
                def gather(k, skipped, last_use):
                    for s in range(SETS):
                        if last_use is not None:
                            e.wait_ge(summed, last_use * CREDIT + (s + 1) * U)
                        e.tensor_copy(idx[:, s, :], index[:, bass.ds(k * (SETS * U) + s * U, U)])\
                            .then_inc(staged, 1)
                        e.wait_ge(staged, (k - skipped) * SETS + (s + 1))
                        e.sem_inc(seen, 1)
                        for i in range(U):
                            e.indirect_dma_start(out=G[:, s, i, :], out_offset=None, in_=table,
                                                 in_offset=IOA(ap=idx[:, s, i:i + 1], axis=0))\
                                .then_inc(landed[s], 16)

                at, last_use = 0, None
                for n, k in enumerate(pre_at + (WI,)):
                    if at < k:
                        gather(at, n, last_use)
                        with e.Fori(at + 1, k) as r:
                            gather(r, n, r)
                        last_use = k
                    at = k + 1

            if own_part is not None:
                @block.sync
                def _(e):
                    own_part.load(e)

            if weights is not None:
                @block.sync
                def _(e):
                    w_t = weights.rearrange("(t p) w -> p t w", p=P)
                    with e.Fori(0, WI) as k:
                        for s in range(SETS):
                            e.wait_ge(summed, k * CREDIT + (s + 1) * U)
                            e.dma_start(W[:, s, :, :], w_t[:, bass.ds(k * (SETS * U) + s * U, U), :])\
                                .then_inc(w_in[s], 16)

            if heads == 2:
                @block.scalar
                def _(e):
                    def turn(k, slot, skipped):
                        for s in range(SETS):
                            e.wait_ge(w_in[s], k * 16 + 16)
                            if slot is None:
                                e.wait_ge(landed[s], (k - skipped) * (16 * U) + 16 * U)
                            rows = rows_of(s, slot)
                            for i in range(U):
                                for h in range(2):
                                    v = rows[:, i, h * P:(h + 1) * P]
                                    ins = e.activation(v, v, ACT.Copy, scale=W[:, s, i, h:h + 1])
                            ins.then_inc(scaled[s], 1)
                    turns(e, turn)

            if heads == 8:
                @block.scalar
                def _(e):
                    with e.Fori(0, WI) as k:
                        for s in range(SETS):
                            e.wait_ge(summed, k * CREDIT + (s + 1) * U)
                            for i in range(U):
                                ins = e.activation(OH[:, s, i, :], g.iota_row[:, :], ACT.Abs, scale=-1.0,
                                                   bias=lrel[:, bass.ds(k * CREDIT + (s * U + i), 1)])
                            ins.then_inc(spread, 1)
                            e.wait_ge(spread, k * SETS + (s + 1))
                            e.activation(OH[:, s, :, :], OH[:, s, :, :], ACT.Relu, scale=-1.0,
                                         bias=g.ones[:, 0:1]).then_inc(hot[s], 1)

            @block.vector
            def _(e):
                if own_part is not None:
                    own_part.vector(e)
                e.memset(acc[:, 0, :], 0.0)
                e.memset(acc[:, 1, :], 0.0).then_inc(added, 1)
                for n in range(BANKS - 1):
                    e.sem_inc(added, 1)

                def prepare(k, s, i, slot, skipped):
                    t = k * CREDIT + (s * U + i)
                    if heads == 8:
                        if i == 0:
                            e.wait_ge(w_in[s], k * 16 + 16)
                            if slot is None:
                                e.wait_ge(landed[s], (k - skipped) * (16 * U) + 16 * U)
                        v = rows_of(s, slot)[:, i, 0:D].rearrange("p (h c) -> p h c", h=8)
                        e.tensor_tensor(v, v, bc_last(W[:, s, i, :], D // 8), ALU.mult).then_inc(scaled[s], 1)
                    else:
                        if i == 0:
                            e.wait_ge(summed, k * CREDIT + (s + 1) * U)
                        e.tensor_scalar(OH[:, s, i, :], g.iota_row[:, :], lrel[:, bass.ds(t, 1)], None,
                                        ALU.is_equal).then_inc(hot[s], 1)

                def turn(k, here, following):
                    for s in range(SETS):
                        _, places = nc.values_load_multi_w_load_instructions(
                            base[0:1, bass.ds(k * CREDIT + s * U, U)], engines=[mybir.EngineType.DVE],
                            min_val=0, max_val=NP - 1,
                            skip_runtime_bounds_check_because="a window starts at the node of one of its edges")
                        for i in range(U):
                            t = k * CREDIT + (s * U + i)
                            e.wait_ge(summed, t + (CREDIT + 1))
                            e.wait_ge(added, t + BANKS)
                            w = acc[:, :, bass.ds(places[i], P)]
                            e.tensor_tensor(w, w, g.ps[i % BANKS][:, 0:D].rearrange("p (h n) -> p h n", h=2),
                                            ALU.add).then_inc(added, 1)
                            if s < SETS - 1:
                                prepare(k, s + 1, i, *here)
                            elif following is not None:
                                prepare(k + 1, 0, i, *following)

                for i in range(U):
                    prepare(0, 0, i, 0 if pre_at else None, 0)
                at = 0
                for n, k in enumerate(pre_at + (WI,)):
                    if at < k:
                        with e.Fori(at, k - 1) as r:
                            turn(r, (None, n), (None, n))
                        turn(k - 1, (None, n), (n, n) if k < WI else None)
                    if k < WI:
                        turn(k, (n, n), (None, n + 1))
                    at = k + 1

            @block.tensor
            def _(e):
                if own_part is not None:
                    own_part.tensor(e)
                for n in range(CREDIT):
                    e.sem_inc(summed, 1)

                def turn(k, slot, skipped):
                    for s in range(SETS):
                        if heads == 8:
                            e.wait_ge(hot[s], k + 1)
                        elif heads == 2:
                            e.wait_ge(scaled[s], k + 1)
                        elif slot is None:
                            e.wait_ge(landed[s], (k - skipped) * (16 * U) + 16 * U)
                        rows = rows_of(s, slot)
                        for i in range(U):
                            t = k * (SETS * U) + (s * U + i)
                            e.wait_ge((scaled if heads == 8 else hot)[s], k * U + (i + 1))
                            if slot != 0 or t >= BANKS:
                                e.wait_ge(added, t + 1)
                            for h in range(2):
                                m = e.matmul(g.ps[i % BANKS][:, h * P:(h + 1) * P], lhsT=rows[:, i, h * P:(h + 1) * P],
                                             rhs=OH[:, s, i, :], start=True, stop=True)
                            m.then_inc(summed, 1)
                turns(e, turn)


def stage_update1(nc, env, acc):
    g = env
    turned, done = g.sem("u1_turned"), g.sem("u1_done")
    with ExitStack() as own:
        norm = Norm(nc, g, own, "n2", g.H2D)
        with nc.Block() as block:
            @block.sync
            def _(e):
                norm.sync(e)

            @block.scalar
            def _(e):
                norm.scalar(e)

            @block.tensor
            def _(e):
                for j in range(NT):
                    if j >= 4:
                        e.wait_ge(done, j - 3)
                    for h in range(2):
                        m = e.transpose(g.ps[4 + j % 4][:, h * P:(h + 1) * P], acc[:, h, j * P:(j + 1) * P],
                                        g.ident[:, :])
                    m.then_inc(turned, 1)
                norm.tensor(e)

            @block.vector
            def _(e):
                for j in range(NT):
                    e.wait_ge(turned, j + 1)
                    e.tensor_tensor(g.X[:, j, :], g.X[:, j, :], g.ps[4 + j % 4][:, 0:D], ALU.add).then_inc(done, 1)
                e.wait_ge(done, NT)
                norm.vector(e)


class OwnPart:

    def __init__(self, nc, g, own, A):
        self.g, self.A = g, A
        self.loaded, self.biased, self.product, self.kept = (g.sem("own_" + x) for x in ("loaded", "biased",
                                                                                        "product", "kept"))
        self.W = own.enter_context(nc.sbuf_tensor("own_W", [P, 2, D], f32))
        self.b = own.enter_context(nc.sbuf_tensor("own_b", [P, D], f32))

    def load(self, e):
        e.dma_start(self.W[:, :, :], self.A["L2_gnn_W_self"].rearrange("(h p) m -> p h m", p=P))\
            .then_inc(self.loaded, 16)
        e.dma_start(self.b[:, :], bc_row(self.A["L2_gnn_b_self"])).then_inc(self.loaded, 16)

    def tensor(self, e):
        g = self.g
        e.wait_ge(self.loaded, 32)
        for j in range(NT):
            if j >= 8:
                e.wait_ge(self.kept, j - 7)
            for h in range(2):
                m = e.matmul(g.ps[j % 8][:, 0:D], lhsT=g.HT[:, h, j * P:(j + 1) * P], rhs=self.W[:, h, :],
                             start=h == 0, stop=h == 1)
            m.then_inc(self.product, 1)
        e.wait_ge(self.kept, NT)

    def vector(self, e):
        g = self.g
        e.wait_ge(self.loaded, 32)
        e.tensor_tensor(g.X[:, :, :], g.X[:, :, :], bc_mid(self.b[:, :], NT), ALU.add).then_inc(self.biased, 1)
        e.wait_ge(self.biased, 1)
        for j in range(NT):
            e.wait_ge(self.product, j + 1)
            e.tensor_tensor(g.X[:, j, :], g.X[:, j, :], g.ps[j % 8][:, 0:D], ALU.add).then_inc(self.kept, 1)


def stage_update2(nc, env, A, acc):
    g = env
    loaded, linked, product, done = g.sem("u2_loaded"), g.sem("u2_linked"), g.sem("u2_product"), g.sem("u2_done")
    with ExitStack() as own:
        W = own.enter_context(nc.sbuf_tensor("u2_W", [P, 2, D], f32))
        rdeg = own.enter_context(nc.sbuf_tensor("u2_rdeg", [P, NT], f32))
        with nc.Block() as block:
            @block.sync
            def _(e):
                e.dma_start(W[:, :, :], A["L2_gnn_W_neigh"].rearrange("(h p) m -> p h m", p=P)).then_inc(loaded, 16)

            @block.tensor
            def _(e):
                e.wait_ge(loaded, 16)
                for j in range(NT):
                    if j >= 4:
                        e.wait_ge(done, j - 3)
                    for h in range(2):
                        m = e.matmul(g.ps[j % 4][:, 0:D], lhsT=acc[:, h, j * P:(j + 1) * P], rhs=W[:, h, :],
                                     start=h == 0, stop=h == 1)
                    m.then_inc(product, 1)

            @block.vector
            def _(e):
                link = Link(e, linked)
                link(e.tensor_single_scalar(rdeg[:, :], g.deg_d[:, :], 1.0, ALU.max))
                link(e.reciprocal(rdeg[:, :], rdeg[:, :]))
                for j in range(NT):
                    e.wait_ge(product, j + 1)
                    e.scalar_tensor_tensor(g.X[:, j, :], g.ps[j % 4][:, 0:D], rdeg[:, j:j + 1], g.X[:, j, :],
                                           ALU.mult, ALU.add).then_inc(done, 1)



def stage_scores3(nc, env, A, pre):
    g = env
    sem = g.sem
    landed, free, hot, row_in, win_in, sc_ready, sc_out = (
        [sem(f"s3_{x}{s}") for s in range(SETS)]
        for x in ("landed", "free", "hot", "row", "win", "sc_ready", "sc_out"))
    staged, seen, att_in = sem("s3_staged"), sem("s3_seen"), sem("s3_att")
    summed, drained, weighed = sem("s3_summed"), sem("s3_drained"), sem("s3_weighed")
    BANKS, PER = 8, SETS * U
    with ExitStack() as own:
        def sb(n, shape, dt=f32):
            return own.enter_context(nc.sbuf_tensor("s3_" + n, shape, dt))
        idx = sb("idx", [P, SETS, U], i32)
        G, XR = sb("G", [P, SETS, U, XLW]), sb("XR", [P, SETS, U, XLW])
        rowb, OT = sb("rowb", [P, SETS, U * P], i32), one_hot_view(g)
        R = sb("R", [P, 2, U, D])
        L = sb("L", [P, 2, U, 8])
        att = sb("att", [P, D])
        SC = sb("SC", [P, SETS, U, 8])
        with nc.Block() as block:
            @block.gpsimd
            def _(e):
                def gather(k, skipped, last_use):
                    for s in range(SETS):
                        if last_use is not None:
                            e.wait_ge(free[s], last_use + 1)
                        e.tensor_copy(idx[:, s, :], g.src_t[:, bass.ds(k * PER + s * U, U)])\
                            .then_inc(staged, 1)
                        e.wait_ge(staged, (k - skipped) * SETS + (s + 1))
                        e.sem_inc(seen, 1)
                        for i in range(U):
                            e.indirect_dma_start(out=G[:, s, i, :], out_offset=None, in_=g.XLD[:, :],
                                                 in_offset=IOA(ap=idx[:, s, i:i + 1], axis=0))\
                                .then_inc(landed[s], 16)

                gather(0, 0, None)
                with e.Fori(1, PRE_SCORES) as k:
                    gather(k, 0, k)
                gather(PRE_SCORES + 1, 1, PRE_SCORES)
                with e.Fori(PRE_SCORES + 2, WI) as k:
                    gather(k, 1, k)

            @block.sync
            def _(e):
                e.dma_start(att[:, :], bc_row(A["L3_gnn_att"].rearrange("h c -> (h c)"))).then_inc(att_in, 16)
                with e.Fori(0, WI) as k:
                    for s in range(SETS):
                        e.wait_ge(free[s], k + 1)
                        e.dma_start(rowb[:, s, :], bc_row(A["dst_row"][bass.ds(k * (PER * P) + s * U * P, U * P)]))\
                            .then_inc(row_in[s], 16)
                        _, places = nc.values_load_multi_w_load_instructions(
                            g.base_d[0:1, bass.ds(k * PER + s * U, U)], engines=[mybir.EngineType.SP],
                            min_val=0, max_val=NP - 1,
                            skip_runtime_bounds_check_because="a window starts at the node of one of its edges")
                        for i in range(U):
                            e.dma_start(XR[:, s, i, :], g.XRD[bass.ds(places[i], P), :]).then_inc(win_in[s], 16)

            @block.scalar
            def _(e):
                sc_t = g.SCD.rearrange("(t p) w -> p t w", p=P)

                def store(k, s):
                    e.wait_ge(sc_ready[s], k * 3 + 3)
                    e.dma_start(sc_t[:, bass.ds(k * PER + s * U, U), :], SC[:, s, :, :]).then_inc(sc_out[s], 16)

                for n in range(BANKS):
                    e.sem_inc(drained, 1)
                with e.Fori(0, WI) as k:
                    for s in range(SETS):
                        e.wait_ge(weighed, k * SETS + (s + 1))
                        for i in range(U):
                            t = k * PER + (s * U + i)
                            bank = g.ps[(s * U + i) % BANKS]
                            e.wait_ge(summed, t + 1)
                            e.activation(L[:, s % 2, i, :], bank[:, D:XLW], ACT.Copy)
                            e.activation(R[:, s % 2, i, :], bank[:, 0:D], ACT.Relu, scale=0.8).then_inc(drained, 1)
                        if s >= 1:
                            store(k, s - 1)
                    store(k, SETS - 1)
                for s in range(SETS):
                    e.wait_ge(sc_out[s], 16 * WI)

            @block.vector
            def _(e):
                e.wait_ge(att_in, 16)

                def one_hot(k, s):
                    e.wait_ge(row_in[s], k * 16 + 16)
                    e.tensor_tensor(OT[:, s, :, :], rowb[:, s, :].rearrange("p (i f) -> p i f", f=P),
                                    bc_last(g.win_d[:, bass.ds(k * PER + s * U, U)], P), ALU.is_equal)\
                        .then_inc(hot[s], 1)

                def finish(k, s, first):
                    e.wait_ge(drained, k * PER + ((s + 1) * U + BANKS))
                    e.sem_inc(free[s], 1)
                    v = R[:, s % 2, :, :]
                    e.tensor_tensor(v, v, bc_mid(att[:, :], U), ALU.mult).then_inc(sc_ready[s], 1)
                    e.wait_ge(sc_ready[s], k * 3 + 1)
                    if not first:
                        e.wait_ge(sc_out[s], k * 16)
                    e.tensor_reduce(SC[:, s, :, :], v.rearrange("p i (h c) -> p i h c", h=8), AX.X, ALU.add)\
                        .then_inc(sc_ready[s], 1)
                    e.wait_ge(sc_ready[s], k * 3 + 2)
                    e.tensor_tensor(SC[:, s, :, :], SC[:, s, :, :], L[:, s % 2, :, :], ALU.add)\
                        .then_inc(sc_ready[s], 1)
                    e.wait_ge(sc_ready[s], k * 3 + 3)
                    e.sem_inc(weighed, 1)

                def turn(k, first=False, last=False):
                    for s in range(SETS):
                        if s < SETS - 1:
                            one_hot(k, s + 1)
                        elif not last:
                            one_hot(k + 1, 0)
                        finish(k, s, first)

                for s in range(SETS):
                    e.sem_inc(free[s], 1)
                for s in range(2):
                    e.sem_inc(weighed, 1)
                one_hot(0, 0)
                turn(0, first=True)
                with e.Fori(1, WI - 1) as k:
                    turn(k)
                turn(WI - 1, last=True)

            @block.tensor
            def _(e):
                def turn(k, skipped, there=False):
                    for s in range(SETS):
                        e.wait_ge(hot[s], k + 1)
                        e.wait_ge(win_in[s], k * (16 * U) + 16 * U)
                        if not there:
                            e.wait_ge(landed[s], (k - skipped) * (16 * U) + 16 * U)
                        rows = pre[:, s * U:(s + 1) * U, :] if there else G[:, s, :, :]
                        for i in range(U):
                            bank = g.ps[(s * U + i) % BANKS]
                            e.wait_ge(drained, k * PER + (s * U + i + 1))
                            e.matmul(bank[:, 0:XLW], lhsT=OT[:, s, i, :], rhs=XR[:, s, i, :], start=True, stop=False)
                            e.matmul(bank[:, 0:XLW], lhsT=g.ident[:, :], rhs=rows[:, i, :], start=False, stop=True)\
                                .then_inc(summed, 1)

                with e.Fori(0, PRE_SCORES) as k:
                    turn(k, 0)
                turn(PRE_SCORES, 0, there=True)
                with e.Fori(PRE_SCORES + 1, WI) as k:
                    turn(k, 1)


def stage_softmax3(nc, env, A, pre):
    g = env
    sem = g.sem
    loaded, linked, asked, answered, act_asked, act_done, soft, stored = (
        sem("x3_loaded"), sem("x3_linked"), sem("x3_ask"), sem("x3_answer"), sem("x3_act_ask"), sem("x3_act"),
        sem("x3_soft"), sem("x3_stored"))
    with ExitStack() as own:
        def sb(n, shape):
            return own.enter_context(nc.sbuf_tensor("x3_" + n, shape, f32))
        S, M, V = (sb(x, [P, ET, 8]) for x in ("S", "M", "V"))
        ew, lw, carry = sb("ew", [P, ET]), sb("lw", [P, ET]), sb("carry", [P, 8])
        ahead = Ahead(nc, g, own, "x3", pre.shape[1])
        with nc.Block() as block:
            @block.gpsimd
            def _(e):
                ahead.gather(e, [g.src_t[:, k * SETS * U:(k + 1) * SETS * U] for k in PRE_AT], g.XLD[:, :], pre)

            @block.sync
            def _(e):
                e.dma_start(S[:, :, :], g.SCD.rearrange("(p j) w -> p j w", j=ET)).then_inc(loaded, 16)
                e.dma_start(ew[:, :], A["ew"][:, :]).then_inc(loaded, 16)
                e.wait_ge(soft, 1)
                e.dma_start(g.WD.rearrange("(p j) w -> p j w", j=ET), S[:, :, :]).then_inc(stored, 16)
                e.wait_ge(stored, 16)

            @block.scalar
            def _(e):
                e.wait_ge(act_asked, 1)
                e.activation(lw[:, :], lw[:, :], ACT.Ln).then_inc(act_done, 1)
                e.wait_ge(act_asked, 2)
                e.activation(S[:, :, :], S[:, :, :], ACT.Exp).then_inc(act_done, 1)

            @block.vector
            def _(e):
                link = Link(e, linked)
                flip, act = Asks(e, asked, answered), Asks(e, act_asked, act_done)
                e.wait_ge(loaded, 32)
                link(e.tensor_single_scalar(lw[:, :], ew[:, :], 2.0 ** -64, ALU.max))
                act()
                link(e.tensor_tensor(V[:, :, :], S[:, :, :], bc_last(lw[:, :], 8), ALU.add))
                seg_softmax(e, g, link, flip, act, 8, g.od, S, M, V, carry, weight=ew[:, :], eps=1e-16)
                e.sem_inc(soft, 1)

            @block.tensor
            def _(e):
                tensor_flips(e, g, asked, answered, scan_flips(8, 4))


def stage_output(nc, env, A, acc, out):
    g = env
    loaded, linked, turned, done, stored = (g.sem("o_loaded"), g.sem("o_linked"), g.sem("o_turned"),
                                            g.sem("o_done"), g.sem("o_stored"))
    with ExitStack() as own:
        b = own.enter_context(nc.sbuf_tensor("o_b", [P, D], f32))
        with nc.Block() as block:
            @block.sync
            def _(e):
                e.dma_start(b[:, :], bc_row(A["L3_gnn_bias"])).then_inc(loaded, 16)
                o = out.rearrange("(j p) d -> p j d", p=P)
                for n in range(5):
                    e.wait_ge(done, 5 * n + 5)
                    e.dma_start(o[:, 5 * n:5 * n + 5, :], g.X[:, 5 * n:5 * n + 5, :]).then_inc(stored, 16)
                e.wait_ge(stored, 80)

            @block.tensor
            def _(e):
                for j in range(NT):
                    if j >= 4:
                        e.wait_ge(done, j - 3)
                    for h in range(2):
                        m = e.transpose(g.ps[j % 4][:, h * P:(h + 1) * P], acc[:, h, j * P:(j + 1) * P],
                                        g.ident[:, :])
                    m.then_inc(turned, 1)

            @block.vector
            def _(e):
                link = Link(e, linked)
                e.wait_ge(loaded, 16)
                link(e.tensor_tensor(g.X[:, :, :], g.X[:, :, :], bc_mid(b[:, :], NT), ALU.add))
                for j in range(NT):
                    e.wait_ge(turned, j + 1)
                    e.tensor_tensor(g.X[:, j, :], g.X[:, j, :], g.ps[j % 4][:, 0:D], ALU.add).then_inc(done, 1)


def build(nc, A, out):
    with ExitStack() as stack:
        g = Env()

        def run(stage, *args, **options):
            taken = []

            def sem(name):
                taken.append(nc.alloc_semaphore(name=name))
                return taken[-1]

            g.sem = sem
            stage(nc, g, *args, **options)
            nc.all_engine_barrier()
            nc.clear_and_free_semaphores(taken)
            nc.all_engine_barrier()

        def sb(name, shape, dt=f32):
            return stack.enter_context(nc.sbuf_tensor(name, shape, dt))

        def dram(name, shape, dt=f32):
            return nc.dram_tensor(name, shape, dt, kind="Internal").ap()

        g.ps = [stack.enter_context(nc.psum_tensor(f"ps{i}", [P, 512], f32)) for i in range(8)]
        g.iota_row, g.iota_p, g.ones = sb("iota_row", [P, P]), sb("iota_p", [P, 1]), sb("ones", [P, P])
        g.ident, g.before, g.after = sb("ident", [P, P]), sb("before", [P, P]), sb("after", [P, P])
        g.X, g.HT = sb("X", [P, NT, D]), sb("HT", [P, 2, NP])
        g.src_t = sb("src_t_sb", [P, ET], i32)
        g.deg_s, g.deg_d, g.start_s, g.start_d = (sb(x, [P, NT]) for x in ("deg_s", "deg_d", "start_s", "start_d"))
        g.T0, g.RKF = dram("T0", (NP, 16)), dram("RKF", (EP,), i32)
        g.lrel_d, g.win_d = sb("lrel_d", [P, ET]), sb("win_d", [P, ET])
        g.base_d = sb("base_d", [1, ET], i32)
        g.put_d, g.put_s, g.end_d, g.end_s = (sb(x, [P, NT], i32) for x in ("put_d", "put_s", "end_d", "end_s"))
        g.flip_in, g.flip_ex = sb("flip_in", [P, 8]), sb("flip_ex", [8, P + 2])
        g.od = Order(sb, "od")
        g.MSG = sb("MSG", [P, NT, 8])
        g.Z8, g.RECD, g.KEYD = dram("Z8", (EP, 8)), dram("RECD", (EP + 2, NRW)), dram("KEYD", (2, EP))
        g.WHD, g.H2D, g.XLD, g.XRD = (dram("WHD", (NP, D)), dram("H2D", (NP, D)), dram("XLD", (NP, XLW)),
                                      dram("XRD", (NP + P, XLW)))
        g.Z2, g.ALD = dram("Z2", (EP, 2)), dram("ALD", (EP, 2))
        g.SLOW, g.DLOW, g.LSD = dram("SLOW", (EP,), bf16), dram("DLOW", (EP,), bf16), dram("LSD", (EP, 8))
        g.LTD = dram("LTD", (NP, 8))
        g.SCD, g.WD = dram("SCD", (EP, 8)), dram("WD", (EP, 8))
        g.MSD = dram("MSD", (EP, 8))
        with ExitStack() as by_src:
            def by_src_sb(name, shape, dt=f32):
                return by_src.enter_context(nc.sbuf_tensor(name, shape, dt))

            g.os = Order(by_src_sb, "os")
            g.lrel_s, g.dhi_s = by_src_sb("lrel_s", [P, ET]), by_src_sb("dhi_s", [P, ET])
            g.dsts_t, g.base_s = by_src_sb("dsts_t", [P, ET], i32), by_src_sb("base_s", [1, ET], i32)
            with ExitStack() as layer0:
                def layer0_sb(name, shape, dt=f32):
                    return layer0.enter_context(nc.sbuf_tensor(name, shape, dt))

                g.dst_t, g.src_c, g.rank_c, g.dsts_c = (layer0_sb(x, [P, ET], i32)
                                                        for x in ("dst_t_sb", "src_c_sb", "rank_c", "dsts_c"))
                g.shi_c, g.LT = layer0_sb("shi_c", [P, ET]), layer0_sb("LT", [P, NT, 8])
                g.AD, g.GAT = layer0_sb("AD", [P, NT, 8]), layer0_sb("GAT", [P, ET, 16])
                run(stage_constants, A)
                run(stage_tables0, A)
                run(stage_rank, A)
                g.PD, g.T1, g.T2 = (layer0_sb(x, [P, ET, 8]) for x in ("PD", "T1", "T2"))
                with ExitStack() as own:
                    REC = own.enter_context(nc.sbuf_tensor("REC", [P, ET, NRW], f32))
                    run(stage_edges0, A, REC)
                g.T3 = layer0_sb("T3", [P, ET, 8])
                run(stage_by_src)
                run(stage_messages0)
            run(stage_update0, A)
            SN, TN = by_src_sb("SN", [P, NT, 2]), by_src_sb("TN", [P, NT, 2])
            with ExitStack() as own:
                T = own.enter_context(nc.sbuf_tensor("T_wh", [P, NT, D], f32))
                a = A["L1_gnn_a"]
                run(stage_norm_project, "n1", [
                    ("p1", A["L1_gnn_W_w"], A["L1_gnn_W_b"],
                     [[(0, a[0:P]), (P, a[0:P])], [(0, a[P:D]), (P, a[P:D])]], 2, 1.0, T,
                     [SN[:, :, :], TN[:, :, :]], g.WHD[:, :], D)], lone=g.deg_s)
            pre = by_src_sb("pre1", [P, len(PRE_AT) * SETS * U, D])
            run(stage_edges1, SN, TN, g.ALD, pre)
            acc = by_src_sb("acc1", [P, 2, ACCW])
            run(stage_aggregate, "a1", g.WHD[:, :], D, g.dsts_t, g.lrel_s, g.base_s, acc, g.ALD, 2, pre,
                one_hot_view(g))
            run(stage_update1, acc)
        with ExitStack() as own:
            acc = own.enter_context(nc.sbuf_tensor("acc2", [P, 2, ACCW], f32))
            run(stage_aggregate, "a2", g.H2D[:, :], D, g.src_t, g.lrel_d, g.base_d, acc,
                own_part=A)
            run(stage_update2, A, acc)
        att = A["L3_gnn_att"].rearrange("h c -> (h c)")
        with ExitStack() as scores:
            pre = scores.enter_context(nc.sbuf_tensor("pre_scores", [P, SETS * U, XLW], f32))
            with ExitStack() as own:
                TL, TR = (own.enter_context(nc.sbuf_tensor(x, [P, NT, XLW], f32)) for x in ("T_xl", "T_xr"))
                run(stage_norm_project, "n3", [
                    ("p3l", A["L3_gnn_W_l"], A["L3_gnn_b_l"], [[(0, att)]], 8, 0.2, TL, [TL[:, :, D:XLW]],
                     g.XLD[:, :], XLW),
                    ("p3r", A["L3_gnn_W_r"], A["L3_gnn_b_r"], [[(0, att)]], 8, 0.2, TR, [TR[:, :, D:XLW]],
                     g.XRD[0:NP, :], XLW)],
                    ([g.src_t[:, PRE_SCORES * SETS * U:(PRE_SCORES + 1) * SETS * U]], g.XLD[:, :], pre))
            run(stage_scores3, A, pre)
        pre = sb("pre3", [P, len(PRE_AT) * SETS * U, XLW])
        run(stage_softmax3, A, pre)
        acc = sb("acc3", [P, 2, ACCW])
        run(stage_aggregate, "a3", g.XLD[:, :], XLW, g.src_t, g.lrel_d, g.base_d, acc, g.WD, 8, pre,
            one_hot_view(g))
        run(stage_output, A, acc, out)


def kernel(**inputs):
    import numpy as _np
    import concourse.bacc as _bacc
    from concourse import mybir as _mybir
    from concourse.bass_utils import run_bass_kernel_spmd as _run

    def edges(a, fill):
        padded = _np.full((EP,) + a.shape[1:], fill, a.dtype)
        padded[:NE] = a
        return padded

    src, dst = edges(_np.asarray(inputs["src"]), NP - 1), edges(_np.asarray(inputs["dst"]), NP - 1)
    bordered = _np.concatenate([_np.full(1, -1, dst.dtype), dst, _np.full(1, NP, dst.dtype)])
    x = _np.zeros((NP, D), _np.float32)
    x[:NN] = inputs["x"]
    laid = {
        "x": x,
        "src_t": src.reshape(ET, P).T, "dst_t": dst.reshape(ET, P).T,
        "src_c": src.reshape(P, ET), "dst_c": _np.stack([bordered[ET * p:ET * p + ET + 2] for p in range(P)]),
        "src_row": src, "dst_row": dst,
        "attr": edges(_np.asarray(inputs["edge_attr_16"]), 0).reshape(P, ET // 8, P).transpose(1, 2, 0),
        "ew": edges(_np.asarray(inputs["edge_weight"]), 1).reshape(P, ET),
    }
    for name, a in inputs.items():
        if name.startswith("L"):
            a = _np.asarray(a)
            laid[name] = a.T if name in ("L2_gnn_W_neigh", "L2_gnn_W_self") else a
    nc = _bacc.Bacc("TRN2", target_bir_lowering=False, num_devices=1)
    arrays, args = {}, {}
    for name, a in laid.items():
        a = _np.ascontiguousarray(a)
        arrays[f"in_{name}_dram"] = a
        args[name] = nc.dram_tensor(f"in_{name}_dram", a.shape, _mybir.dt.from_np(a.dtype),
                                    kind="ExternalInput").ap()
    out = nc.dram_tensor("out_0_dram", (NP, D), _mybir.dt.float32, kind="ExternalOutput").ap()
    build(nc, args, out)
    r = _run(nc, [arrays], core_ids=[0])
    return r.results[0]["out_0_dram"][:NN]
```
